# Optimizing a Trainium2 kernel written in Bass

```python
import numpy as np
import jax
import jax.numpy as jnp

def _softmax(x, axis=-1):
    return jax.nn.softmax(x, axis=axis)

def _gelu(x):
    return jax.nn.gelu(x, approximate=True)

def _silu(x):
    return jax.nn.silu(x)

def _sigmoid(x):
    return jax.nn.sigmoid(x)

def _layernorm(x, axis=-1, eps=1e-05):
    m = jnp.mean(x, axis=axis, keepdims=True)
    v = jnp.var(x, axis=axis, keepdims=True)
    return (x - m) / jnp.sqrt(v + eps)

def _scatter_add(tgt, idx, src, axis=0):
    return tgt.at[idx].add(src)

def _segment_sum(src, seg, n):
    return jax.ops.segment_sum(src, seg, n)
kernel_name = 'mk_xattn_ffn_d2_seqx_r8_5e05f7'

def setup_inputs(seed: int=0):
    np.random.seed(seed)
    _w = jnp.asarray

    def _rec_inputs():
        import jax
        import jax.numpy as jnp
        _rk = jax.random.key(seed)
        x = 7.22e-05 + 1 * jax.random.normal(jax.random.fold_in(_rk, 1), (128, 64, 128), jnp.float32)
        _lenS = 64 - jax.random.randint(jax.random.fold_in(_rk, 7), (128,), 0, max(1, 64 // 4) + 1, jnp.int32)
        _lenS2 = 64 - jax.random.randint(jax.random.fold_in(_rk, 8), (128,), 0, max(1, 64 // 4) + 1, jnp.int32)
        _ctx_1024P = jax.random.normal(jax.random.fold_in(_rk, 11), (128, 16, 128), jnp.float32)
        _ctx_1024c = jax.random.dirichlet(jax.random.fold_in(_rk, 511), 0.3 * jnp.ones((16,), jnp.float32), (128, 64))
        _ctx_1024t = jnp.einsum('bsk,bkd->bsd', _ctx_1024c, _ctx_1024P)
        _ctx_1024t = _ctx_1024t * jax.lax.rsqrt(jnp.mean(jnp.square(_ctx_1024t)) + 1e-12) * 0.953939
        ctx_1024 = 4.13588e-05 + 0.999923 * (_ctx_1024t + 0.3 * jax.random.normal(jax.random.fold_in(_rk, 611), (128, 64, 128), jnp.float32))
        _validS = jnp.arange(64)[None, :] < _lenS[:, None]
        _validS2 = jnp.arange(64)[None, :] < _lenS2[:, None]
        _causal = jnp.tril(jnp.ones((64, 64), dtype=bool))
        mask_BxS2_bf0 = jnp.logical_not(jnp.ones((128, 64), dtype=bool))
        return (x, ctx_1024, mask_BxS2_bf0)
    x, ctx_1024, mask_BxS2_bf0 = _rec_inputs()

    def _L0_xattn_setup():
        import jax, jax.numpy as jnp
        import numpy as np
        DIM = 128
        N_HEAD = 16
        BS, QLEN, KLEN = (4, 256, 256)
        key = jax.random.key(seed)
        ks = jax.random.split(key, 12)
        s = 1.0 / np.sqrt(DIM)
        inp = {'q_in': jax.random.normal(ks[0], (BS, QLEN, DIM), jnp.float32), 'k_in': jax.random.normal(ks[1], (BS, KLEN, DIM), jnp.float32), 'v_in': jax.random.normal(ks[2], (BS, KLEN, DIM), jnp.float32), 'key_padding_mask': jnp.zeros((BS, KLEN), dtype=bool), 'Wq': jax.random.normal(ks[3], (DIM, DIM), jnp.float32) * s, 'bq': jnp.zeros((DIM,), jnp.float32), 'Wk': jax.random.normal(ks[4], (DIM, DIM), jnp.float32) * s, 'bk': jnp.zeros((DIM,), jnp.float32), 'Wv': jax.random.normal(ks[5], (DIM, DIM), jnp.float32) * s, 'bv': jnp.zeros((DIM,), jnp.float32), 'Wo': jax.random.normal(ks[6], (DIM, DIM), jnp.float32) * s, 'bo': jnp.zeros((DIM,), jnp.float32)}
        return inp
    _L0_xattn_all = _L0_xattn_setup()
    _L0_xattn_in = {k: v for k, v in _L0_xattn_all.items() if k in ('Wq', 'bq', 'Wk', 'bk', 'Wv', 'bv', 'Wo', 'bo')}
    del _L0_xattn_all

    def _L0_ffn_setup():
        import jax, jax.numpy as jnp
        import numpy as np
        E = 32
        K = 4
        H = 128
        F = 128
        LIMIT = 7.0
        ALPHA = 1.702
        EPS = 1e-05

        def _rmsnorm(x, scale):
            t = x * jax.lax.rsqrt(jnp.mean(x * x, axis=-1, keepdims=True) + EPS)
            return t * scale

        def _swiglu(h):
            glu = jnp.minimum(h[..., ::2], LIMIT)
            lin = jnp.clip(h[..., 1::2], -LIMIT, LIMIT)
            return glu * jax.nn.sigmoid(ALPHA * glu) * (lin + 1.0)
        key = jax.random.key(seed)
        ks = jax.random.split(key, 8)
        B, S = (1, 128)
        x = jax.random.normal(ks[0], (B, S, H), dtype=jnp.float32)
        norm_scale = jnp.ones((H,), dtype=jnp.float32)
        gate_w = jax.random.normal(ks[1], (E, H), dtype=jnp.float32) * 0.02
        gate_b = jnp.zeros((E,), dtype=jnp.float32)
        w1 = jax.random.normal(ks[2], (E, 2 * F, H), dtype=jnp.float32) * 0.02
        b1 = jnp.zeros((E, 2 * F), dtype=jnp.float32)
        w2 = jax.random.normal(ks[3], (E, H, F), dtype=jnp.float32) * 0.02
        b2 = jnp.zeros((E, H), dtype=jnp.float32)
        return {'x': x, 'norm_scale': norm_scale, 'gate_w': gate_w, 'gate_b': gate_b, 'w1': w1, 'b1': b1, 'w2': w2, 'b2': b2}
    _L0_ffn_all = _L0_ffn_setup()
    _L0_ffn_in = {k: v for k, v in _L0_ffn_all.items() if k in ('norm_scale', 'gate_w', 'gate_b', 'w1', 'b1', 'w2', 'b2')}
    del _L0_ffn_all

    def _L1_xattn_setup():
        import jax, jax.numpy as jnp
        import numpy as np
        D_MODEL = 128
        NUM_HEADS = 16
        HEAD_DIM = D_MODEL // NUM_HEADS
        ROPE_BASE = 10000.0

        def _rope_cos_sin(seq_len, head_dim, dtype):
            inv_freq = 1.0 / ROPE_BASE ** (jnp.arange(0, head_dim, 2, dtype=jnp.float32) / head_dim)
            t = jnp.arange(seq_len, dtype=jnp.float32)
            freqs = jnp.einsum('i,j->ij', t, inv_freq)
            emb = jnp.concatenate([freqs, freqs], axis=-1)
            return (jnp.cos(emb).astype(dtype), jnp.sin(emb).astype(dtype))

        def _rotate_half(x):
            x1, x2 = jnp.split(x, 2, axis=-1)
            return jnp.concatenate([-x2, x1], axis=-1)
        key = jax.random.key(seed)
        ks = jax.random.split(key, 12)
        B, S, D = (4, 256, D_MODEL)
        scale = 1.0 / np.sqrt(D)
        inp = {'query': jax.random.normal(ks[0], (B, S, D), jnp.float32), 'key': jax.random.normal(ks[1], (B, S, D), jnp.float32), 'value': jax.random.normal(ks[2], (B, S, D), jnp.float32), 'Wq': jax.random.normal(ks[3], (D, D), jnp.float32) * scale, 'bq': jnp.zeros((D,), jnp.float32), 'Wk': jax.random.normal(ks[4], (D, D), jnp.float32) * scale, 'bk': jnp.zeros((D,), jnp.float32), 'Wv': jax.random.normal(ks[5], (D, D), jnp.float32) * scale, 'bv': jnp.zeros((D,), jnp.float32), 'Wo': jax.random.normal(ks[6], (D, D), jnp.float32) * scale, 'bo': jnp.zeros((D,), jnp.float32)}
        return inp
    _L1_xattn_all = _L1_xattn_setup()
    _L1_xattn_in = {k: v for k, v in _L1_xattn_all.items() if k in ('Wq', 'bq', 'Wk', 'bk', 'Wv', 'bv', 'Wo', 'bo')}
    del _L1_xattn_all

    def _L1_ffn_setup():
        import jax, jax.numpy as jnp
        import numpy as np
        DIM = 128
        HIDDEN = 352
        NUM_EXPERTS = 8
        TOP_K = 2
        BATCH, SEQ = (4, 256)
        key = jax.random.key(seed)
        ks = jax.random.split(key, 5)
        x = jax.random.normal(ks[0], (BATCH, SEQ, DIM), dtype=jnp.float32)
        gate_w = jax.random.normal(ks[1], (NUM_EXPERTS, DIM), dtype=jnp.float32) * 0.02
        w1 = jax.random.normal(ks[2], (NUM_EXPERTS, HIDDEN, DIM), dtype=jnp.float32) * 0.02
        w3 = jax.random.normal(ks[3], (NUM_EXPERTS, HIDDEN, DIM), dtype=jnp.float32) * 0.02
        w2 = jax.random.normal(ks[4], (NUM_EXPERTS, DIM, HIDDEN), dtype=jnp.float32) * 0.02
        return {'x': x, 'gate_w': gate_w, 'w1': w1, 'w3': w3, 'w2': w2}
    _L1_ffn_all = _L1_ffn_setup()
    _L1_ffn_in = {k: v for k, v in _L1_ffn_all.items() if k in ('gate_w', 'w1', 'w3', 'w2')}
    del _L1_ffn_all
    return {'x': x, 'ctx_1024': ctx_1024, 'mask_BxS2_bf0': mask_BxS2_bf0, 'L0_xattn_Wq': _L0_xattn_in['Wq'], 'L0_xattn_bq': _L0_xattn_in['bq'], 'L0_xattn_Wk': _L0_xattn_in['Wk'], 'L0_xattn_bk': _L0_xattn_in['bk'], 'L0_xattn_Wv': _L0_xattn_in['Wv'], 'L0_xattn_bv': _L0_xattn_in['bv'], 'L0_xattn_Wo': _L0_xattn_in['Wo'], 'L0_xattn_bo': _L0_xattn_in['bo'], 'L0_ffn_norm_scale': _L0_ffn_in['norm_scale'], 'L0_ffn_gate_w': _L0_ffn_in['gate_w'], 'L0_ffn_gate_b': _L0_ffn_in['gate_b'], 'L0_ffn_w1': _L0_ffn_in['w1'], 'L0_ffn_b1': _L0_ffn_in['b1'], 'L0_ffn_w2': _L0_ffn_in['w2'], 'L0_ffn_b2': _L0_ffn_in['b2'], 'L1_xattn_Wq': _L1_xattn_in['Wq'], 'L1_xattn_bq': _L1_xattn_in['bq'], 'L1_xattn_Wk': _L1_xattn_in['Wk'], 'L1_xattn_bk': _L1_xattn_in['bk'], 'L1_xattn_Wv': _L1_xattn_in['Wv'], 'L1_xattn_bv': _L1_xattn_in['bv'], 'L1_xattn_Wo': _L1_xattn_in['Wo'], 'L1_xattn_bo': _L1_xattn_in['bo'], 'L1_ffn_gate_w': _L1_ffn_in['gate_w'], 'L1_ffn_w1': _L1_ffn_in['w1'], 'L1_ffn_w3': _L1_ffn_in['w3'], 'L1_ffn_w2': _L1_ffn_in['w2']}

def reference(x, ctx_1024, mask_BxS2_bf0, L0_xattn_Wq, L0_xattn_bq, L0_xattn_Wk, L0_xattn_bk, L0_xattn_Wv, L0_xattn_bv, L0_xattn_Wo, L0_xattn_bo, L0_ffn_norm_scale, L0_ffn_gate_w, L0_ffn_gate_b, L0_ffn_w1, L0_ffn_b1, L0_ffn_w2, L0_ffn_b2, L1_xattn_Wq, L1_xattn_bq, L1_xattn_Wk, L1_xattn_bk, L1_xattn_Wv, L1_xattn_bv, L1_xattn_Wo, L1_xattn_bo, L1_ffn_gate_w, L1_ffn_w1, L1_ffn_w3, L1_ffn_w2):
    import jax
    import jax.numpy as jnp

    def _L0_xattn_ref(q_in, k_in, v_in, key_padding_mask, Wq, bq, Wk, bk, Wv, bv, Wo, bo):
        import jax, jax.numpy as jnp
        import numpy as np
        DIM = 128
        N_HEAD = 16
        BS, QLEN, KLEN = (4, 256, 256)
        bs, q_len, _ = q_in.shape
        k_len = k_in.shape[1]
        h = N_HEAD
        d = DIM // h
        q = (q_in @ Wq + bq).reshape(bs, q_len, h, d).transpose(0, 2, 1, 3)
        k = (k_in @ Wk + bk).reshape(bs, k_len, h, d).transpose(0, 2, 1, 3)
        v = (v_in @ Wv + bv).reshape(bs, k_len, h, d).transpose(0, 2, 1, 3)
        score = jnp.einsum('bhqd,bhkd->bhqk', q, k) / jnp.sqrt(jnp.float32(d))
        mask = key_padding_mask[:, None, None, :]
        score = jnp.where(mask, jnp.float32(-1e+30), score)
        attn = jax.nn.softmax(score, axis=-1)
        out = jnp.einsum('bhqk,bhkd->bhqd', attn, v).transpose(0, 2, 1, 3).reshape(bs, q_len, DIM)
        return out @ Wo + bo

    def _L0_ffn_ref(x, norm_scale, gate_w, gate_b, w1, b1, w2, b2):
        import jax, jax.numpy as jnp
        import numpy as np
        E = 32
        K = 4
        H = 128
        F = 128
        LIMIT = 7.0
        ALPHA = 1.702
        EPS = 1e-05

        def _rmsnorm(x, scale):
            t = x * jax.lax.rsqrt(jnp.mean(x * x, axis=-1, keepdims=True) + EPS)
            return t * scale

        def _swiglu(h):
            glu = jnp.minimum(h[..., ::2], LIMIT)
            lin = jnp.clip(h[..., 1::2], -LIMIT, LIMIT)
            return glu * jax.nn.sigmoid(ALPHA * glu) * (lin + 1.0)
        B, S, _ = x.shape
        t = _rmsnorm(x, norm_scale)
        g = t @ gate_w.T + gate_b
        tf = t.reshape(-1, H)
        gf = g.reshape(-1, E)
        T = tf.shape[0]
        vals, idx = jax.lax.top_k(gf, K)
        w = jax.nn.softmax(vals, axis=-1)
        combine = jnp.zeros((T, E), dtype=tf.dtype).at[jnp.arange(T)[:, None], idx].add(w)
        h1 = jnp.einsum('th,efh->tef', tf, w1) + b1
        h = _swiglu(h1)
        hw = h * combine[:, :, None]
        out = jnp.einsum('tef,ehf->th', hw, w2) + combine @ b2
        return x + out.reshape(B, S, H)

    def _L1_xattn_ref(query, key, value, Wq, bq, Wk, bk, Wv, bv, Wo, bo):
        import jax, jax.numpy as jnp
        import numpy as np
        D_MODEL = 128
        NUM_HEADS = 16
        HEAD_DIM = D_MODEL // NUM_HEADS
        ROPE_BASE = 10000.0

        def _rope_cos_sin(seq_len, head_dim, dtype):
            inv_freq = 1.0 / ROPE_BASE ** (jnp.arange(0, head_dim, 2, dtype=jnp.float32) / head_dim)
            t = jnp.arange(seq_len, dtype=jnp.float32)
            freqs = jnp.einsum('i,j->ij', t, inv_freq)
            emb = jnp.concatenate([freqs, freqs], axis=-1)
            return (jnp.cos(emb).astype(dtype), jnp.sin(emb).astype(dtype))

        def _rotate_half(x):
            x1, x2 = jnp.split(x, 2, axis=-1)
            return jnp.concatenate([-x2, x1], axis=-1)
        B, T, D = query.shape
        H, hd = (NUM_HEADS, HEAD_DIM)
        Q = (query @ Wq + bq).reshape(B, T, H, hd).transpose(0, 2, 1, 3)
        K = (key @ Wk + bk).reshape(B, -1, H, hd).transpose(0, 2, 1, 3)
        V = (value @ Wv + bv).reshape(B, -1, H, hd).transpose(0, 2, 1, 3)
        cos, sin = _rope_cos_sin(T, hd, Q.dtype)
        Q = Q * cos + _rotate_half(Q) * sin
        K = K * cos + _rotate_half(K) * sin
        scores = jnp.einsum('bhtd,bhsd->bhts', Q, K) / jnp.sqrt(jnp.asarray(hd, Q.dtype))
        attn = jax.nn.softmax(scores, axis=-1)
        context = jnp.einsum('bhts,bhsd->bhtd', attn, V)
        context = context.transpose(0, 2, 1, 3).reshape(B, T, D)
        return context @ Wo + bo

    def _L1_ffn_ref(x, gate_w, w1, w3, w2):
        import jax, jax.numpy as jnp
        import numpy as np
        DIM = 128
        HIDDEN = 352
        NUM_EXPERTS = 8
        TOP_K = 2
        BATCH, SEQ = (4, 256)
        orig_shape = x.shape
        xf = x.reshape(-1, x.shape[-1])
        T = xf.shape[0]
        E, K = (gate_w.shape[0], TOP_K)
        scores = jax.nn.softmax(xf @ gate_w.T, axis=-1)
        expert_weights, expert_indices = jax.lax.top_k(scores, K)
        expert_weights = expert_weights / jnp.sum(expert_weights, axis=-1, keepdims=True)
        x_rep = jnp.repeat(xf, K, axis=0)
        flat_idx = expert_indices.reshape(-1)
        y = jnp.zeros_like(x_rep)
        for e in range(E):
            m = (flat_idx == e)[:, None]
            xe = jnp.where(m, x_rep, 0.0)
            h = jax.nn.silu(xe @ w1[e].T) * (xe @ w3[e].T)
            out = h @ w2[e].T
            y = y + jnp.where(m, out, 0.0)
        y = jnp.sum(y.reshape(T, K, -1) * expert_weights[..., None], axis=1)
        return y.reshape(orig_shape)
    x = x + _L0_xattn_ref(_layernorm(x, axis=-1), ctx_1024, ctx_1024, mask_BxS2_bf0, L0_xattn_Wq, L0_xattn_bq, L0_xattn_Wk, L0_xattn_bk, L0_xattn_Wv, L0_xattn_bv, L0_xattn_Wo, L0_xattn_bo)
    x = x + _L0_ffn_ref(_layernorm(x, axis=-1), L0_ffn_norm_scale, L0_ffn_gate_w, L0_ffn_gate_b, L0_ffn_w1, L0_ffn_b1, L0_ffn_w2, L0_ffn_b2)
    x = x + _L1_xattn_ref(_layernorm(x, axis=-1), ctx_1024, ctx_1024, L1_xattn_Wq, L1_xattn_bq, L1_xattn_Wk, L1_xattn_bk, L1_xattn_Wv, L1_xattn_bv, L1_xattn_Wo, L1_xattn_bo)
    x = x + _L1_ffn_ref(_layernorm(x, axis=-1), L1_ffn_gate_w, L1_ffn_w1, L1_ffn_w3, L1_ffn_w2)
    return x

_drawn_inputs = setup_inputs


def setup_inputs(seed=0):
    import zlib

    import numpy as np

    out = dict(_drawn_inputs(seed))
    spreads = {'L0_xattn_bq': (0.0, 0.366),
     'L0_xattn_bk': (0.0, 0.8),
     'L0_xattn_bv': (0.0, 0.1),
     'L0_xattn_bo': (0.0, 0.1),
     'L0_ffn_norm_scale': (1.0, 0.6),
     'L0_ffn_gate_b': (0.0, 0.502),
     'L0_ffn_b1': (0.0, 0.8),
     'L0_ffn_b2': (0.0, 0.389),
     'L1_xattn_bq': (0.0, 0.8),
     'L1_xattn_bk': (0.0, 0.8),
     'L1_xattn_bv': (0.0, 0.1),
     'L1_xattn_bo': (0.0, 0.1)}
    factors = {'L0_ffn_gate_w': 2.909,
     'L0_ffn_w1': 8.0,
     'L0_ffn_w2': 8.0,
     'L1_ffn_gate_w': 8.0,
     'L1_ffn_w1': 8.0,
     'L1_ffn_w3': 8.0,
     'L1_ffn_w2': 8.0}
    for name, (base, spread) in spreads.items():
        noise = np.random.default_rng([zlib.crc32(name.encode()), seed]).standard_normal(out[name].shape)
        drawn = base * np.exp(spread * noise) if base else spread * noise
        out[name] = jnp.asarray(drawn.astype(out[name].dtype))
    for name, factor in factors.items():
        out[name] = (out[name] * factor).astype(out[name].dtype)
    return out
```

```python
from contextlib import ExitStack
from functools import partial

import concourse.bass as bass
from concourse import mybir

F32 = mybir.dt.float32
BF16 = mybir.dt.bfloat16
I32 = mybir.dt.int32
U32 = mybir.dt.uint32
U8 = mybir.dt.uint8
ALU = mybir.AluOpType
ACT = mybir.ActivationFunctionType
AX = mybir.AxisListType

P = 128
B, S, D = 128, 64, 128
HEADS = 16
HD = D // HEADS
TOKENS = B * S
TILES = TOKENS // P
ITERS = TILES // 2
UNITS = 4
SCALE = float(HD) ** -0.5
EPS = 1e-5
MASKED = -1e30

E0, K0, F0 = 32, 4, 128
E1, K1, F1 = 8, 2, 352
F1_BLOCKS = [128, 128, 96]
SLOT_TILES = [TOKENS * K0 // P + E0, TOKENS * K1 // P + E1]
GROUP = 4
LIMIT = 7.0
ARENA = 13824


class Step:

    def __init__(self, m, c, base=0):
        self.m, self.c, self.base = m, c, base
        self.n = m * 2 + c
        self.half = m + c // 2
        self.par = c % 2
        self.g = self.n + base

    def at(self, k):
        return Step(self.m, self.c + k, self.base)

    def first(self, k):
        return isinstance(self.g, int) and self.g < k


def hold(eng, sem, value):
    eng.wait_ge(sem, value)
    eng.nop(nofuse=True)


def build(nc, a, out, xs, ys, bias_parts):
    with ExitStack() as ctx:
        def sb(name, shape, dt=F32):
            return ctx.enter_context(nc.sbuf_tensor(name, shape, dt))

        def sem(name):
            return ctx.enter_context(nc.semaphore(name))

        bank = [ctx.enter_context(nc.psum_tensor(f"bank{i}", [P, 512], F32)) for i in range(8)]

        X = sb("X", [P, TILES, D])
        T = sb("T", [P, TILES, D])
        W = sb("W", [P, E0 * 3 * F0])
        top = sb("top", [P, TILES, 8])
        top_at = sb("top_at", [P, TILES, 8], U32)
        wts = sb("wts", [P, TILES, K0])
        slot = sb("slot", [P, TILES, K0], I32)
        tile_expert = sb("tile_expert", [1, SLOT_TILES[0]], I32)
        ident = sb("ident", [P, P])
        head_of = sb("head_of", [P, 4])
        before = sb("before", [P, P], BF16)
        ones_b = sb("ones_b", [P, P], BF16)
        seq_of = sb("seq_of", [2, P], BF16)
        mask_rows = sb("mask_rows", [2, TILES, S], BF16)
        cos = sb("cos", [P, S])
        sin = sb("sin", [P, S])
        ones_f = sb("ones_f", [P, 1])
        power = sb("power", [P, 2])
        Wm = sb("Wm", [P, 10, D])
        bias_t = sb("bias_t", [P, 6])
        bias_r = sb("bias_r", [P, 5, D])
        gate_w = sb("gate_w", [P, E0 + E1])
        gate_b = sb("gate_b", [P, E0])
        Vbd = [sb(f"Vbd{q}", [P, 8, 4, 2, HD + 1]) for q in range(2)]
        zeros = sb("zeros", [P, 9 * D])

        arena = sb("arena", [P, ARENA])
        place = [0]

        def carve(width, dt=F32):
            lo = place[0]
            place[0] += width if dt in (F32, I32, U32) else (width + 1) // 2
            assert place[0] <= ARENA, place[0]
            v = arena[:, lo:place[0]]
            return v if dt == F32 else v.bitcast(dt)

        def carve2(width, dt=F32):
            return [carve(width, dt) for _ in range(2)]

        W0a = W[:, 0:E0 * 256].rearrange("p (e f) -> p e f", e=E0)
        W0b = W[:, E0 * 256:E0 * 384].rearrange("p (e f) -> p e f", e=E0)
        W1a = W[:, 0:E1 * 704].rearrange("p (e f) -> p e f", e=E1)
        W1b = W[:, E1 * 704:E1 * 1088].rearrange("p (e f) -> p e f", e=E1)
        expert_in = sem("expert_in")

        const_in = sem("const_in")
        setup_dve = sem("setup_dve")
        setup_pool = sem("setup_pool")
        N_CONST = 22
        wide_t = carve(P)
        mask_u8 = arena[0:2, 256:256 + TILES * S // 4].bitcast(U8)
        with nc.Block() as block:
            @block.sync
            def _(sp):
                row = lambda x: x.rearrange("(a n) -> a n", a=1).broadcast_to([P, D])
                col = lambda x: x.rearrange("(n a) -> n a", a=1)
                loads = [(ident[:], a["ident"]), (head_of[:], a["head_of"]), (wide_t, a["before"]),
                         (cos[:], a["cos"]), (sin[:], a["sin"]), (gate_w[:, 0:E0], a["gate0"]),
                         (gate_w[:, E0:E0 + E1], a["gate1"]),
                         (Wm[:].rearrange("p w d -> p (w d)").rearrange("p (w d) -> p w d", w=10), a["proj"]),
                         (gate_b[:], a["L0_ffn_gate_b"].rearrange("(a n) -> a n", a=1).broadcast_to([P, E0])),
                         (mask_u8.rearrange("b (i s) -> b i s", i=TILES),
                          a["mask"].rearrange("(i b) s -> b i s", b=2)),
                         (arena[0:2, 4096:4096 + P], a["seq_of"])]
                for n, name in enumerate(("L0_xattn_bq", "L0_xattn_bk", "L1_xattn_bq", "L1_xattn_bk", "bqr", "bkr")):
                    loads.append((bias_t[:, n:n + 1], col(a[name])))
                for n, name in enumerate(("L0_xattn_bv", "L0_xattn_bo", "L0_ffn_norm_scale", "L1_xattn_bv",
                                          "L1_xattn_bo")):
                    loads.append((bias_r[:, n, :], row(a[name])))
                assert len(loads) == N_CONST
                for dst, src in loads:
                    sp.dma_start(dst, src).then_inc(const_in, 16)
                sp.dma_start(W0a, a["w1_0"]).then_inc(expert_in, 16)
                sp.dma_start(W0b, a["w2_0"]).then_inc(expert_in, 16)

            @block.vector
            def _(dve):
                nc.vector.memset(zeros[:], 0.0)
                nc.vector.memset(ones_b[:], 1.0)
                nc.vector.memset(ones_f[:], 1.0)
                nc.vector.memset(power[:], -0.5)
                dve.wait_ge(const_in, 16 * N_CONST)
                nc.vector.tensor_copy(before[:], wide_t)
                nc.vector.tensor_copy(seq_of[:], arena[0:2, 4096:4096 + P])
                nc.vector.tensor_scalar(mask_rows[:].rearrange("b i s -> b (i s)"), mask_u8, MASKED, None,
                                        ALU.mult).then_inc(setup_dve, 1)
                dve.wait_ge(setup_dve, 1)

            @block.gpsimd
            def _(pool):
                for q in range(2):
                    nc.gpsimd.memset(Vbd[q][:], 0.0).then_inc(setup_pool, 1)
                pool.wait_ge(setup_pool, 2)
                for q in range(2):
                    nc.gpsimd.memset(Vbd[q][0:64, :, :, 0, HD:HD + 1], 1.0)
                    nc.gpsimd.memset(Vbd[q][64:128, :, :, 1, HD:HD + 1], 1.0).then_inc(setup_pool, 1)
                pool.wait_ge(setup_pool, 4)

        x_rows = a["x"].rearrange("b s d -> (b s) d").rearrange("(i p) d -> p i d", p=P)
        ctx_rows = a["ctx_1024"].rearrange("b s d -> (b s) d").rearrange("(i p) d -> p i d", p=P)
        xs_fill = xs.rearrange("(n p r) d -> n p (r d)", p=P, r=9)
        ys_rows = ys.rearrange("(g c p) d -> g p c d", c=GROUP, p=P)
        xs_rows = xs.rearrange("(g c p) d -> g p c d", c=GROUP, p=P)

        x_in = [sem(f"x_in{q}") for q in range(2)]
        ctx_in = [sem(f"ctx_in{q}") for q in range(2)]
        filled = sem("filled")
        gathered = [sem(f"gathered{q}") for q in range(2)]
        names = ("stats_a", "moments_a", "eps_a", "rstd_a", "normed", "cx_psum", "cx", "v_psum", "vbd", "qk_psum",
                 "qk", "rot_psum", "rot", "rope_mul", "rope", "kbd", "score_psum", "score_max", "centred", "t_psum",
                 "probs", "o_psum", "o_copied", "o_recip", "o_normed", "ot_psum", "ot", "wo_psum", "x_plus_bo",
                 "added", "stats_r", "moments_r", "pool_r", "rstd_r", "ms_r", "z", "t_ready", "t_kept", "tt_psum", "tt",
                 "gate_psum", "logits", "top8", "chosen", "top_kept", "index_copied", "combined")
        s = {n: sem(n) for n in names}

        def attention(layer):
            place[0] = 0
            ctx_t = carve2(2 * D)
            xn = carve2(2 * D)
            CX = carve2(4 * D)
            QK = carve2(4 * D)
            QKe, QKr = carve(4 * D), carve(4 * D)
            Kbd = carve2(1024)
            mx = carve(32)
            Sc = carve2(512)
            Pt = carve2(512)
            AO = carve2(2 * HEADS * (HD + 1))
            rec = carve2(2 * HEADS)
            aon = carve2(2 * D)
            aoT = carve2(2 * D)
            xb = carve2(2 * D)
            z = None if layer else carve2(2 * D)
            t = carve2(2 * D)
            tT = carve2(2 * D)
            lg, tp, ta = carve2(2 * (E1 if layer else E0)), carve2(16), carve2(16, U32)
            small = {n: carve2(w) for n, w in (("st_a", 12), ("mv_a", 4), ("ve_a", 2), ("rs_a", 2), ("st_r", 12),
                                               ("mv_r", 4), ("ve_r", 2), ("rs_r", 2), ("ms", 2), ("ms1", 2),
                                               ("ms2", 2), ("r2", 2))}
            gb = carve2(2 * K0 * D) if layer else None
            gi = carve2(2 * K0, I32) if layer else None

            wq, wk, wv, wo = (Wm[:, 4 * layer + n, :] for n in range(4))
            bq, bk = bias_t[:, 2 * layer:2 * layer + 1], bias_t[:, 2 * layer + 1:2 * layer + 2]
            bv, bo = bias_r[:, 3 * layer, :], bias_r[:, 3 * layer + 1, :]
            n_e = E1 if layer else E0
            gw = gate_w[:, E0:E0 + E1] if layer else gate_w[:, 0:E0]
            S_, T_, O_, M_, P_ = bank[0:2], bank[2:4], bank[4:6], bank[6], bank[7]
            base = layer * ITERS

            def tiles(buf, i):
                return buf[:, bass.ds(i.n * 2, 2), :]

            def bodies(eng, body):
                at = lambda k: Step(0, k, base)
                for n in (-1, 0, 1, 2, 3):
                    body(at(n), True, 0 <= n, 1 <= n, 2 <= n)
                with eng.Fori(2, (ITERS - 2) // 2) as m:
                    for c in range(2):
                        body(Step(m, c, base), True, True, True, True)
                body(at(ITERS - 2), True, True, True, True)
                body(at(ITERS - 1), False, True, True, True)
                body(at(ITERS), False, False, True, True)
                body(at(ITERS + 1), False, False, False, True)

            with nc.Block() as block:
                @block.sync
                def _(sp):
                    def load(i):
                        q = i.par
                        if not i.first(2):
                            sp.wait_ge(s["cx_psum"], i.g - 1)
                        sp.dma_start(ctx_t[q].rearrange("p (i d) -> p i d", i=2),
                                     ctx_rows[:, bass.ds(i.n * 2, 2), :]).then_inc(ctx_in[q], 16)
                        if not layer:
                            sp.dma_start(tiles(X, i), x_rows[:, bass.ds(i.n * 2, 2), :]).then_inc(x_in[q], 16)

                    load(Step(0, 0, base))
                    load(Step(0, 1, base))
                    if not layer:
                        sp.dma_start(xs_fill[0], zeros[:]).then_inc(filled, 16)
                        sp.dma_start(xs_fill[1], zeros[:]).then_inc(filled, 16)
                    with sp.Fori(1, ITERS // 2) as m:
                        for c in range(2):
                            i = Step(m, c, base)
                            load(i)
                            if not layer:
                                sp.dma_start(xs_fill[bass.ds(i.n, 1)].rearrange("a p x -> (a p) x"),
                                             zeros[:]).then_inc(filled, 16)
                    if not layer:
                        sp.wait_ge(filled, 16 * ITERS)
                    if layer:
                        sp.dma_start(W1a, a["w13_1"]).then_inc(expert_in, 16)
                        sp.dma_start(W1b[:, :, :], a["w2_1"]).then_inc(expert_in, 16)

                @block.gpsimd
                def _(pool):
                    def rsqrt(out_, src, src_sem, value, mid, mid_sem, done):
                        pool.wait_ge(src_sem, value)
                        nc.gpsimd.tensor_scalar(mid, src, EPS, None, ALU.add).then_inc(mid_sem, 1)

                    def body(i, prep, units, post, last):
                        nx, pv = i.at(1), i.at(-1)
                        if layer and prep:
                            q = nx.par
                            if not (isinstance(nx.n, int) and nx.n < 2):
                                pool.wait_ge(s["combined"], nx.n - 1)
                            nc.gpsimd.tensor_copy(gi[q].rearrange("p (i k) -> p i k", i=2),
                                                  tiles(slot, nx)).then_inc(s["index_copied"], 1)
                            hold(pool, s["index_copied"], nx.n + 1)
                            for k in range(2 * K0):
                                nc.gpsimd.indirect_dma_start(
                                    out=gb[q][:, k * D:(k + 1) * D], out_offset=None, in_=ys,
                                    in_offset=bass.IndirectOffsetOnAxis(ap=gi[q][:, k:k + 1], axis=0),
                                ).then_inc(gathered[q], 16)
                        if prep:
                            q = nx.par
                            ve, rs = small["ve_a"][q], small["rs_a"][q]
                            hold(pool, s["moments_a"], nx.g + 1)
                            nc.gpsimd.tensor_scalar(ve, small["mv_a"][q].rearrange("p (i c) -> p i c", i=2)[:, :, 1],
                                                    EPS, None, ALU.add).then_inc(s["eps_a"], 1)
                            pool.wait_ge(s["eps_a"], nx.g + 1)
                            nc.gpsimd.tensor_tensor(rs, ve, power[:], ALU.pow).then_inc(s["rstd_a"], 1)
                        if post:
                            q = pv.par
                            if not pv.first(2):
                                hold(pool, s["added"], pv.g - 1)
                            nc.gpsimd.tensor_tensor(xb[q].rearrange("p (i d) -> p i d", i=2), tiles(X, pv),
                                                    bo.unsqueeze(1).broadcast_to([P, 2, D]),
                                                    ALU.add).then_inc(s["x_plus_bo"], 1)
                        if prep:
                            q = nx.par
                            pool.wait_ge(s["rope"] if layer else s["qk"], (nx.n if layer else nx.g) + 1)
                            kk = QK[q][:, 2 * D:4 * D].rearrange("p (b k) -> p b k", b=4)
                            nc.gpsimd.tensor_tensor(
                                Kbd[q].rearrange("p (b j k) -> p b j k", b=4, j=4),
                                kk.unsqueeze(2).broadcast_to([P, 4, 4, S]),
                                head_of[:].unsqueeze(1).unsqueeze(3).broadcast_to([P, 4, 4, S]),
                                ALU.mult).then_inc(s["kbd"], 1)
                        if post:
                            q = pv.par
                            mv, ve, rs = small["mv_r"][q], small["ve_r"][q], small["rs_r"][q]
                            var = mv.rearrange("p (i c) -> p i c", i=2)[:, :, 1]
                            hold(pool, s["moments_r"], pv.g + 1)
                            nc.gpsimd.tensor_scalar(ve, var, EPS, None, ALU.add).then_inc(s["pool_r"], 1)
                            pool.wait_ge(s["pool_r"], pv.g + 1)
                            nc.gpsimd.tensor_tensor(rs, ve, power[:], ALU.pow).then_inc(s["rstd_r"], 1)
                            if not layer:
                                ms, ms1, ms2 = small["ms"][q], small["ms1"][q], small["ms2"][q]
                                pool.wait_ge(s["rstd_r"], pv.g + 1)
                                nc.gpsimd.tensor_tensor(ms, rs, rs, ALU.mult).then_inc(s["ms_r"], 1)
                                pool.wait_ge(s["ms_r"], pv.g * 4 + 1)
                                nc.gpsimd.tensor_tensor(ms1, ms, var, ALU.mult).then_inc(s["ms_r"], 1)
                                hold(pool, s["ms_r"], pv.g * 4 + 2)
                                nc.gpsimd.tensor_scalar(ms2, ms1, EPS, None, ALU.add).then_inc(s["ms_r"], 1)
                                pool.wait_ge(s["ms_r"], pv.g * 4 + 3)
                                nc.gpsimd.tensor_tensor(small["r2"][q], ms2, power[:], ALU.pow).then_inc(s["ms_r"], 1)
                            hold(pool, s["t_ready"], pv.g + 1)
                            if not layer:
                                nc.gpsimd.tensor_tensor(tiles(X, pv), tiles(X, pv),
                                                        z[q].rearrange("p (i d) -> p i d", i=2), ALU.add)
                            nc.gpsimd.tensor_copy(tiles(T, pv), t[q].rearrange("p (i d) -> p i d", i=2)
                                                  ).then_inc(s["t_kept"], 1)

                        if last:
                            pp = i.at(-2)
                            pool.wait_ge(s["chosen"], pp.g + 1)
                            nc.gpsimd.tensor_copy(tiles(top, pp), tp[pp.par].rearrange("p (i e) -> p i e", i=2))
                            nc.gpsimd.tensor_copy(tiles(top_at, pp), ta[pp.par].rearrange("p (i e) -> p i e", i=2)
                                                  ).then_inc(s["top_kept"], 1)

                    bodies(pool, body)

                @block.vector
                def _(dve):
                    def stats(i, st, mv, stats_sem, moments_sem):
                        q = i.par
                        for j in range(2):
                            nc.vector.bn_stats(st[q][:, 6 * j:6 * j + 6],
                                               X[:, bass.ds(i.n * 2 + j, 1), :].rearrange("p i d -> p (i d)")
                                               ).then_inc(s[stats_sem], 1)
                        hold(dve, s[stats_sem], i.g * 2 + 2)
                        for j in range(2):
                            last = nc.vector.bn_aggr(mv[q][:, 2 * j:2 * j + 2], st[q][:, 6 * j:6 * j + 6])
                        last.then_inc(s[moments_sem], 1)

                    def normalise(i, dst, mv, rs):
                        q = i.par
                        for j in range(2):
                            last = nc.vector.tensor_scalar(
                                dst[q][:, j * D:(j + 1) * D],
                                X[:, bass.ds(i.n * 2 + j, 1), :].rearrange("p i d -> p (i d)"),
                                mv[q][:, 2 * j:2 * j + 1], rs[q][:, j:j + 1], ALU.subtract, ALU.mult)
                        return last

                    def combine(i):
                        q = i.par
                        dve.wait_ge(gathered[q], (i.half + 1) * 16 * 2 * K0)
                        for k in range(K0):
                            for j in range(2):
                                xt = X[:, bass.ds(i.n * 2 + j, 1), :].rearrange("p i d -> p (i d)")
                                at = (j * K0 + k) * D
                                last = nc.vector.scalar_tensor_tensor(
                                    xt, gb[q][:, at:at + D], wts[:, bass.ds(i.n * 2 + j, 1), k], xt,
                                    ALU.mult, ALU.add)
                            if k < K0 - 1:
                                last.then_inc(combine_step, 1)
                                dve.wait_ge(combine_step, i.n * (K0 - 1) + k + 1)
                        last.then_inc(s["combined"], 1)

                    def score_unit(i, r):
                        g4 = i.g * UNITS
                        dve.wait_ge(s["score_psum"], g4 + r + 1)
                        src = S_[r % 2][:, :].rearrange("p (h k) -> p h k", k=S)
                        m8 = mx[:, 8 * r:8 * r + 8]
                        nc.vector.tensor_reduce(m8, src, AX.X, ALU.max).then_inc(s["score_max"], 1)
                        dve.wait_ge(s["score_max"], g4 + r + 1)
                        nc.vector.tensor_tensor(Sc[r % 2].rearrange("p (h k) -> p h k", k=S), src,
                                                m8.unsqueeze(2).broadcast_to([P, 8, S]),
                                                ALU.subtract).then_inc(s["centred"], 1)

                    def body(i, prep, units, post, last):
                        nx, pv, pp = i.at(1), i.at(-1), i.at(-2)
                        if last:
                            dve.wait_ge(s["gate_psum"], pp.g + 1)
                            src = P_[:, 0:2 * n_e].rearrange("p (i e) -> p i e", i=2)
                            q = pp.par
                            dst = lg[q][:, 0:2 * n_e].rearrange("p (i e) -> p i e", i=2)
                            if layer:
                                nc.vector.tensor_copy(dst, src).then_inc(s["logits"], 1)
                            else:
                                nc.vector.tensor_tensor(dst, src, gate_b[:].unsqueeze(1).broadcast_to([P, 2, E0]),
                                                        ALU.add).then_inc(s["logits"], 1)
                            hold(dve, s["logits"], pp.g + 1)
                            for j in range(2):
                                nc.vector.max(tp[q][:, 8 * j:8 * j + 8], lg[q][:, j * n_e:(j + 1) * n_e]
                                              ).then_inc(s["top8"], 1)
                            hold(dve, s["top8"], pp.g * 2 + 2)
                            for j in range(2):
                                last_ = nc.vector.max_index(ta[q][:, 8 * j:8 * j + 8], tp[q][:, 8 * j:8 * j + 8],
                                                            lg[q][:, j * n_e:(j + 1) * n_e])
                            last_.then_inc(s["chosen"], 1)
                        if post:
                            q = pv.par
                            dve.wait_ge(s["o_copied"], pv.g + 1)
                            ao = AO[q].rearrange("p (h c) -> p h c", c=HD + 1)
                            nc.vector.reciprocal(rec[q].unsqueeze(2), ao[:, :, HD:HD + 1]).then_inc(s["o_recip"], 1)
                            dve.wait_ge(s["o_recip"], pv.g + 1)
                            nc.vector.tensor_tensor(aon[q].rearrange("p (h c) -> p h c", c=HD), ao[:, :, 0:HD],
                                                    rec[q].unsqueeze(2).broadcast_to([P, 2 * HEADS, HD]),
                                                    ALU.mult).then_inc(s["o_normed"], 1)
                        if prep:
                            if layer:
                                combine(nx)
                                hold(dve, s["combined"], nx.n + 1)
                            else:
                                hold(dve, x_in[nx.par], (nx.half + 1) * 16)
                            stats(nx, small["st_a"], small["mv_a"], "stats_a", "moments_a")
                        if units:
                            score_unit(i, 0)
                        if prep:
                            dve.wait_ge(s["rstd_a"], nx.g + 1)
                            normalise(nx, xn, small["mv_a"], small["rs_a"]).then_inc(s["normed"], 1)
                        if units:
                            score_unit(i, 1)
                            score_unit(i, 2)
                        if post:
                            q = pv.par
                            dve.wait_ge(s["wo_psum"], pv.g + 1)
                            dve.wait_ge(s["x_plus_bo"], pv.g + 1)
                            nc.vector.tensor_tensor(tiles(X, pv), P_[:, 0:2 * D].rearrange("p (i d) -> p i d", i=2),
                                                    xb[q].rearrange("p (i d) -> p i d", i=2),
                                                    ALU.add).then_inc(s["added"], 1)
                            hold(dve, s["added"], pv.g + 1)
                            stats(pv, small["st_r"], small["mv_r"], "stats_r", "moments_r")
                        if units:
                            score_unit(i, 3)
                        if prep:
                            q = nx.par
                            dve.wait_ge(s["v_psum"], nx.g + 1)
                            for u in range(2):
                                rows = slice(64 * u, 64 * u + 64)
                                src = M_[rows, :].rearrange("p (b h u d) -> p h b u d", b=4, u=2, d=HD)[:, :, :, u, :]
                                bvv = bv[rows, :].rearrange("p (h u d) -> p h u d", u=2, d=HD)[:, :, u, :]
                                last_ = nc.vector.tensor_tensor(
                                    Vbd[q][rows, :, :, u, 0:HD], src,
                                    bvv.unsqueeze(2).broadcast_to([64, 8, 4, HD]), ALU.add)
                            last_.then_inc(s["vbd"], 1)
                        if prep and layer:
                            q = nx.par
                            dve.wait_ge(s["rot"], nx.n + 1)
                            for buf, tab in ((QKe, cos), (QKr, sin)):
                                v = buf.rearrange("p (b s) -> p b s", s=S)
                                nc.vector.tensor_tensor(v, v, tab[:].unsqueeze(1).broadcast_to([P, 8, S]),
                                                        ALU.mult).then_inc(s["rope_mul"], 1)
                            dve.wait_ge(s["rope_mul"], nx.n * 2 + 2)
                            nc.vector.tensor_tensor(QK[q], QKe, QKr, ALU.add).then_inc(s["rope"], 1)
                        if post:
                            q = pv.par
                            dve.wait_ge(s["rstd_r"], pv.g + 1)
                            if not pv.first(2):
                                dve.wait_ge(s["t_kept"], pv.g - 1)
                            if layer:
                                normalise(pv, t, small["mv_r"], small["rs_r"]).then_inc(s["t_ready"], 1)
                            else:
                                normalise(pv, z, small["mv_r"], small["rs_r"]).then_inc(s["z"], 1)
                                dve.wait_ge(s["z"], pv.g + 1)
                                dve.wait_ge(s["ms_r"], pv.g * 4 + 4)
                                for j in range(2):
                                    last_ = nc.vector.scalar_tensor_tensor(
                                        t[q][:, j * D:(j + 1) * D], z[q][:, j * D:(j + 1) * D],
                                        small["r2"][q][:, j:j + 1], bias_r[:, 2, :], ALU.mult, ALU.mult)
                                last_.then_inc(s["t_ready"], 1)

                    bodies(dve, body)

                @block.scalar
                def _(act):
                    def project(dst, src_bank, b0, b1):
                        nc.scalar.activation(dst[:, 0:2 * D], src_bank[:, 0:2 * D], ACT.Identity, bias=b0)
                        return nc.scalar.activation(dst[:, 2 * D:4 * D], src_bank[:, 2 * D:4 * D], ACT.Identity,
                                                    bias=b1)

                    def exps(i, r):
                        act.wait_ge(s["t_psum"], i.g * UNITS + r + 1)
                        nc.scalar.activation(Pt[r % 2], T_[r % 2][:, :], ACT.Exp, scale=SCALE
                                             ).then_inc(s["probs"], 1)

                    def body(i, prep, units, post, last):
                        nx, pv = i.at(1), i.at(-1)
                        if post:
                            act.wait_ge(s["ot_psum"], pv.g + 1)
                            nc.scalar.activation(aoT[pv.par], P_[:, 0:2 * D], ACT.Copy).then_inc(s["ot"], 1)
                        if units:
                            exps(i, 0)
                        if prep:
                            act.wait_ge(s["cx_psum"], nx.g + 1)
                            nc.scalar.activation(CX[nx.par], M_[:, :], ACT.Copy).then_inc(s["cx"], 1)
                        if units:
                            exps(i, 1)
                            exps(i, 2)
                        if prep:
                            act.wait_ge(s["qk_psum"], nx.g + 1)
                            if layer:
                                if not (isinstance(nx.n, int) and nx.n < 1):
                                    act.wait_ge(s["rope"], nx.n)
                                project(QKe, P_, bq, bk).then_inc(s["qk"], 1)
                                act.wait_ge(s["rot_psum"], nx.n + 1)
                                project(QKr, P_, bias_t[:, 4:5], bias_t[:, 5:6]).then_inc(s["rot"], 1)
                            else:
                                project(QK[nx.par], P_, bq, bk).then_inc(s["qk"], 1)
                        if units:
                            exps(i, 3)
                        if post:
                            act.wait_ge(s["tt_psum"], pv.g + 1)
                            nc.scalar.activation(tT[pv.par], M_[:, 0:2 * D], ACT.Copy).then_inc(s["tt"], 1)
                        if units:
                            act.wait_ge(s["o_psum"], i.g + 1)
                            for w in range(2):
                                for b in range(2):
                                    rows = slice(64 * b, 64 * b + 64)
                                    c = 2 * (HD + 1)
                                    src = O_[w][rows, 0:16 * c].rearrange("p (h b c) -> p h b c", h=8, b=2)[:, :, b, :]
                                    dst = AO[i.par][rows, w * 8 * c:(w + 1) * 8 * c].rearrange("p (h c) -> p h c", h=8)
                                    last_ = nc.scalar.activation(dst, src, ACT.Copy)
                            last_.then_inc(s["o_copied"], 1)

                    bodies(act, body)

                @block.tensor
                def _(pe):
                    def scores(i, r):
                        g4 = i.g * UNITS
                        if not (isinstance(g4, int) and g4 + r < 2):
                            (pe.wait_ge if layer else partial(hold, pe))(s["centred"], g4 + r - 1)
                        sbk = S_[r % 2]
                        if not layer:
                            nc.tensor.matmul(sbk[:, :].rearrange("p (w j k) -> p w j k", w=2, j=4), seq_of[:],
                                             mask_rows[:, bass.ds(i.n * 2, 2), :].unsqueeze(2)
                                             .broadcast_to([2, 2, 4, S]), start=True, stop=False,
                                             skip_group_check=True)
                        rows = slice(32 * r, 32 * r + 32)
                        for w in range(2):
                            for b in range(2):
                                sq = 2 * w + b
                                last = nc.tensor.matmul(
                                    sbk[64 * b:64 * b + 64, 256 * w:256 * w + 256],
                                    QK[i.par][rows, 64 * sq:64 * sq + 64], Kbd[i.par][rows, 256 * sq:256 * sq + 256],
                                    start=bool(layer), stop=True, skip_group_check=True)
                        last.then_inc(s["score_psum"], 1)

                    def turn(i, r):
                        pe.wait_ge(s["centred"], i.g * UNITS + r + 1)
                        for k in range(4):
                            last = nc.tensor.transpose(T_[r % 2][:, k * P:(k + 1) * P],
                                                       Sc[r % 2][:, k * P:(k + 1) * P], ident[:])
                        last.then_inc(s["t_psum"], 1)

                    def values(i, r):
                        if r == 0:
                            pe.wait_ge(s["vbd"], i.g + 1)
                            if not i.first(1):
                                pe.wait_ge(s["o_copied"], i.g)
                        pe.wait_ge(s["probs"], i.g * UNITS + r + 1)
                        c = 4 * (HD + 1)
                        for w in range(2):
                            for jj in range(2):
                                hp = 2 * r + jj
                                k = 2 * w + jj
                                last = nc.tensor.matmul(
                                    O_[w][:, c * hp:c * hp + c], Pt[r % 2][:, k * P:(k + 1) * P],
                                    Vbd[i.par][:, hp, 2 * w:2 * w + 2, :, :], start=True, stop=True)
                        if r == UNITS - 1:
                            last.then_inc(s["o_psum"], 1)

                    def body(i, prep, units, post, last):
                        nx, pv, pp = i.at(1), i.at(-1), i.at(-2)
                        if units:
                            pe.wait_ge(s["kbd"], i.g + 1)
                            scores(i, 0)
                            scores(i, 1)
                        if post:
                            q = pv.par
                            pe.wait_ge(s["o_normed"], pv.g + 1)
                            if not pv.first(1):
                                pe.wait_ge(s["logits"], pv.g)
                            for w in range(2):
                                last_ = nc.tensor.transpose(P_[:, w * P:(w + 1) * P], aon[q][:, w * P:(w + 1) * P],
                                                            ident[:])
                            last_.then_inc(s["ot_psum"], 1)
                        if units:
                            turn(i, 0)
                            scores(i, 2)
                        if prep:
                            q = nx.par
                            pe.wait_ge(ctx_in[q], (nx.half + nx.base // 2 + 1) * 16)
                            pe.wait_ge(s["normed"], nx.g + 1)
                            if not nx.first(1):
                                pe.wait_ge(s["vbd"], nx.g)
                            if not nx.first(3):
                                pe.wait_ge(s["tt"], nx.g - 2)
                            for w in range(2):
                                nc.tensor.transpose(M_[:, w * P:(w + 1) * P], ctx_t[q][:, w * P:(w + 1) * P], ident[:])
                            for w in range(2):
                                last_ = nc.tensor.transpose(M_[:, (2 + w) * P:(3 + w) * P],
                                                            xn[q][:, w * P:(w + 1) * P], ident[:])
                            last_.then_inc(s["cx_psum"], 1)
                        if units:
                            values(i, 0)
                            turn(i, 1)
                        if post:
                            pe.wait_ge(s["ot"], pv.g + 1)
                            for w in range(2):
                                last_ = nc.tensor.matmul(P_[:, w * P:(w + 1) * P], aoT[q_(pv)][:, w * P:(w + 1) * P],
                                                         wo, start=True, stop=True)
                            last_.then_inc(s["wo_psum"], 1)
                        if units:
                            scores(i, 3)
                            values(i, 1)
                        if prep:
                            q = nx.par
                            pe.wait_ge(s["cx"], nx.g + 1)
                            for b in range(4):
                                for u in range(2):
                                    last_ = nc.tensor.matmul(M_[64 * u:64 * u + 64, b * P:(b + 1) * P],
                                                             CX[q][:, b * S:(b + 1) * S], wv, start=True, stop=True)
                            last_.then_inc(s["v_psum"], 1)
                        if units:
                            turn(i, 2)
                        if prep:
                            q = nx.par
                            if post:
                                pe.wait_ge(s["added"], pv.g + 1)
                            nc.tensor.matmul(P_[:, 0:2 * D], wq, CX[q][:, 2 * D:4 * D], start=True, stop=True)
                            nc.tensor.matmul(P_[:, 2 * D:4 * D], wk, CX[q][:, 0:2 * D], start=True, stop=True
                                             ).then_inc(s["qk_psum"], 1)
                        if units:
                            values(i, 2)
                        if prep and layer:
                            pe.wait_ge(s["qk"], nx.g + 1)
                            nc.tensor.matmul(P_[:, 0:2 * D], Wm[:, 8, :], CX[q][:, 2 * D:4 * D], start=True, stop=True)
                            nc.tensor.matmul(P_[:, 2 * D:4 * D], Wm[:, 9, :], CX[q][:, 0:2 * D], start=True, stop=True
                                             ).then_inc(s["rot_psum"], 1)
                        if units:
                            turn(i, 3)
                        if post:
                            pe.wait_ge(s["t_ready"], pv.g + 1)
                            if prep:
                                pe.wait_ge(s["vbd"], nx.g + 1)
                            for w in range(2):
                                last_ = nc.tensor.transpose(M_[:, w * P:(w + 1) * P],
                                                            t[pv.par][:, w * P:(w + 1) * P], ident[:])
                            last_.then_inc(s["tt_psum"], 1)
                        if units:
                            values(i, 3)
                        if post:
                            pe.wait_ge(s["tt"], pv.g + 1)
                            if prep:
                                pe.wait_ge(s["rot"] if layer else s["qk"], (nx.n if layer else nx.g) + 1)
                            for w in range(2):
                                last_ = nc.tensor.matmul(P_[:, w * n_e:(w + 1) * n_e],
                                                         tT[pv.par][:, w * P:(w + 1) * P], gw, start=True, stop=True)
                            last_.then_inc(s["gate_psum"], 1)

                    q_ = lambda i: i.par
                    bodies(pe, body)

        combine_step = sem("combine_step")

        chain = sem("chain")
        chained = [0]
        hot = sem("hot")
        ranks = sem("ranks")
        expo = sem("expo")
        at_least = sem("at_least")
        owner = sem("owner")
        slot_iota = sem("slot_iota")
        index_in = sem("index_in")
        moved = [sem(f"moved{q}") for q in range(2)]
        scattered = [sem(f"scattered{q}") for q in range(2)]
        b_in, b_moved = sem("b_in"), sem("b_moved")

        def slots(layer):
            E, K = (E1, K1) if layer else (E0, K0)
            NT = SLOT_TILES[layer]
            TE = TILES * E
            chunks = TE // 512
            place[0] = 0
            oh = [carve(TE, BF16) for _ in range(K)]
            CT, INC, POS = (carve(TE) for _ in range(3))
            TMP = CT
            iota_e = carve(E)
            at_f = carve(TILES * K)
            expw = carve(TILES * K)
            wsum = carve(TILES)
            wrec = carve(TILES)
            count = carve(E)
            count_i = carve(E, I32)
            padded = carve(E)
            pad_end = carve(E)
            shift = carve(E)
            diag = carve(E)
            my_end = carve(1)
            slot_f = carve(TILES * K)
            start_of_tile = carve(NT)
            ge = carve(NT, BF16)
            e_f = carve(NT)
            ie = lambda v: v.rearrange("p (i e) -> p i e", e=E)
            ei = lambda v: v.rearrange("p (e i) -> p e i", e=E)
            ik = lambda v: v.rearrange("p (i k) -> p i k", k=K)

            with nc.Block() as block:
                @block.gpsimd
                def _(pool):
                    nc.gpsimd.iota(iota_e, pattern=[[1, E]], base=0, channel_multiplier=0,
                                   allow_small_or_imprecise_dtypes=True).then_inc(slot_iota, 1)
                    nc.gpsimd.iota(start_of_tile, pattern=[[P, NT]], base=0, channel_multiplier=0,
                                   allow_small_or_imprecise_dtypes=True).then_inc(slot_iota, 1)

                @block.vector
                def _(dve):
                    def link(ins):
                        chained[0] += 1
                        ins.then_inc(chain, 1)
                        dve.wait_ge(chain, chained[0])

                    nc.vector.tensor_copy(ik(at_f), top_at[:, :, 0:K])
                    link(nc.vector.tensor_tensor(ik(expw), top[:, :, 0:K],
                                                 top[:, :, 0:1].broadcast_to([P, TILES, K]), ALU.subtract))
                    dve.wait_ge(slot_iota, 2 * layer + 2)
                    for k in range(K):
                        nc.vector.tensor_tensor(ie(oh[k]), iota_e.unsqueeze(1).broadcast_to([P, TILES, E]),
                                                ik(at_f)[:, :, k:k + 1].broadcast_to([P, TILES, E]),
                                                ALU.is_equal).then_inc(hot, 1)
                    dve.wait_ge(expo, layer + 1)
                    link(nc.vector.tensor_reduce(wsum, ik(expw), AX.X, ALU.add))
                    link(nc.vector.reciprocal(wrec, wsum))
                    link(nc.vector.tensor_tensor(wts[:, :, 0:K], ik(expw),
                                                 wrec.unsqueeze(2).broadcast_to([P, TILES, K]), ALU.mult))
                    dve.wait_ge(ranks, layer + 1)
                    w = 512 // E
                    for c in range(chunks):
                        last = nc.vector.tensor_copy(ei(CT)[:, :, c * w:(c + 1) * w],
                                                     bank[4 + c][:, :].rearrange("p (i e) -> p e i", e=E))
                    link(last)
                    link(nc.vector.tensor_tensor_scan(INC, ones_f[:].broadcast_to([P, TE]), CT, 0.0,
                                                      ALU.mult, ALU.add))
                    ends = ei(INC)[:, :, TILES - 1]
                    nc.vector.tensor_copy(count[:, 0:1], ends[:, 0:1])
                    link(nc.vector.tensor_tensor(count[:, 1:E], ends[:, 1:E], ends[:, 0:E - 1], ALU.subtract))
                    link(nc.vector.tensor_scalar(count_i, count, float(P - 1), None, ALU.add))
                    link(nc.vector.tensor_scalar(count_i, count_i, -P, None, ALU.bitwise_and))
                    link(nc.vector.tensor_copy(padded, count_i))
                    link(nc.vector.tensor_tensor_scan(pad_end, ones_f[:].broadcast_to([P, E]), padded, 0.0,
                                                      ALU.mult, ALU.add))
                    link(nc.vector.tensor_tensor(shift, pad_end, padded, ALU.subtract))
                    link(nc.vector.tensor_tensor(shift, shift, ends, ALU.subtract))
                    link(nc.vector.tensor_tensor(shift, shift, count, ALU.add))
                    link(nc.vector.tensor_tensor(diag[0:E, :], pad_end[0:E, :], ident[0:E, 0:E], ALU.mult))
                    link(nc.vector.tensor_reduce(my_end[0:E, :], diag[0:E, :], AX.X, ALU.add))
                    nc.vector.tensor_scalar(ge[0:E, :], start_of_tile[0:E, :], my_end[0:E, :], None,
                                            ALU.is_ge).then_inc(at_least, 1)
                    link(nc.vector.tensor_tensor(INC, INC, CT, ALU.subtract))
                    link(nc.vector.tensor_tensor(ei(INC), ei(INC), shift.unsqueeze(2).broadcast_to([P, E, TILES]),
                                                 ALU.add))
                    for c in range(chunks):
                        last = nc.vector.tensor_tensor(ie(POS)[:, c * w:(c + 1) * w, :],
                                                       bank[c][:, :].rearrange("p (i e) -> p i e", e=E),
                                                       INC.rearrange("p (e i) -> p i e", e=E)[:, c * w:(c + 1) * w, :],
                                                       ALU.add)
                    link(last)
                    for k in range(K):
                        link(nc.vector.tensor_tensor(TMP, oh[k], POS, ALU.mult))
                        link(nc.vector.tensor_reduce(ik(slot_f)[:, :, k], ie(TMP), AX.X, ALU.add))
                    link(nc.vector.tensor_copy(slot[:, :, 0:K], ik(slot_f)))
                    dve.wait_ge(owner, layer + 1)
                    link(nc.vector.tensor_scalar(e_f[0:1, :], bank[7][0:1, 0:NT] if not layer else bank[1][0:1, 0:NT],
                                                 float(E - 1), None, ALU.min))
                    link(nc.vector.tensor_copy(tile_expert[0:1, 0:NT], e_f[0:1, :]))

                @block.scalar
                def _(act):
                    act.wait_ge(chain, chained_before + 1)
                    nc.scalar.activation(expw, expw, ACT.Exp).then_inc(expo, 1)

                @block.tensor
                def _(pe):
                    for k in range(K):
                        pe.wait_ge(hot, layer * K0 + k + 1)
                        for c in range(chunks):
                            nc.tensor.matmul(bank[c][:, :], before[:], oh[k][:, 512 * c:512 * c + 512],
                                             start=(k == 0), stop=(k == K - 1))
                            last = nc.tensor.matmul(bank[4 + c][:, :], ones_b[:], oh[k][:, 512 * c:512 * c + 512],
                                                    start=(k == 0), stop=(k == K - 1))
                    last.then_inc(ranks, 1)
                    pe.wait_ge(at_least, layer + 1)
                    dst = bank[7] if not layer else bank[1]
                    nc.tensor.matmul(dst[0:1, 0:NT], ones_b[0:E, 0:1], ge[0:E, :], start=True, stop=True
                                     ).then_inc(owner, 1)

        def dispatch(layer):
            K = K1 if layer else K0
            place[0] = 0
            rows = carve2(GROUP * D)
            idx = carve2(GROUP * K, I32)
            count = TILES // GROUP
            base = layer * (TILES // GROUP)
            with nc.Block() as block:
                @block.scalar
                def _(act):
                    def move(i, skip):
                        q = i.par
                        if not skip:
                            act.wait_ge(scattered[q], i.half * 16 * GROUP * K + done[layer])
                        nc.scalar.activation(rows[q].rearrange("p (i d) -> p i d", i=GROUP),
                                             T[:, bass.ds(i.n * GROUP, GROUP), :], ACT.Copy).then_inc(moved[q], 1)

                    move(Step(0, 0), True)
                    move(Step(0, 1), True)
                    with act.Fori(1, count // 2) as m:
                        for c in range(2):
                            move(Step(m, c), False)

                @block.gpsimd
                def _(pool):
                    with pool.Fori(0, count // 2) as m:
                        for c in range(2):
                            i = Step(m, c, base)
                            q = i.par
                            nc.gpsimd.tensor_copy(idx[q].rearrange("p (i k) -> p i k", i=GROUP),
                                                  slot[:, bass.ds(i.n * GROUP, GROUP), 0:K]).then_inc(index_in, 1)
                            pool.wait_ge(index_in, i.g + 1)
                            hold(pool, moved[q], i.half + base // 2 + 1)
                            for t in range(GROUP):
                                for k in range(K):
                                    nc.gpsimd.indirect_dma_start(
                                        out=xs, out_offset=bass.IndirectOffsetOnAxis(
                                            ap=idx[q][:, t * K + k:t * K + k + 1], axis=0),
                                        in_=rows[q][:, t * D:(t + 1) * D], in_offset=None,
                                    ).then_inc(scattered[q], 16)
                            pool.wait_ge(scattered[q], (i.half + 1) * 16 * GROUP * K + done[layer])

        done = [0, 16 * TILES * K0 // 2]

        slots_in = [sem(f"slots_in{q}") for q in range(2)]
        results_out = [sem(f"results_out{q}") for q in range(2)]
        e = {n: sem(n) for n in ("xt_psum", "xt", "h_psum", "clipped", "gated", "hidden", "ht_psum", "ht", "y_psum",
                                 "y")}
        e1 = {n: sem(n) for n in ("h1_psum", "silu1", "hidden1", "ht1_psum", "ht1", "y1_psum")}

        def load_and_store(block, XE, YE, groups, base):
            @block.sync
            def _(sp):
                def load(i):
                    if not i.first(2):
                        sp.wait_ge(e["xt_psum"], i.g - 1)
                    sp.dma_start(XE[i.par].rearrange("p (c d) -> p c d", c=GROUP),
                                 xs_rows[bass.ds(i.n, 1)].rearrange("a p c d -> p (a c) d")
                                 ).then_inc(slots_in[i.par], 16)

                def store(i):
                    sp.wait_ge(e["y"], i.g + 1)
                    sp.dma_start(ys_rows[bass.ds(i.n, 1)].rearrange("a p c d -> p (a c) d"),
                                 YE[i.par].rearrange("p (c d) -> p c d", c=GROUP)
                                 ).then_inc(results_out[i.par], 16)

                at = lambda k: Step(0, k, base)
                load(at(0))
                load(at(1))
                with sp.Fori(0, groups // 2 - 1) as m:
                    for c in range(2):
                        load(Step(m, c + 2, base))
                        store(Step(m, c, base))
                store(at(groups - 2))
                store(at(groups - 1))
                for q in range(2):
                    sp.wait_ge(results_out[q], 16 * (groups + base) // 2)

        def pipeline(eng, groups, base, body):
            at = lambda k: Step(0, k, base)
            body(at(-1), True, False, False)
            body(at(0), True, True, False)
            for n in (1, 2, 3):
                body(at(n), True, True, True)
            with eng.Fori(2, groups // 2 - 1) as m:
                for c in range(2):
                    body(Step(m, c, base), True, True, True)
            body(at(groups - 2), True, True, True)
            body(at(groups - 1), False, True, True)
            body(at(groups), False, False, True)

        def transposed_rows(i, pe, XE, A_):
            pe.wait_ge(slots_in[i.par], (i.half + i.base // 2 + 1) * 16)
            if not i.first(2):
                pe.wait_ge(e["xt"], i.g - 1)
            for c in range(GROUP):
                last = nc.tensor.transpose(A_[i.par][:, c * P:(c + 1) * P], XE[i.par][:, c * P:(c + 1) * P], ident[:])
            last.then_inc(e["xt_psum"], 1)

        def expert_of(pe, i, c, experts):
            return pe.value_load(tile_expert[0:1, bass.ds(i.n * GROUP + c, 1)], min_val=0, max_val=experts - 1)

        def experts0():
            groups = SLOT_TILES[0] // GROUP
            place[0] = 0
            XE, XT, GL, LN, HA, AT, YE = (carve2(GROUP * D) for _ in range(7))
            AG = GL
            b12 = carve(E0 * 384, BF16)[0:3, :].rearrange("r (e f) -> r e f", e=E0)
            A_, H_, C_, Y_ = bank[0:2], bank[2:6], bank[6], bank[7]
            part_f, rest = HA[0][0:E0, 0:384], AT[0][0:E0, 0:384]
            parts = [XE[0], XE[1], XT[0]]
            parts = [p.bitcast(BF16)[0:E0, 0:384] for p in parts]
            with nc.Block() as block:
                @block.sync
                def _(sp):
                    sp.dma_start(part_f[:, 0:256], a["b1_0"]).then_inc(b_in, 16)
                    sp.dma_start(part_f[:, 256:384], a["L0_ffn_b2"]).then_inc(b_in, 16)
                    for n in range(3):
                        sp.wait_ge(b_moved, 1 + 2 * n if n < 2 else 4)
                        sp.dma_start(bias_parts[n], parts[n]).then_inc(b_in, 16)
                    sp.wait_ge(b_in, 80)
                    sp.dma_start(b12, bias_parts).then_inc(b_in, 16)
                    sp.wait_ge(b_in, 96)
                    sp.wait_ge(expert_in, 32)

                @block.vector
                def _(dve):
                    dve.wait_ge(b_in, 32)
                    nc.vector.tensor_copy(parts[0], part_f).then_inc(b_moved, 1)
                    dve.wait_ge(b_moved, 1)
                    nc.vector.tensor_tensor(rest, part_f, parts[0], ALU.subtract).then_inc(b_moved, 1)
                    dve.wait_ge(b_moved, 2)
                    nc.vector.tensor_copy(parts[1], rest).then_inc(b_moved, 1)
                    dve.wait_ge(b_moved, 3)
                    nc.vector.tensor_tensor(parts[2], rest, parts[1], ALU.subtract).then_inc(b_moved, 1)

            with nc.Block() as block:
                load_and_store(block, XE, YE, groups, 0)

                @block.tensor
                def _(pe):
                    def hidden(i, half):
                        if half == 0:
                            pe.wait_ge(e["xt"], i.g + 1)
                        if not i.first(2):
                            pe.wait_ge(e["clipped"], (i.g - 2) * 2 + half + 1)
                        pe.nop(nofuse=True)
                        for c in (2 * half, 2 * half + 1):
                            x_e = expert_of(pe, i, c, E0)
                            h = H_[2 * i.par + half][:, 256 * (c % 2):256 * (c % 2) + 256]
                            nc.tensor.matmul(h, ones_b[0:3, :], b12[:, bass.ds(x_e, 1), 0:256], start=True, stop=False,
                                             skip_group_check=True)
                            last = nc.tensor.matmul(h, XT[i.par][:, c * P:(c + 1) * P], W0a[:, bass.ds(x_e, 1), :],
                                                    start=False, stop=True, skip_group_check=True)
                        last.then_inc(e["h_psum"], 1)

                    def body(i, ahead, main, behind):
                        nx, pv = i.at(1), i.at(-1)
                        if ahead:
                            transposed_rows(nx, pe, XE, A_)
                        if main:
                            hidden(i, 0)
                        if behind:
                            pe.wait_ge(e["hidden"], pv.g + 1)
                            if not pv.first(1):
                                pe.wait_ge(e["ht"], pv.g)
                            for c in range(GROUP):
                                last = nc.tensor.transpose(C_[:, c * P:(c + 1) * P],
                                                           HA[pv.par][:, c * P:(c + 1) * P], ident[:])
                            last.then_inc(e["ht_psum"], 1)
                        if main:
                            hidden(i, 1)
                        if behind:
                            pe.wait_ge(e["ht"], pv.g + 1)
                            if not pv.first(1):
                                pe.wait_ge(e["y"], pv.g)
                            pe.nop(nofuse=True)
                            for c in range(GROUP):
                                x_e = expert_of(pe, pv, c, E0)
                                y = Y_[:, c * P:(c + 1) * P]
                                nc.tensor.matmul(y, ones_b[0:3, :], b12[:, bass.ds(x_e, 1), 256:384], start=True,
                                                 stop=False, skip_group_check=True)
                                last = nc.tensor.matmul(y, AT[pv.par][:, c * P:(c + 1) * P],
                                                        W0b[:, bass.ds(x_e, 1), :], start=False, stop=True,
                                                        skip_group_check=True)
                            last.then_inc(e["y_psum"], 1)

                    pipeline(pe, groups, 0, body)

                @block.scalar
                def _(act):
                    def body(i, ahead, main, behind):
                        nx, pv = i.at(1), i.at(-1)
                        if ahead:
                            act.wait_ge(e["xt_psum"], nx.g + 1)
                            nc.scalar.activation(XT[nx.par], A_[nx.par][:, :], ACT.Copy).then_inc(e["xt"], 1)
                        if behind:
                            act.wait_ge(e["ht_psum"], pv.g + 1)
                            nc.scalar.activation(AT[pv.par], C_[:, :], ACT.Copy).then_inc(e["ht"], 1)
                        if main:
                            act.wait_ge(e["clipped"], i.g * 2 + 2)
                            nc.scalar.activation(AG[i.par], GL[i.par], ACT.Gelu_apprx_sigmoid).then_inc(e["gated"], 1)

                    pipeline(act, groups, 0, body)

                @block.vector
                def _(dve):
                    def body(i, ahead, main, behind):
                        pv = i.at(-1)
                        if main:
                            for half in range(2):
                                dve.wait_ge(e["h_psum"], i.g * 2 + half + 1)
                                h = H_[2 * i.par + half][:, :].rearrange("p (c u f) -> p c u f", c=2, u=2)
                                at = slice(half * 256, half * 256 + 256)
                                nc.vector.tensor_scalar(GL[i.par][:, at].rearrange("p (c f) -> p c f", c=2),
                                                        h[:, :, 0, :], LIMIT, None, ALU.min)
                                nc.vector.tensor_scalar(LN[i.par][:, at].rearrange("p (c f) -> p c f", c=2),
                                                        h[:, :, 1, :], LIMIT, -LIMIT, ALU.min, ALU.max
                                                        ).then_inc(e["clipped"], 1)
                            dve.wait_ge(e["gated"], i.g + 1)
                            dve.wait_ge(e["clipped"], i.g * 2 + 2)
                            nc.vector.scalar_tensor_tensor(HA[i.par], LN[i.par], 1.0, AG[i.par], ALU.add, ALU.mult
                                                           ).then_inc(e["hidden"], 1)
                        if behind:
                            dve.wait_ge(e["y_psum"], pv.g + 1)
                            if not pv.first(2):
                                dve.wait_ge(results_out[pv.par], pv.half * 16)
                            nc.vector.tensor_copy(YE[pv.par], Y_[:, :]).then_inc(e["y"], 1)

                    pipeline(dve, groups, 0, body)

        def experts1():
            groups = SLOT_TILES[1] // GROUP
            base = SLOT_TILES[0] // GROUP
            place[0] = 0
            XE, XT, YE = (carve2(GROUP * D) for _ in range(3))
            SI, HM = carve2(F1), carve2(F1)
            AT = carve2(3 * P)
            A_, H_, C_, Y_ = bank[0], bank[1:5], bank[5], bank[6:8]

            with nc.Block() as block:
                load_and_store(block, XE, YE, groups, base)

                def tiles_of(eng, body):
                    at = lambda k: Step(0, k, base)
                    for n in (0, 1):
                        for c in range(GROUP):
                            body(at(n), c, n > 0 or c > 0, n > 0 or c > 1, True)
                    with eng.Fori(1, groups // 2) as m:
                        for n in range(2):
                            for c in range(GROUP):
                                body(Step(m, n, base), c, True, True, True)
                    body(at(groups), 0, True, True, False)
                    body(at(groups), 1, False, True, False)

                def back(i, c, k):
                    return (i.at(-1), c - k + GROUP) if c < k else (i, c - k)

                @block.tensor
                def _(pe):
                    def body(i, c, lag1, lag2, main):
                        if main and c == 0:
                            pe.wait_ge(slots_in[i.par], (i.half + base // 2 + 1) * 16)
                            pe.wait_ge(e["xt"], i.g)
                            for k in range(GROUP):
                                last = nc.tensor.transpose(A_[:, k * P:(k + 1) * P], XE[i.par][:, k * P:(k + 1) * P],
                                                           ident[:])
                            last.then_inc(e["xt_psum"], 1)
                            hold(pe, e["xt"], i.g + 1)
                        if main:
                            r = c % 2
                            if not (isinstance(i.n, int) and i.n * GROUP + c < 2):
                                hold(pe, e1["hidden1"], i.n * GROUP + c - 1)
                            x_e = expert_of(pe, i, c, E1)
                            for u in range(2):
                                last = nc.tensor.matmul(H_[2 * r + u][:, 0:F1], XT[i.par][:, c * P:(c + 1) * P],
                                                        W1a[:, bass.ds(x_e, 1), u * F1:(u + 1) * F1],
                                                        start=True, stop=True)
                            last.then_inc(e1["h1_psum"], 1)
                        if lag2:
                            j, d = back(i, c, 2)
                            count = j.n * GROUP + d
                            pe.wait_ge(e1["ht1"], count + 1)
                            if d == 0 and not (isinstance(j.n, int) and j.n < 2):
                                pe.wait_ge(e["y"], j.g - 1)
                            pe.nop(nofuse=True)
                            x_e = expert_of(pe, j, d, E1)
                            for k, f in enumerate(F1_BLOCKS):
                                last = nc.tensor.matmul(Y_[j.par][:, d * P:(d + 1) * P],
                                                        AT[d % 2][0:f, k * P:(k + 1) * P],
                                                        W1b[0:f, bass.ds(x_e, 1), k * P:(k + 1) * P],
                                                        start=(k == 0), stop=(k == 2))
                            if d == GROUP - 1:
                                last.then_inc(e1["y1_psum"], 1)
                        if lag1:
                            j, d = back(i, c, 1)
                            count = j.n * GROUP + d
                            pe.wait_ge(e1["hidden1"], count + 1)
                            for k, f in enumerate(F1_BLOCKS):
                                last = nc.tensor.transpose(C_[0:f, k * P:(k + 1) * P],
                                                           HM[d % 2][:, k * P:k * P + f], ident[:])
                            last.then_inc(e1["ht1_psum"], 1)

                    tiles_of(pe, body)

                @block.scalar
                def _(act):
                    def body(i, c, lag1, lag2, main):
                        if main and c == 0:
                            act.wait_ge(e["xt_psum"], i.g + 1)
                            nc.scalar.activation(XT[i.par], A_[:, :], ACT.Copy).then_inc(e["xt"], 1)
                        if main:
                            act.wait_ge(e1["h1_psum"], i.n * GROUP + c + 1)
                            nc.scalar.activation(SI[c % 2], H_[2 * (c % 2)][:, 0:F1], ACT.Silu
                                                 ).then_inc(e1["silu1"], 1)
                        if lag1:
                            j, d = back(i, c, 1)
                            count = j.n * GROUP + d
                            act.wait_ge(e1["ht1_psum"], count + 1)
                            nc.scalar.activation(AT[d % 2][:, 0:2 * P], C_[:, 0:2 * P], ACT.Copy)
                            nc.scalar.activation(AT[d % 2][0:96, 2 * P:3 * P], C_[0:96, 2 * P:3 * P], ACT.Copy
                                                 ).then_inc(e1["ht1"], 1)

                    tiles_of(act, body)

                @block.vector
                def _(dve):
                    def body(i, c, lag1, lag2, main):
                        if main:
                            dve.wait_ge(e1["silu1"], i.n * GROUP + c + 1)
                            nc.vector.tensor_tensor(HM[c % 2], H_[2 * (c % 2) + 1][:, 0:F1], SI[c % 2], ALU.mult
                                                    ).then_inc(e1["hidden1"], 1)
                        if lag2:
                            j, d = back(i, c, 2)
                            if d == GROUP - 1:
                                dve.wait_ge(e1["y1_psum"], j.n + 1)
                                if not (isinstance(j.n, int) and j.n < 2):
                                    dve.wait_ge(results_out[j.par], (j.half + base // 2) * 16)
                                nc.vector.tensor_copy(YE[j.par], Y_[j.par][:, :]).then_inc(e["y"], 1)

                    tiles_of(dve, body)

        final_index = sem("final_index")
        final_in = [sem(f"final_in{q}") for q in range(2)]
        final_sum = sem("final_sum")
        stored = [sem(f"stored{q}") for q in range(2)]

        def finish():
            place[0] = 0
            gb = carve2(2 * K1 * D)
            gi = carve2(2 * K1, I32)
            res = carve2(2 * D)
            out_rows = out.rearrange("b s d -> (b s) d").rearrange("(i p) d -> p i d", p=P)
            with nc.Block() as block:
                @block.gpsimd
                def _(pool):
                    def gather(i, skip):
                        q = i.par
                        if not skip:
                            pool.wait_ge(final_sum, (i.n - 1) * 2)
                        nc.gpsimd.tensor_copy(gi[q].rearrange("p (i k) -> p i k", i=2),
                                              slot[:, bass.ds(i.n * 2, 2), 0:K1]).then_inc(final_index, 1)
                        hold(pool, final_index, i.n + 1)
                        for k in range(2 * K1):
                            nc.gpsimd.indirect_dma_start(
                                out=gb[q][:, k * D:(k + 1) * D], out_offset=None, in_=ys,
                                in_offset=bass.IndirectOffsetOnAxis(ap=gi[q][:, k:k + 1], axis=0),
                            ).then_inc(final_in[q], 16)

                    gather(Step(0, 0), True)
                    gather(Step(0, 1), True)
                    with pool.Fori(1, ITERS // 2) as m:
                        for c in range(2):
                            gather(Step(m, c), False)

                @block.vector
                def _(dve):
                    def add(i, skip):
                        q = i.par
                        dve.wait_ge(final_in[q], (i.half + 1) * 16 * 2 * K1)
                        if not skip:
                            dve.wait_ge(stored[q], i.half * 16)
                        for k in range(K1):
                            for j in range(2):
                                xt = X[:, bass.ds(i.n * 2 + j, 1), :].rearrange("p i d -> p (i d)")
                                at = (j * K1 + k) * D
                                src = xt if k == 0 else res[q][:, j * D:(j + 1) * D]
                                last = nc.vector.scalar_tensor_tensor(
                                    res[q][:, j * D:(j + 1) * D], gb[q][:, at:at + D],
                                    wts[:, bass.ds(i.n * 2 + j, 1), k], src, ALU.mult, ALU.add)
                            last.then_inc(final_sum, 1)
                            if k < K1 - 1:
                                dve.wait_ge(final_sum, i.n * K1 + k + 1)

                    add(Step(0, 0), True)
                    add(Step(0, 1), True)
                    with dve.Fori(1, ITERS // 2) as m:
                        for c in range(2):
                            add(Step(m, c), False)

                @block.sync
                def _(sp):
                    with sp.Fori(0, ITERS // 2) as m:
                        for c in range(2):
                            i = Step(m, c)
                            sp.wait_ge(final_sum, (i.n + 1) * K1)
                            sp.dma_start(out_rows[:, bass.ds(i.n * 2, 2), :],
                                         res[i.par].rearrange("p (i d) -> p i d", i=2)).then_inc(stored[i.par], 16)
                    for q in range(2):
                        sp.wait_ge(stored[q], 16 * ITERS // 2)

        attention(0)
        chained_before = chained[0]
        slots(0)
        dispatch(0)
        experts0()
        attention(1)
        chained_before = chained[0]
        slots(1)
        dispatch(1)
        experts1()
        finish()


def kernel(**inputs):
    import numpy as np
    import concourse.bacc as bacc
    from concourse.bass_utils import run_bass_kernel_spmd as run

    nc = bacc.Bacc("TRN2", target_bir_lowering=False, num_devices=1)
    i = {k: np.ascontiguousarray(v) for k, v in inputs.items()}
    arrays = {k: i[k] for k in ("x", "ctx_1024", "L0_xattn_bq", "L0_xattn_bk", "L0_xattn_bv", "L0_xattn_bo",
                                "L1_xattn_bq", "L1_xattn_bk", "L1_xattn_bv", "L1_xattn_bo",
                                "L0_ffn_norm_scale", "L0_ffn_gate_b", "L0_ffn_b2")}
    arrays["mask"] = i["mask_BxS2_bf0"]
    half = np.arange(D).reshape(HEADS, 2, HD // 2)[:, ::-1].reshape(-1)
    arrays["proj"] = np.ascontiguousarray(np.stack(
        [i["L0_xattn_" + n] for n in ("Wq", "Wk", "Wv", "Wo")] + [i["L1_xattn_" + n] for n in ("Wq", "Wk", "Wv", "Wo")]
        + [i["L1_xattn_Wq"][:, half], i["L1_xattn_Wk"][:, half]], axis=1))
    arrays["bqr"] = np.ascontiguousarray(i["L1_xattn_bq"][half])
    arrays["bkr"] = np.ascontiguousarray(i["L1_xattn_bk"][half])
    arrays["gate0"] = np.ascontiguousarray(i["L0_ffn_gate_w"].T)
    arrays["gate1"] = np.ascontiguousarray(i["L1_ffn_gate_w"].T)
    w1 = i["L0_ffn_w1"].reshape(E0, F0, 2, D).transpose(3, 0, 2, 1).reshape(D, E0, 2 * F0)
    arrays["w1_0"] = np.ascontiguousarray(w1)
    arrays["b1_0"] = np.ascontiguousarray(i["L0_ffn_b1"].reshape(E0, F0, 2).transpose(0, 2, 1).reshape(E0, 2 * F0))
    arrays["w2_0"] = np.ascontiguousarray(i["L0_ffn_w2"].transpose(2, 0, 1))
    arrays["w13_1"] = np.ascontiguousarray(
        np.concatenate([i["L1_ffn_w1"].transpose(2, 0, 1), i["L1_ffn_w3"].transpose(2, 0, 1)], axis=2))
    w2 = np.zeros((E1, D, 3 * P), np.float32)
    w2[:, :, :F1] = i["L1_ffn_w2"]
    arrays["w2_1"] = np.ascontiguousarray(w2.reshape(E1, D, 3, P).transpose(3, 0, 2, 1).reshape(P, E1, 3 * P))
    arrays["ident"] = np.eye(P, dtype=np.float32)
    arrays["before"] = np.triu(np.ones((P, P), np.float32), 1)
    arrays["head_of"] = (np.arange(P)[:, None] // HD % 4 == np.arange(4)[None, :]).astype(np.float32)
    arrays["seq_of"] = (np.arange(P)[None, :] // S == np.arange(2)[:, None]).astype(np.float32)
    freq = (1.0 / np.float32(10000.0) ** (np.arange(0, HD, 2, dtype=np.float32) / np.float32(HD))).astype(np.float32)
    angle = (np.arange(S, dtype=np.float32)[None, :] * freq[np.arange(P) % (HD // 2)][:, None]).astype(np.float32)
    sign = np.where(np.arange(P) % HD < HD // 2, -1.0, 1.0).astype(np.float32)[:, None]
    arrays["cos"] = np.cos(angle).astype(np.float32)
    arrays["sin"] = (np.sin(angle) * sign).astype(np.float32)
    args = {n: nc.dram_tensor("in_" + n, v.shape, mybir.dt.from_np(v.dtype), kind="ExternalInput").ap()
            for n, v in arrays.items()}
    out = nc.dram_tensor("out_x", (B, S, D), F32, kind="ExternalOutput").ap()
    xs = nc.dram_tensor("slot_rows", (SLOT_TILES[0] * P, D), F32, kind="Internal").ap()
    ys = nc.dram_tensor("slot_results", (SLOT_TILES[0] * P, D), F32, kind="Internal").ap()
    parts = nc.dram_tensor("bias_parts", (3, E0, 3 * F0), BF16, kind="Internal").ap()
    build(nc, args, out, xs, ys, parts)
    r = run(nc, [{"in_" + n: v for n, v in arrays.items()}], core_ids=[0])
    return r.results[0]["out_x"]
```

```python
from contextlib import ExitStack
from functools import partial

import concourse.bass as bass
from concourse import mybir

F32 = mybir.dt.float32
BF16 = mybir.dt.bfloat16
I32 = mybir.dt.int32
U32 = mybir.dt.uint32
U8 = mybir.dt.uint8
ALU = mybir.AluOpType
ACT = mybir.ActivationFunctionType
AX = mybir.AxisListType

P = 128
B, S, D = 128, 64, 128
HEADS = 16
HD = D // HEADS
TOKENS = B * S
TILES = TOKENS // P
ITERS = TILES // 2
UNITS = 4
SCALE = float(HD) ** -0.5
EPS = 1e-5
MASKED = -1e30

E0, K0, F0 = 32, 4, 128
E1, K1, F1 = 8, 2, 352
F1_BLOCKS = [128, 128, 96]
SLOT_TILES = [TOKENS * K0 // P + E0, TOKENS * K1 // P + E1]
GROUP = 4
LIMIT = 7.0
ARENA = 15904


class Step:

    def __init__(self, m, c, base=0):
        self.m, self.c, self.base = m, c, base
        self.n = m * 2 + c
        self.half = m + c // 2
        self.par = c % 2
        self.g = self.n + base

    def at(self, k):
        return Step(self.m, self.c + k, self.base)

    def first(self, k):
        return isinstance(self.g, int) and self.g < k


def hold(eng, sem, value):
    eng.wait_ge(sem, value)
    eng.nop(nofuse=True)


def build(nc, a, out, xs, ys, bias_parts):
    with ExitStack() as ctx:
        def sb(name, shape, dt=F32):
            return ctx.enter_context(nc.sbuf_tensor(name, shape, dt))

        def sem(name):
            return ctx.enter_context(nc.semaphore(name))

        bank = [ctx.enter_context(nc.psum_tensor(f"bank{i}", [P, 512], F32)) for i in range(8)]

        X = sb("X", [P, TILES, D])
        T = sb("T", [P, TILES, D])
        W = sb("W", [P, E0 * 3 * F0])
        top = sb("top", [P, TILES, 8])
        top_at = sb("top_at", [P, TILES, 8], U32)
        wts = sb("wts", [P, TILES, K0])
        slot = sb("slot", [P, TILES, K0], I32)
        group_experts = sb("group_experts", [1, SLOT_TILES[0] // GROUP], I32)
        ident = sb("ident", [P, P])
        head_of = sb("head_of", [P, 4])
        before = sb("before", [P, P], BF16)
        ones_b = sb("ones_b", [P, P], BF16)
        seq_of = sb("seq_of", [2, P], BF16)
        mask_rows = sb("mask_rows", [2, TILES, S], BF16)
        cos = sb("cos", [P, S])
        sin = sb("sin", [P, S])
        ones_f = sb("ones_f", [P, 1])
        power = sb("power", [P, 2])
        Wm = sb("Wm", [P, 10, D])
        bias_t = sb("bias_t", [P, 6])
        bias_r = sb("bias_r", [P, 5, D])
        gate_w = sb("gate_w", [P, E0 + E1])
        gate_b = sb("gate_b", [P, E0])
        Vbd = [sb(f"Vbd{q}", [P, 8, 4, 2, HD + 1]) for q in range(2)]
        zeros = sb("zeros", [P, 9 * D])

        arena = sb("arena", [P, ARENA])
        place = [0]

        def carve(width, dt=F32):
            lo = place[0]
            place[0] += width if dt in (F32, I32, U32) else (width + 1) // 2
            assert place[0] <= ARENA, place[0]
            v = arena[:, lo:place[0]]
            return v if dt == F32 else v.bitcast(dt)

        def carve2(width, dt=F32):
            return [carve(width, dt) for _ in range(2)]

        W0a = W[:, 0:E0 * 256].rearrange("p (e f) -> p e f", e=E0)
        W0b = W[:, E0 * 256:E0 * 384].rearrange("p (e f) -> p e f", e=E0)
        W1a = W[:, 0:E1 * 704].rearrange("p (e f) -> p e f", e=E1)
        W1b = W[:, E1 * 704:E1 * 1088].rearrange("p (e f) -> p e f", e=E1)
        expert_in = sem("expert_in")

        const_in = sem("const_in")
        setup_dve = sem("setup_dve")
        setup_pool = sem("setup_pool")
        N_CONST = 22
        wide_t = carve(P)
        mask_u8 = arena[0:2, 256:256 + TILES * S // 4].bitcast(U8)
        with nc.Block() as block:
            @block.sync
            def _(sp):
                row = lambda x: x.rearrange("(a n) -> a n", a=1).broadcast_to([P, D])
                col = lambda x: x.rearrange("(n a) -> n a", a=1)
                loads = [(ident[:], a["ident"]), (head_of[:], a["head_of"]), (wide_t, a["before"]),
                         (cos[:], a["cos"]), (sin[:], a["sin"]), (gate_w[:, 0:E0], a["gate0"]),
                         (gate_w[:, E0:E0 + E1], a["gate1"]),
                         (Wm[:].rearrange("p w d -> p (w d)").rearrange("p (w d) -> p w d", w=10), a["proj"]),
                         (gate_b[:], a["L0_ffn_gate_b"].rearrange("(a n) -> a n", a=1).broadcast_to([P, E0])),
                         (mask_u8.rearrange("b (i s) -> b i s", i=TILES),
                          a["mask"].rearrange("(i b) s -> b i s", b=2)),
                         (arena[0:2, 4096:4096 + P], a["seq_of"])]
                for n, name in enumerate(("L0_xattn_bq", "L0_xattn_bk", "L1_xattn_bq", "L1_xattn_bk", "bqr", "bkr")):
                    loads.append((bias_t[:, n:n + 1], col(a[name])))
                for n, name in enumerate(("L0_xattn_bv", "L0_xattn_bo", "L0_ffn_norm_scale", "L1_xattn_bv",
                                          "L1_xattn_bo")):
                    loads.append((bias_r[:, n, :], row(a[name])))
                assert len(loads) == N_CONST
                for dst, src in loads:
                    sp.dma_start(dst, src).then_inc(const_in, 16)
                sp.dma_start(W0a, a["w1_0"]).then_inc(expert_in, 16)
                sp.dma_start(W0b, a["w2_0"]).then_inc(expert_in, 16)

            @block.vector
            def _(dve):
                nc.vector.memset(zeros[:], 0.0)
                nc.vector.memset(ones_b[:], 1.0)
                nc.vector.memset(ones_f[:], 1.0)
                nc.vector.memset(power[:], -0.5)
                dve.wait_ge(const_in, 16 * N_CONST)
                nc.vector.tensor_copy(before[:], wide_t)
                nc.vector.tensor_copy(seq_of[:], arena[0:2, 4096:4096 + P])
                nc.vector.tensor_scalar(mask_rows[:].rearrange("b i s -> b (i s)"), mask_u8, MASKED, None,
                                        ALU.mult).then_inc(setup_dve, 1)
                dve.wait_ge(setup_dve, 1)

            @block.gpsimd
            def _(pool):
                for q in range(2):
                    nc.gpsimd.memset(Vbd[q][:], 0.0).then_inc(setup_pool, 1)
                pool.wait_ge(setup_pool, 2)
                for q in range(2):
                    nc.gpsimd.memset(Vbd[q][0:64, :, :, 0, HD:HD + 1], 1.0)
                    nc.gpsimd.memset(Vbd[q][64:128, :, :, 1, HD:HD + 1], 1.0).then_inc(setup_pool, 1)
                pool.wait_ge(setup_pool, 4)

        x_rows = a["x"].rearrange("b s d -> (b s) d").rearrange("(i p) d -> p i d", p=P)
        ctx_rows = a["ctx_1024"].rearrange("b s d -> (b s) d").rearrange("(i p) d -> p i d", p=P)
        xs_fill = xs.rearrange("(n p r) d -> n p (r d)", p=P, r=9)
        ys_rows = ys.rearrange("(g c p) d -> g p c d", c=GROUP, p=P)
        xs_rows = xs.rearrange("(g c p) d -> g p c d", c=GROUP, p=P)

        x_in = [sem(f"x_in{q}") for q in range(2)]
        ctx_in = [sem(f"ctx_in{q}") for q in range(2)]
        filled = sem("filled")
        gathered = [sem(f"gathered{q}") for q in range(2)]
        names = ("stats_a", "moments_a", "eps_a", "rstd_a", "normed", "cx_psum", "cx", "v_psum", "vbd", "qk_psum",
                 "qk", "rot_psum", "rot", "keys", "queries", "rope", "kbd", "score_psum", "score_max", "centred",
                 "t_psum",
                 "probs", "o_psum", "o_copied", "o_recip", "o_normed", "ot_psum", "ot", "wo_psum", "x_plus_bo",
                 "added", "stats_r", "moments_r", "pool_r", "rstd_r", "ms_r", "z", "t_ready", "t_kept", "tt_psum", "tt",
                 "gate_psum", "logits", "top8", "chosen", "top_kept", "index_copied", "combined", "q_zero", "z_added")
        s = {n: sem(n) for n in names}

        def attention(layer):
            place[0] = 0
            ctx_t = carve2(2 * D)
            xn = carve2(2 * D)
            CX = carve2(4 * D)
            Qz = carve2(UNITS * 2 * D)
            QKs = carve2(4 * D) if layer else None
            Kt = [v[:, 2 * D:4 * D] for v in QKs] if layer else carve2(2 * D)
            QKe, QKr = (carve(4 * D), carve(4 * D)) if layer else (None, None)
            Kbd = carve2(1024)
            mx = carve(32)
            Sc = carve2(512)
            Pt = carve2(512)
            AO = carve2(2 * HEADS * (HD + 1))
            rec = carve2(2 * HEADS)
            aon = carve2(2 * D)
            aoT = carve2(2 * D)
            xb = carve2(2 * D)
            z = None if layer else carve2(2 * D)
            t = carve2(2 * D)
            tT = carve2(2 * D)
            lg, tp, ta = carve2(2 * (E1 if layer else E0)), carve2(16), carve2(16, U32)
            small = {n: carve2(w) for n, w in (("st_a", 12), ("mv_a", 4), ("ve_a", 2), ("rs_a", 2), ("st_r", 12),
                                               ("mv_r", 4), ("ve_r", 2), ("rs_r", 2), ("ms", 2), ("ms1", 2),
                                               ("ms2", 2), ("r2", 2))}
            gb = carve2(2 * K0 * D) if layer else None
            gi = carve2(2 * K0, I32) if layer else None

            wq, wk, wv, wo = (Wm[:, 4 * layer + n, :] for n in range(4))
            bq, bk = bias_t[:, 2 * layer:2 * layer + 1], bias_t[:, 2 * layer + 1:2 * layer + 2]
            bv, bo = bias_r[:, 3 * layer, :], bias_r[:, 3 * layer + 1, :]
            n_e = E1 if layer else E0
            gw = gate_w[:, E0:E0 + E1] if layer else gate_w[:, 0:E0]
            S_, T_, O_, M_, P_ = bank[0:2], bank[2:4], bank[4:6], bank[6], bank[7]
            base = layer * ITERS

            def tiles(buf, i):
                return buf[:, bass.ds(i.n * 2, 2), :]

            def bodies(eng, body):
                at = lambda n: body(Step(0, n, base), lambda k: 0 <= n + k < ITERS)
                for n in range(-4, 4):
                    at(n)
                with eng.Fori(2, (ITERS - 4) // 2) as m:
                    for c in range(2):
                        body(Step(m, c, base), lambda k: True)
                for n in range(ITERS - 4, ITERS + 3):
                    at(n)

            with nc.Block() as block:
                @block.vector
                def _(dve):
                    for q in range(2):
                        nc.vector.memset(Qz[q], 0.0).then_inc(s["q_zero"], 1)
                    dve.wait_ge(s["q_zero"], 2 * layer + 2)

            with nc.Block() as block:
                @block.sync
                def _(sp):
                    def load(i):
                        q = i.par
                        if not i.first(2):
                            sp.wait_ge(s["cx_psum"], i.g - 1)
                        if not layer:
                            sp.dma_start(tiles(X, i), x_rows[:, bass.ds(i.n * 2, 2), :]).then_inc(x_in[q], 16)
                        sp.dma_start(ctx_t[q].rearrange("p (i d) -> p i d", i=2),
                                     ctx_rows[:, bass.ds(i.n * 2, 2), :]).then_inc(ctx_in[q], 16)

                    load(Step(0, 0, base))
                    load(Step(0, 1, base))
                    if not layer:
                        sp.dma_start(xs_fill[0], zeros[:]).then_inc(filled, 16)
                        sp.dma_start(xs_fill[1], zeros[:]).then_inc(filled, 16)
                    with sp.Fori(1, ITERS // 2) as m:
                        for c in range(2):
                            i = Step(m, c, base)
                            load(i)
                            if not layer:
                                sp.dma_start(xs_fill[bass.ds(i.n, 1)].rearrange("a p x -> (a p) x"),
                                             zeros[:]).then_inc(filled, 16)
                    if not layer:
                        sp.wait_ge(filled, 16 * ITERS)
                    if layer:
                        sp.dma_start(W1a, a["w13_1"]).then_inc(expert_in, 16)
                        sp.dma_start(W1b[:, :, :], a["w2_1"]).then_inc(expert_in, 16)

                @block.gpsimd
                def _(pool):
                    def gather(i, half):
                        q = i.par
                        if half == 0:
                            if not (isinstance(i.n, int) and i.n < 2):
                                pool.wait_ge(s["combined"], (i.n - 1) * K0)
                            nc.gpsimd.tensor_copy(gi[q].rearrange("p (i k) -> p i k", i=2),
                                                  tiles(slot, i)).then_inc(s["index_copied"], 1)
                            hold(pool, s["index_copied"], i.n + 1)
                        for k in range(half * K0, (half + 1) * K0):
                            nc.gpsimd.indirect_dma_start(
                                out=gb[q][:, k * D:(k + 1) * D], out_offset=None, in_=ys,
                                in_offset=bass.IndirectOffsetOnAxis(ap=gi[q][:, k:k + 1], axis=0),
                            ).then_inc(gathered[q], 16)

                    def scale_inputs(i):
                        ve, rs = small["ve_a"][i.par], small["rs_a"][i.par]
                        hold(pool, s["moments_a"], i.g + 1)
                        nc.gpsimd.tensor_scalar(ve, small["mv_a"][i.par].rearrange("p (i c) -> p i c", i=2)[:, :, 1],
                                                EPS, None, ALU.add).then_inc(s["eps_a"], 1)
                        pool.wait_ge(s["eps_a"], i.g + 1)
                        nc.gpsimd.tensor_tensor(rs, ve, power[:], ALU.pow).then_inc(s["rstd_a"], 1)

                    def spread_keys(i):
                        pool.wait_ge(s["rope" if layer else "keys"], i.n + 1)
                        nc.gpsimd.tensor_tensor(
                            Kbd[i.par].rearrange("p (b j k) -> p b j k", b=4, j=4),
                            Kt[i.par].rearrange("p (b k) -> p b k", b=4).unsqueeze(2).broadcast_to([P, 4, 4, S]),
                            head_of[:].unsqueeze(1).unsqueeze(3).broadcast_to([P, 4, 4, S]),
                            ALU.mult).then_inc(s["kbd"], 1)

                    def scale_outputs(i):
                        q = i.par
                        mv, ve, rs = small["mv_r"][q], small["ve_r"][q], small["rs_r"][q]
                        var = mv.rearrange("p (i c) -> p i c", i=2)[:, :, 1]
                        hold(pool, s["moments_r"], i.g + 1)
                        nc.gpsimd.tensor_scalar(ve, var, EPS, None, ALU.add).then_inc(s["pool_r"], 1)
                        pool.wait_ge(s["pool_r"], i.g + 1)
                        nc.gpsimd.tensor_tensor(rs, ve, power[:], ALU.pow).then_inc(s["rstd_r"], 1)
                        if not layer:
                            ms, ms1, ms2 = small["ms"][q], small["ms1"][q], small["ms2"][q]
                            pool.wait_ge(s["rstd_r"], i.g + 1)
                            nc.gpsimd.tensor_tensor(ms, rs, rs, ALU.mult).then_inc(s["ms_r"], 1)
                            pool.wait_ge(s["ms_r"], i.g * 4 + 1)
                            nc.gpsimd.tensor_tensor(ms1, ms, var, ALU.mult).then_inc(s["ms_r"], 1)
                            hold(pool, s["ms_r"], i.g * 4 + 2)
                            nc.gpsimd.tensor_scalar(ms2, ms1, EPS, None, ALU.add).then_inc(s["ms_r"], 1)
                            pool.wait_ge(s["ms_r"], i.g * 4 + 3)
                            nc.gpsimd.tensor_tensor(small["r2"][q], ms2, power[:], ALU.pow).then_inc(s["ms_r"], 1)

                    def body(i, on):
                        ex, nx, pv, pp, p3 = i.at(2), i.at(1), i.at(-1), i.at(-2), i.at(-3)
                        if on(-1):
                            if not pv.first(2):
                                hold(pool, s["added"], pv.g - 1)
                            nc.gpsimd.tensor_tensor(xb[pv.par].rearrange("p (i d) -> p i d", i=2), tiles(X, pv),
                                                    bo.unsqueeze(1).broadcast_to([P, 2, D]),
                                                    ALU.add).then_inc(s["x_plus_bo"], 1)
                        if layer and on(4):
                            gather(i.at(4), 0)
                        if not layer and on(2):
                            scale_inputs(ex)
                        if on(1):
                            spread_keys(nx)
                        if layer and on(2):
                            scale_inputs(ex)
                        if not layer and on(-2):
                            hold(pool, s["z"], pp.n + 1)
                            nc.gpsimd.tensor_tensor(tiles(X, pp), tiles(X, pp),
                                                    z[pp.par].rearrange("p (i d) -> p i d", i=2), ALU.add
                                                    ).then_inc(s["z_added"], 1)
                        if layer and on(4):
                            gather(i.at(4), 1)
                        if on(-3):
                            pool.wait_ge(s["chosen"], p3.g + 1)
                            nc.gpsimd.tensor_copy(tiles(top, p3), tp[p3.par].rearrange("p (i e) -> p i e", i=2))
                            nc.gpsimd.tensor_copy(tiles(top_at, p3), ta[p3.par].rearrange("p (i e) -> p i e", i=2)
                                                  ).then_inc(s["top_kept"], 1)
                        if on(-1):
                            scale_outputs(pv)

                    bodies(pool, body)

                @block.vector
                def _(dve):
                    def stats(i, st, mv, stats_sem, moments_sem):
                        q = i.par
                        for j in range(2):
                            nc.vector.bn_stats(st[q][:, 6 * j:6 * j + 6],
                                               X[:, bass.ds(i.n * 2 + j, 1), :].rearrange("p i d -> p (i d)")
                                               ).then_inc(s[stats_sem], 1)
                        hold(dve, s[stats_sem], i.g * 2 + 2)
                        for j in range(2):
                            last = nc.vector.bn_aggr(mv[q][:, 2 * j:2 * j + 2], st[q][:, 6 * j:6 * j + 6])
                        last.then_inc(s[moments_sem], 1)

                    def normalise(i, dst, mv, rs):
                        q = i.par
                        for j in range(2):
                            last = nc.vector.tensor_scalar(
                                dst[q][:, j * D:(j + 1) * D],
                                X[:, bass.ds(i.n * 2 + j, 1), :].rearrange("p i d -> p (i d)"),
                                mv[q][:, 2 * j:2 * j + 1], rs[q][:, j:j + 1], ALU.subtract, ALU.mult)
                        return last

                    def combine(i, k):
                        q = i.par
                        if k == 0:
                            dve.wait_ge(gathered[q], (i.half + 1) * 16 * 2 * K0)
                        else:
                            dve.wait_ge(s["combined"], i.n * K0 + k)
                        for j in range(2):
                            xt = X[:, bass.ds(i.n * 2 + j, 1), :].rearrange("p i d -> p (i d)")
                            at = (j * K0 + k) * D
                            last = nc.vector.scalar_tensor_tensor(
                                xt, gb[q][:, at:at + D], wts[:, bass.ds(i.n * 2 + j, 1), k], xt,
                                ALU.mult, ALU.add)
                        last.then_inc(s["combined"], 1)

                    def score_unit(i, r):
                        g4 = i.g * UNITS
                        dve.wait_ge(s["score_psum"], g4 + r + 1)
                        src = S_[r % 2][:, :].rearrange("p (h k) -> p h k", k=S)
                        m8 = mx[:, 8 * r:8 * r + 8]
                        nc.vector.tensor_reduce(m8, src, AX.X, ALU.max).then_inc(s["score_max"], 1)
                        dve.wait_ge(s["score_max"], g4 + r + 1)
                        nc.vector.tensor_tensor(Sc[r % 2].rearrange("p (h k) -> p h k", k=S), src,
                                                m8.unsqueeze(2).broadcast_to([P, 8, S]),
                                                ALU.subtract).then_inc(s["centred"], 1)

                    def read_logits(i):
                        dve.wait_ge(s["gate_psum"], i.g + 1)
                        src = P_[:, 0:2 * n_e].rearrange("p (i e) -> p i e", i=2)
                        q = i.par
                        dst = lg[q][:, 0:2 * n_e].rearrange("p (i e) -> p i e", i=2)
                        if layer:
                            nc.vector.tensor_copy(dst, src).then_inc(s["logits"], 1)
                        else:
                            nc.vector.tensor_tensor(dst, src, gate_b[:].unsqueeze(1).broadcast_to([P, 2, E0]),
                                                    ALU.add).then_inc(s["logits"], 1)

                    def choose(i):
                        q = i.par
                        if not i.first(2):
                            dve.wait_ge(s["top_kept"], i.g - 1)
                        hold(dve, s["logits"], i.g + 1)
                        for j in range(2):
                            nc.vector.max(tp[q][:, 8 * j:8 * j + 8], lg[q][:, j * n_e:(j + 1) * n_e]
                                          ).then_inc(s["top8"], 1)
                        hold(dve, s["top8"], i.g * 2 + 2)
                        for j in range(2):
                            last = nc.vector.max_index(ta[q][:, 8 * j:8 * j + 8], tp[q][:, 8 * j:8 * j + 8],
                                                       lg[q][:, j * n_e:(j + 1) * n_e])
                        last.then_inc(s["chosen"], 1)

                    def divide(i):
                        q = i.par
                        dve.wait_ge(s["o_copied"], i.g + 1)
                        ao = AO[q].rearrange("p (h c) -> p h c", c=HD + 1)
                        nc.vector.reciprocal(rec[q].unsqueeze(2), ao[:, :, HD:HD + 1]).then_inc(s["o_recip"], 1)
                        dve.wait_ge(s["o_recip"], i.g + 1)
                        nc.vector.tensor_tensor(aon[q].rearrange("p (h c) -> p h c", c=HD), ao[:, :, 0:HD],
                                                rec[q].unsqueeze(2).broadcast_to([P, 2 * HEADS, HD]),
                                                ALU.mult).then_inc(s["o_normed"], 1)

                    def place_values(i):
                        q = i.par
                        dve.wait_ge(s["v_psum"], i.g + 1)
                        for u in range(2):
                            rows = slice(64 * u, 64 * u + 64)
                            src = M_[rows, :].rearrange("p (b h u d) -> p h b u d", b=4, u=2, d=HD)[:, :, :, u, :]
                            bvv = bv[rows, :].rearrange("p (h u d) -> p h u d", u=2, d=HD)[:, :, u, :]
                            last = nc.vector.tensor_tensor(
                                Vbd[q][rows, :, :, u, 0:HD], src,
                                bvv.unsqueeze(2).broadcast_to([64, 8, 4, HD]), ALU.add)
                        last.then_inc(s["vbd"], 1)

                    def weigh(i, buf, b0, b1, tab, done):
                        for h, b in ((0, b0), (1, b1)):
                            at = slice(h * 2 * D, (h + 1) * 2 * D)
                            last = nc.vector.scalar_tensor_tensor(
                                buf[:, at].rearrange("p (b s) -> p b s", s=S),
                                P_[:, at].rearrange("p (b s) -> p b s", s=S), b,
                                tab[:].unsqueeze(1).broadcast_to([P, 4, S]), ALU.add, ALU.mult)
                        last.then_inc(s[done], 1)

                    def rotate(i):
                        dve.wait_ge(s["rot_psum"], i.n + 1)
                        weigh(i, QKr, bias_t[:, 4:5], bias_t[:, 5:6], sin, "rot")
                        dve.wait_ge(s["rot"], i.n + 1)
                        nc.vector.tensor_tensor(QKs[i.par], QKe, QKr, ALU.add).then_inc(s["rope"], 1)

                    def expert_rows(i):
                        q = i.par
                        dve.wait_ge(s["rstd_r"], i.g + 1)
                        if not i.first(2):
                            dve.wait_ge(s["t_kept"], i.g - 1)
                            if not layer:
                                dve.wait_ge(s["z_added"], i.n - 1)
                            dve.wait_ge(s["tt_psum"], i.g - 1)
                        if layer:
                            normalise(i, t, small["mv_r"], small["rs_r"]).then_inc(s["t_ready"], 1)
                        else:
                            normalise(i, z, small["mv_r"], small["rs_r"]).then_inc(s["z"], 1)
                            dve.wait_ge(s["z"], i.g + 1)
                            dve.wait_ge(s["ms_r"], i.g * 4 + 4)
                            for j in range(2):
                                last = nc.vector.scalar_tensor_tensor(
                                    t[q][:, j * D:(j + 1) * D], z[q][:, j * D:(j + 1) * D],
                                    small["r2"][q][:, j:j + 1], bias_r[:, 2, :], ALU.mult, ALU.mult)
                            last.then_inc(s["t_ready"], 1)

                    def body(i, on):
                        ex, nx, pv, pp = i.at(2), i.at(1), i.at(-1), i.at(-2)
                        if on(0):
                            score_unit(i, 0)
                        if on(-3):
                            read_logits(i.at(-3))
                        if on(0):
                            score_unit(i, 1)
                        if layer and on(1):
                            dve.wait_ge(s["qk_psum"], nx.g + 1)
                            if not (isinstance(nx.n, int) and nx.n < 1):
                                dve.wait_ge(s["rope"], nx.n)
                            weigh(nx, QKe, bq, bk, cos, "qk")
                        if layer and on(1):
                            place_values(nx)
                        if layer and on(3):
                            combine(i.at(3), 0)
                        if layer and on(1):
                            rotate(nx)
                        if layer and on(0):
                            score_unit(i, 2)
                        if on(-1):
                            divide(pv)
                        if layer and on(3):
                            combine(i.at(3), 1)
                        if on(-3):
                            choose(i.at(-3))
                        if on(2):
                            if layer:
                                hold(dve, s["combined"], (ex.n + 1) * K0)
                            else:
                                hold(dve, x_in[ex.par], (ex.half + 1) * 16)
                            stats(ex, small["st_a"], small["mv_a"], "stats_a", "moments_a")
                        if layer and on(3):
                            combine(i.at(3), 2)
                        if not layer and on(1):
                            place_values(nx)
                        if not layer and on(0):
                            score_unit(i, 2)
                        if on(0):
                            score_unit(i, 3)
                        if layer and on(3):
                            combine(i.at(3), 3)
                        if on(-2):
                            expert_rows(pp)
                        if on(2):
                            dve.wait_ge(s["rstd_a"], ex.g + 1)
                            normalise(ex, xn, small["mv_a"], small["rs_a"]).then_inc(s["normed"], 1)
                        if on(-1):
                            dve.wait_ge(s["wo_psum"], pv.g + 1)
                            dve.wait_ge(s["x_plus_bo"], pv.g + 1)
                            nc.vector.tensor_tensor(tiles(X, pv), P_[:, 0:2 * D].rearrange("p (i d) -> p i d", i=2),
                                                    xb[pv.par].rearrange("p (i d) -> p i d", i=2),
                                                    ALU.add).then_inc(s["added"], 1)
                            hold(dve, s["added"], pv.g + 1)
                            stats(pv, small["st_r"], small["mv_r"], "stats_r", "moments_r")
                    bodies(dve, body)

                @block.scalar
                def _(act):
                    def exps(i, r):
                        act.wait_ge(s["t_psum"], i.g * UNITS + r + 1)
                        nc.scalar.activation(Pt[r % 2], T_[r % 2][:, :], ACT.Exp, scale=SCALE
                                             ).then_inc(s["probs"], 1)

                    def projections(i):
                        if layer:
                            act.wait_ge(s["rope"], i.n + 1)
                        else:
                            act.wait_ge(s["qk_psum"], i.n + 1)
                            nc.scalar.activation(Kt[i.par], P_[:, 2 * D:4 * D], ACT.Identity, bias=bk
                                                 ).then_inc(s["keys"], 1)
                        for r in range(UNITS):
                            rows = slice(32 * r, 32 * r + 32)
                            at = Qz[i.par][rows, r * 2 * D:(r + 1) * 2 * D]
                            if layer:
                                last = nc.scalar.activation(at, QKs[i.par][rows, 0:2 * D], ACT.Copy)
                            else:
                                last = nc.scalar.activation(at, P_[rows, 0:2 * D], ACT.Identity, bias=bq[rows, :])
                        last.then_inc(s["queries"], 1)

                    def copy_outputs(i):
                        act.wait_ge(s["o_psum"], i.g + 1)
                        for w in range(2):
                            for b in range(2):
                                rows = slice(64 * b, 64 * b + 64)
                                c = 2 * (HD + 1)
                                src = O_[w][rows, 0:16 * c].rearrange("p (h b c) -> p h b c", h=8, b=2)[:, :, b, :]
                                dst = AO[i.par][rows, w * 8 * c:(w + 1) * 8 * c].rearrange("p (h c) -> p h c", h=8)
                                last = nc.scalar.activation(dst, src, ACT.Copy)
                        last.then_inc(s["o_copied"], 1)

                    def body(i, on):
                        ex, nx, pv, pp = i.at(2), i.at(1), i.at(-1), i.at(-2)
                        if on(0):
                            exps(i, 0)
                        if on(1) and not layer:
                            projections(nx)
                        if on(0):
                            exps(i, 1)
                        if on(1) and layer:
                            projections(nx)
                        if on(-1):
                            act.wait_ge(s["ot_psum"], pv.g + 1)
                            nc.scalar.activation(aoT[pv.par], P_[:, 0:2 * D], ACT.Copy).then_inc(s["ot"], 1)
                        if on(0):
                            exps(i, 2)
                            exps(i, 3)
                        if on(-2):
                            act.wait_ge(s["t_ready"], pp.g + 1)
                            nc.scalar.activation(tiles(T, pp), t[pp.par].rearrange("p (i d) -> p i d", i=2), ACT.Copy
                                                 ).then_inc(s["t_kept"], 1)
                            act.wait_ge(s["tt_psum"], pp.g + 1)
                            nc.scalar.activation(tT[pp.par], M_[:, 0:2 * D], ACT.Copy).then_inc(s["tt"], 1)
                        if on(2):
                            act.wait_ge(s["cx_psum"], ex.g + 1)
                            nc.scalar.activation(CX[ex.par], M_[:, :], ACT.Copy).then_inc(s["cx"], 1)
                        if on(0):
                            copy_outputs(i)

                    bodies(act, body)

                @block.tensor
                def _(pe):
                    def scores(i, r):
                        g4 = i.g * UNITS
                        if not (isinstance(g4, int) and g4 + r < 2):
                            (pe.wait_ge if layer else partial(hold, pe))(s["centred"], g4 + r - 1)
                        sbk = S_[r % 2]
                        if not layer:
                            nc.tensor.matmul(sbk[:, :].rearrange("p (w j k) -> p w j k", w=2, j=4), seq_of[:],
                                             mask_rows[:, bass.ds(i.n * 2, 2), :].unsqueeze(2)
                                             .broadcast_to([2, 2, 4, S]), start=True, stop=False,
                                             skip_group_check=True)
                        for w in range(2):
                            for b in range(2):
                                sq = 2 * w + b
                                last = nc.tensor.matmul(
                                    sbk[64 * b:64 * b + 64, 256 * w:256 * w + 256],
                                    Qz[i.par][:, 256 * r + 64 * sq:256 * r + 64 * sq + 64],
                                    Kbd[i.par][:, 256 * sq:256 * sq + 256],
                                    start=bool(layer), stop=True, skip_group_check=True)
                        last.then_inc(s["score_psum"], 1)

                    def turn(i, r):
                        pe.wait_ge(s["centred"], i.g * UNITS + r + 1)
                        for k in range(4):
                            last = nc.tensor.transpose(T_[r % 2][:, k * P:(k + 1) * P],
                                                       Sc[r % 2][:, k * P:(k + 1) * P], ident[:])
                        last.then_inc(s["t_psum"], 1)

                    def values(i, r):
                        if r == 0:
                            pe.wait_ge(s["vbd"], i.g + 1)
                            if not i.first(1):
                                pe.wait_ge(s["o_copied"], i.g)
                        pe.wait_ge(s["probs"], i.g * UNITS + r + 1)
                        c = 4 * (HD + 1)
                        for w in range(2):
                            for jj in range(2):
                                hp = 2 * r + jj
                                k = 2 * w + jj
                                last = nc.tensor.matmul(
                                    O_[w][:, c * hp:c * hp + c], Pt[r % 2][:, k * P:(k + 1) * P],
                                    Vbd[i.par][:, hp, 2 * w:2 * w + 2, :, :], start=True, stop=True)
                        if r == UNITS - 1:
                            last.then_inc(s["o_psum"], 1)

                    def inputs(i):
                        q = i.par
                        pe.wait_ge(ctx_in[q], (i.half + i.base // 2 + 1) * 16)
                        pe.wait_ge(s["normed"], i.g + 1)
                        if not i.first(1):
                            pe.wait_ge(s["vbd"], i.g)
                        if not i.first(4):
                            pe.wait_ge(s["tt"], i.g - 3)
                        for w in range(2):
                            nc.tensor.transpose(M_[:, w * P:(w + 1) * P], ctx_t[q][:, w * P:(w + 1) * P], ident[:])
                        for w in range(2):
                            last = nc.tensor.transpose(M_[:, (2 + w) * P:(3 + w) * P],
                                                       xn[q][:, w * P:(w + 1) * P], ident[:])
                        last.then_inc(s["cx_psum"], 1)

                    def projections(i, wq, wk, done):
                        nc.tensor.matmul(P_[:, 0:2 * D], wq, CX[i.par][:, 2 * D:4 * D], start=True, stop=True)
                        nc.tensor.matmul(P_[:, 2 * D:4 * D], wk, CX[i.par][:, 0:2 * D], start=True, stop=True
                                         ).then_inc(done, 1)

                    def body(i, on):
                        ex, nx, pv, pp = i.at(2), i.at(1), i.at(-1), i.at(-2)
                        if on(0):
                            turn(i, 0)
                        if on(1):
                            if not nx.first(3):
                                pe.wait_ge(s["added"], nx.g - 2)
                            if not nx.first(4):
                                pe.wait_ge(s["logits"], nx.g - 3)
                            pe.wait_ge(s["cx"], nx.g + 1)
                            projections(nx, wq, wk, s["qk_psum"])
                            for b in range(4):
                                for u in range(2):
                                    last = nc.tensor.matmul(M_[64 * u:64 * u + 64, b * P:(b + 1) * P],
                                                            CX[nx.par][:, b * S:(b + 1) * S], wv, start=True,
                                                            stop=True)
                            last.then_inc(s["v_psum"], 1)
                        if on(0):
                            scores(i, 2)
                        if layer and on(1):
                            pe.wait_ge(s["qk"], nx.n + 1)
                            projections(nx, Wm[:, 8, :], Wm[:, 9, :], s["rot_psum"])
                        if on(0):
                            values(i, 0)
                            turn(i, 1)
                        if on(0):
                            scores(i, 3)
                            values(i, 1)
                        if on(-1):
                            pe.wait_ge(s["o_normed"], pv.g + 1)
                            if on(1):
                                pe.wait_ge(s["rot" if layer else "queries"], nx.n + 1)
                            else:
                                pe.wait_ge(s["logits"], pv.g - 1)
                            for w in range(2):
                                last = nc.tensor.transpose(P_[:, w * P:(w + 1) * P],
                                                           aon[pv.par][:, w * P:(w + 1) * P], ident[:])
                            last.then_inc(s["ot_psum"], 1)
                        if on(0):
                            turn(i, 2)
                        if on(-1):
                            pe.wait_ge(s["ot"], pv.g + 1)
                            for w in range(2):
                                last = nc.tensor.matmul(P_[:, w * P:(w + 1) * P],
                                                        aoT[pv.par][:, w * P:(w + 1) * P], wo, start=True, stop=True)
                            last.then_inc(s["wo_psum"], 1)
                        if on(1):
                            pe.wait_ge(s["kbd"], nx.g + 1)
                            pe.wait_ge(s["queries"], nx.g + 1)
                            scores(nx, 0)
                        if on(0):
                            turn(i, 3)
                            values(i, 2)
                        if on(1):
                            scores(nx, 1)
                        if on(-2):
                            pe.wait_ge(s["t_ready"], pp.g + 1)
                            if on(1):
                                pe.wait_ge(s["vbd"], nx.g + 1)
                            for w in range(2):
                                last = nc.tensor.transpose(M_[:, w * P:(w + 1) * P],
                                                           t[pp.par][:, w * P:(w + 1) * P], ident[:])
                            last.then_inc(s["tt_psum"], 1)
                        if on(0):
                            values(i, 3)
                        if on(2):
                            inputs(ex)
                        if on(-2):
                            pe.wait_ge(s["tt"], pp.g + 1)
                            if on(-1):
                                pe.wait_ge(s["added"], pv.g + 1)
                            else:
                                pe.wait_ge(s["logits"], pp.g)
                            for w in range(2):
                                last = nc.tensor.matmul(P_[:, w * n_e:(w + 1) * n_e],
                                                        tT[pp.par][:, w * P:(w + 1) * P], gw, start=True, stop=True)
                            last.then_inc(s["gate_psum"], 1)

                    bodies(pe, body)

        combine_step = sem("combine_step")

        chain = sem("chain")
        chained = [0]
        hot = sem("hot")
        ranks = sem("ranks")
        expo = sem("expo")
        at_least = sem("at_least")
        owner = sem("owner")
        slot_iota = sem("slot_iota")
        index_in = sem("index_in")
        moved = [sem(f"moved{q}") for q in range(2)]
        scattered = [sem(f"scattered{q}") for q in range(2)]
        b_in, b_moved = sem("b_in"), sem("b_moved")

        def slots(layer):
            E, K = (E1, K1) if layer else (E0, K0)
            NT = SLOT_TILES[layer]
            TE = TILES * E
            chunks = TE // 512
            place[0] = 0
            oh = [carve(TE, BF16) for _ in range(K)]
            CT, INC, POS = (carve(TE) for _ in range(3))
            TMP = CT
            iota_e = carve(E)
            at_f = carve(TILES * K)
            expw = carve(TILES * K)
            wsum = carve(TILES)
            wrec = carve(TILES)
            count = carve(E)
            count_i = carve(E, I32)
            padded = carve(E)
            pad_end = carve(E)
            shift = carve(E)
            diag = carve(E)
            my_end = carve(1)
            slot_f = carve(TILES * K)
            start_of_tile = carve(NT)
            ge = carve(NT, BF16)
            e_f = carve(NT)
            word_f = carve(NT // GROUP)
            ie = lambda v: v.rearrange("p (i e) -> p i e", e=E)
            ei = lambda v: v.rearrange("p (e i) -> p e i", e=E)
            ik = lambda v: v.rearrange("p (i k) -> p i k", k=K)

            with nc.Block() as block:
                @block.gpsimd
                def _(pool):
                    nc.gpsimd.iota(iota_e, pattern=[[1, E]], base=0, channel_multiplier=0,
                                   allow_small_or_imprecise_dtypes=True).then_inc(slot_iota, 1)
                    nc.gpsimd.iota(start_of_tile, pattern=[[P, NT]], base=0, channel_multiplier=0,
                                   allow_small_or_imprecise_dtypes=True).then_inc(slot_iota, 1)

                @block.vector
                def _(dve):
                    def link(ins):
                        chained[0] += 1
                        ins.then_inc(chain, 1)
                        dve.wait_ge(chain, chained[0])

                    nc.vector.tensor_copy(ik(at_f), top_at[:, :, 0:K])
                    link(nc.vector.tensor_tensor(ik(expw), top[:, :, 0:K],
                                                 top[:, :, 0:1].broadcast_to([P, TILES, K]), ALU.subtract))
                    dve.wait_ge(slot_iota, 2 * layer + 2)
                    for k in range(K):
                        nc.vector.tensor_tensor(ie(oh[k]), iota_e.unsqueeze(1).broadcast_to([P, TILES, E]),
                                                ik(at_f)[:, :, k:k + 1].broadcast_to([P, TILES, E]),
                                                ALU.is_equal).then_inc(hot, 1)
                    dve.wait_ge(expo, layer + 1)
                    link(nc.vector.tensor_reduce(wsum, ik(expw), AX.X, ALU.add))
                    link(nc.vector.reciprocal(wrec, wsum))
                    link(nc.vector.tensor_tensor(wts[:, :, 0:K], ik(expw),
                                                 wrec.unsqueeze(2).broadcast_to([P, TILES, K]), ALU.mult))
                    dve.wait_ge(ranks, layer + 1)
                    w = 512 // E
                    for c in range(chunks):
                        last = nc.vector.tensor_copy(ei(CT)[:, :, c * w:(c + 1) * w],
                                                     bank[4 + c][:, :].rearrange("p (i e) -> p e i", e=E))
                    link(last)
                    link(nc.vector.tensor_tensor_scan(INC, ones_f[:].broadcast_to([P, TE]), CT, 0.0,
                                                      ALU.mult, ALU.add))
                    ends = ei(INC)[:, :, TILES - 1]
                    nc.vector.tensor_copy(count[:, 0:1], ends[:, 0:1])
                    link(nc.vector.tensor_tensor(count[:, 1:E], ends[:, 1:E], ends[:, 0:E - 1], ALU.subtract))
                    link(nc.vector.tensor_scalar(count_i, count, float(P - 1), None, ALU.add))
                    link(nc.vector.tensor_scalar(count_i, count_i, -P, None, ALU.bitwise_and))
                    link(nc.vector.tensor_copy(padded, count_i))
                    link(nc.vector.tensor_tensor_scan(pad_end, ones_f[:].broadcast_to([P, E]), padded, 0.0,
                                                      ALU.mult, ALU.add))
                    link(nc.vector.tensor_tensor(shift, pad_end, padded, ALU.subtract))
                    link(nc.vector.tensor_tensor(shift, shift, ends, ALU.subtract))
                    link(nc.vector.tensor_tensor(shift, shift, count, ALU.add))
                    link(nc.vector.tensor_tensor(diag[0:E, :], pad_end[0:E, :], ident[0:E, 0:E], ALU.mult))
                    link(nc.vector.tensor_reduce(my_end[0:E, :], diag[0:E, :], AX.X, ALU.add))
                    nc.vector.tensor_scalar(ge[0:E, :], start_of_tile[0:E, :], my_end[0:E, :], None,
                                            ALU.is_ge).then_inc(at_least, 1)
                    link(nc.vector.tensor_tensor(INC, INC, CT, ALU.subtract))
                    link(nc.vector.tensor_tensor(ei(INC), ei(INC), shift.unsqueeze(2).broadcast_to([P, E, TILES]),
                                                 ALU.add))
                    for c in range(chunks):
                        last = nc.vector.tensor_tensor(ie(POS)[:, c * w:(c + 1) * w, :],
                                                       bank[c][:, :].rearrange("p (i e) -> p i e", e=E),
                                                       INC.rearrange("p (e i) -> p i e", e=E)[:, c * w:(c + 1) * w, :],
                                                       ALU.add)
                    link(last)
                    for k in range(K):
                        link(nc.vector.tensor_tensor(TMP, oh[k], POS, ALU.mult))
                        link(nc.vector.tensor_reduce(ik(slot_f)[:, :, k], ie(TMP), AX.X, ALU.add))
                    link(nc.vector.tensor_copy(slot[:, :, 0:K], ik(slot_f)))
                    dve.wait_ge(owner, layer + 1)
                    link(nc.vector.tensor_scalar(e_f[0:1, :], bank[7][0:1, 0:NT] if not layer else bank[1][0:1, 0:NT],
                                                 float(E - 1), None, ALU.min))
                    digit = e_f[0:1, :].rearrange("a (g c) -> a g c", c=GROUP)
                    word = word_f[0:1, :].unsqueeze(2)
                    link(nc.vector.tensor_copy(word, digit[:, :, GROUP - 1:GROUP]))
                    for c in reversed(range(GROUP - 1)):
                        link(nc.vector.scalar_tensor_tensor(word, word, float(E0), digit[:, :, c:c + 1], ALU.mult,
                                                            ALU.add))
                    link(nc.vector.tensor_copy(group_experts[0:1, 0:NT // GROUP], word_f[0:1, :]))

                @block.scalar
                def _(act):
                    act.wait_ge(chain, chained_before + 1)
                    nc.scalar.activation(expw, expw, ACT.Exp).then_inc(expo, 1)

                @block.tensor
                def _(pe):
                    for k in range(K):
                        pe.wait_ge(hot, layer * K0 + k + 1)
                        for c in range(chunks):
                            nc.tensor.matmul(bank[c][:, :], before[:], oh[k][:, 512 * c:512 * c + 512],
                                             start=(k == 0), stop=(k == K - 1))
                            last = nc.tensor.matmul(bank[4 + c][:, :], ones_b[:], oh[k][:, 512 * c:512 * c + 512],
                                                    start=(k == 0), stop=(k == K - 1))
                    last.then_inc(ranks, 1)
                    pe.wait_ge(at_least, layer + 1)
                    dst = bank[7] if not layer else bank[1]
                    nc.tensor.matmul(dst[0:1, 0:NT], ones_b[0:E, 0:1], ge[0:E, :], start=True, stop=True
                                     ).then_inc(owner, 1)

        def dispatch(layer):
            K = K1 if layer else K0
            place[0] = 0
            rows = carve2(GROUP * D)
            idx = carve2(GROUP * K, I32)
            count = TILES // GROUP
            base = layer * (TILES // GROUP)
            with nc.Block() as block:
                @block.scalar
                def _(act):
                    def move(i, skip):
                        q = i.par
                        if not skip:
                            act.wait_ge(scattered[q], i.half * 16 * GROUP * K + done[layer])
                        nc.scalar.activation(rows[q].rearrange("p (i d) -> p i d", i=GROUP),
                                             T[:, bass.ds(i.n * GROUP, GROUP), :], ACT.Copy).then_inc(moved[q], 1)

                    move(Step(0, 0), True)
                    move(Step(0, 1), True)
                    with act.Fori(1, count // 2) as m:
                        for c in range(2):
                            move(Step(m, c), False)

                @block.gpsimd
                def _(pool):
                    with pool.Fori(0, count // 2) as m:
                        for c in range(2):
                            i = Step(m, c, base)
                            q = i.par
                            nc.gpsimd.tensor_copy(idx[q].rearrange("p (i k) -> p i k", i=GROUP),
                                                  slot[:, bass.ds(i.n * GROUP, GROUP), 0:K]).then_inc(index_in, 1)
                            pool.wait_ge(index_in, i.g + 1)
                            hold(pool, moved[q], i.half + base // 2 + 1)
                            for t in range(GROUP):
                                for k in range(K):
                                    nc.gpsimd.indirect_dma_start(
                                        out=xs, out_offset=bass.IndirectOffsetOnAxis(
                                            ap=idx[q][:, t * K + k:t * K + k + 1], axis=0),
                                        in_=rows[q][:, t * D:(t + 1) * D], in_offset=None,
                                    ).then_inc(scattered[q], 16)
                            pool.wait_ge(scattered[q], (i.half + 1) * 16 * GROUP * K + done[layer])

        done = [0, 16 * TILES * K0 // 2]

        slots_in = [sem(f"slots_in{q}") for q in range(2)]
        results_out = [sem(f"results_out{q}") for q in range(2)]
        e = {n: sem(n) for n in ("xt_psum", "xt", "h_psum", "clipped", "gated", "hidden", "ht_psum", "ht", "y_psum",
                                 "y")}
        e1 = {n: sem(n) for n in ("h1_psum", "silu1", "hidden1", "ht1_psum", "ht1", "y1_psum")}

        def load_and_store(block, XE, YE, groups, base):
            @block.sync
            def _(sp):
                def load(i):
                    if not i.first(2):
                        sp.wait_ge(e["xt_psum"], i.g - 1)
                    sp.dma_start(XE[i.par].rearrange("p (c d) -> p c d", c=GROUP),
                                 xs_rows[bass.ds(i.n, 1)].rearrange("a p c d -> p (a c) d")
                                 ).then_inc(slots_in[i.par], 16)

                load(Step(0, 0, base))
                load(Step(0, 1, base))
                with sp.Fori(1, groups // 2) as m:
                    for c in range(2):
                        load(Step(m, c, base))

            @block.gpsimd
            def _(pool):
                def store(i):
                    hold(pool, e["y"], i.g + 1)
                    pool.dma_start(ys_rows[bass.ds(i.n, 1)].rearrange("a p c d -> p (a c) d"),
                                 YE[i.par].rearrange("p (c d) -> p c d", c=GROUP)
                                 ).then_inc(results_out[i.par], 16)

                with pool.Fori(0, groups // 2) as m:
                    for c in range(2):
                        store(Step(m, c, base))
                for q in range(2):
                    pool.wait_ge(results_out[q], 16 * (groups + base) // 2)

        def pipeline(eng, groups, base, body):
            at = lambda k: Step(0, k, base)
            body(at(-1), True, False, False)
            body(at(0), True, True, False)
            for n in (1, 2, 3):
                body(at(n), True, True, True)
            with eng.Fori(2, groups // 2 - 1) as m:
                for c in range(2):
                    body(Step(m, c, base), True, True, True)
            body(at(groups - 2), True, True, True)
            body(at(groups - 1), False, True, True)
            body(at(groups), False, False, True)

        def transposed_rows(i, pe, XE, A_):
            pe.wait_ge(slots_in[i.par], (i.half + i.base // 2 + 1) * 16)
            if not i.first(2):
                pe.wait_ge(e["xt"], i.g - 1)
            for c in range(GROUP):
                last = nc.tensor.transpose(A_[i.par][:, c * P:(c + 1) * P], XE[i.par][:, c * P:(c + 1) * P], ident[:])
            last.then_inc(e["xt_psum"], 1)

        def experts_of(i, experts):
            word = nc.tensor.value_load(group_experts[0:1, bass.ds(i.n, 1)], min_val=0, max_val=E0 ** GROUP - 1)
            return [nc.s_assert_within(word // E0 ** c % E0, 0, experts - 1,
                                       skip_runtime_bounds_check_because="each is clamped to the experts when packed")
                    for c in range(GROUP)]

        def experts0():
            groups = SLOT_TILES[0] // GROUP
            place[0] = 0
            XE, XT, GL, LN, HA, AT, YE = (carve2(GROUP * D) for _ in range(7))
            AG = GL
            b12 = carve(E0 * 384, BF16)[0:3, :].rearrange("r (e f) -> r e f", e=E0)
            A_, H_, C_, Y_ = bank[0:2], bank[2:6], bank[6], bank[7]
            part_f, rest = HA[0][0:E0, 0:384], AT[0][0:E0, 0:384]
            parts = [XE[0], XE[1], XT[0]]
            parts = [p.bitcast(BF16)[0:E0, 0:384] for p in parts]
            with nc.Block() as block:
                @block.sync
                def _(sp):
                    sp.dma_start(part_f[:, 0:256], a["b1_0"]).then_inc(b_in, 16)
                    sp.dma_start(part_f[:, 256:384], a["L0_ffn_b2"]).then_inc(b_in, 16)
                    for n in range(3):
                        sp.wait_ge(b_moved, 1 + 2 * n if n < 2 else 4)
                        sp.dma_start(bias_parts[n], parts[n]).then_inc(b_in, 16)
                    sp.wait_ge(b_in, 80)
                    sp.dma_start(b12, bias_parts).then_inc(b_in, 16)
                    sp.wait_ge(b_in, 96)
                    sp.wait_ge(expert_in, 32)

                @block.vector
                def _(dve):
                    dve.wait_ge(b_in, 32)
                    nc.vector.tensor_copy(parts[0], part_f).then_inc(b_moved, 1)
                    dve.wait_ge(b_moved, 1)
                    nc.vector.tensor_tensor(rest, part_f, parts[0], ALU.subtract).then_inc(b_moved, 1)
                    dve.wait_ge(b_moved, 2)
                    nc.vector.tensor_copy(parts[1], rest).then_inc(b_moved, 1)
                    dve.wait_ge(b_moved, 3)
                    nc.vector.tensor_tensor(parts[2], rest, parts[1], ALU.subtract).then_inc(b_moved, 1)

            with nc.Block() as block:
                load_and_store(block, XE, YE, groups, 0)

                @block.tensor
                def _(pe):
                    def hidden(i, half, own):
                        if half == 0:
                            pe.wait_ge(e["xt"], i.g + 1)
                        if not i.first(2):
                            pe.wait_ge(e["clipped"], (i.g - 2) * 2 + half + 1)
                        pe.nop(nofuse=True)
                        for c in (2 * half, 2 * half + 1):
                            x_e = own[c]
                            h = H_[2 * i.par + half][:, 256 * (c % 2):256 * (c % 2) + 256]
                            nc.tensor.matmul(h, ones_b[0:3, :], b12[:, bass.ds(x_e, 1), 0:256], start=True, stop=False,
                                             skip_group_check=True)
                            last = nc.tensor.matmul(h, XT[i.par][:, c * P:(c + 1) * P], W0a[:, bass.ds(x_e, 1), :],
                                                    start=False, stop=True, skip_group_check=True)
                        last.then_inc(e["h_psum"], 1)

                    def body(i, ahead, main, behind):
                        nx, pv = i.at(1), i.at(-1)
                        if ahead:
                            transposed_rows(nx, pe, XE, A_)
                        own = experts_of(i, E0) if main else None
                        if main:
                            hidden(i, 0, own)
                        if behind:
                            pe.wait_ge(e["hidden"], pv.g + 1)
                            if not pv.first(1):
                                pe.wait_ge(e["ht"], pv.g)
                            for c in range(GROUP):
                                last = nc.tensor.transpose(C_[:, c * P:(c + 1) * P],
                                                           HA[pv.par][:, c * P:(c + 1) * P], ident[:])
                            last.then_inc(e["ht_psum"], 1)
                        if main:
                            hidden(i, 1, own)
                        own_before = experts_of(pv, E0) if behind else None
                        if behind:
                            pe.wait_ge(e["ht"], pv.g + 1)
                            if not pv.first(1):
                                pe.wait_ge(e["y"], pv.g)
                            pe.nop(nofuse=True)
                            for c in range(GROUP):
                                x_e = own_before[c]
                                y = Y_[:, c * P:(c + 1) * P]
                                nc.tensor.matmul(y, ones_b[0:3, :], b12[:, bass.ds(x_e, 1), 256:384], start=True,
                                                 stop=False, skip_group_check=True)
                                last = nc.tensor.matmul(y, AT[pv.par][:, c * P:(c + 1) * P],
                                                        W0b[:, bass.ds(x_e, 1), :], start=False, stop=True,
                                                        skip_group_check=True)
                            last.then_inc(e["y_psum"], 1)

                    pipeline(pe, groups, 0, body)

                @block.scalar
                def _(act):
                    def body(i, ahead, main, behind):
                        nx, pv = i.at(1), i.at(-1)
                        if ahead:
                            act.wait_ge(e["xt_psum"], nx.g + 1)
                            nc.scalar.activation(XT[nx.par], A_[nx.par][:, :], ACT.Copy).then_inc(e["xt"], 1)
                        if behind:
                            act.wait_ge(e["ht_psum"], pv.g + 1)
                            nc.scalar.activation(AT[pv.par], C_[:, :], ACT.Copy).then_inc(e["ht"], 1)
                        if main:
                            act.wait_ge(e["clipped"], i.g * 2 + 2)
                            nc.scalar.activation(AG[i.par], GL[i.par], ACT.Gelu_apprx_sigmoid).then_inc(e["gated"], 1)

                    pipeline(act, groups, 0, body)

                @block.vector
                def _(dve):
                    def body(i, ahead, main, behind):
                        pv = i.at(-1)
                        if main:
                            for half in range(2):
                                dve.wait_ge(e["h_psum"], i.g * 2 + half + 1)
                                h = H_[2 * i.par + half][:, :].rearrange("p (c u f) -> p c u f", c=2, u=2)
                                at = slice(half * 256, half * 256 + 256)
                                nc.vector.tensor_scalar(GL[i.par][:, at].rearrange("p (c f) -> p c f", c=2),
                                                        h[:, :, 0, :], LIMIT, None, ALU.min)
                                nc.vector.tensor_scalar(LN[i.par][:, at].rearrange("p (c f) -> p c f", c=2),
                                                        h[:, :, 1, :], LIMIT, -LIMIT, ALU.min, ALU.max
                                                        ).then_inc(e["clipped"], 1)
                            dve.wait_ge(e["gated"], i.g + 1)
                            dve.wait_ge(e["clipped"], i.g * 2 + 2)
                            nc.vector.scalar_tensor_tensor(HA[i.par], LN[i.par], 1.0, AG[i.par], ALU.add, ALU.mult
                                                           ).then_inc(e["hidden"], 1)
                        if behind:
                            dve.wait_ge(e["y_psum"], pv.g + 1)
                            if not pv.first(2):
                                dve.wait_ge(results_out[pv.par], pv.half * 16)
                            nc.vector.tensor_copy(YE[pv.par], Y_[:, :]).then_inc(e["y"], 1)

                    pipeline(dve, groups, 0, body)

        def experts1():
            groups = SLOT_TILES[1] // GROUP
            base = SLOT_TILES[0] // GROUP
            place[0] = 0
            XE, XT, YE = (carve2(GROUP * D) for _ in range(3))
            SI, HM = carve2(F1), carve2(F1)
            AT = carve2(3 * P)
            A_, H_, C_, Y_ = bank[0], bank[1:5], bank[5], bank[6:8]

            with nc.Block() as block:
                load_and_store(block, XE, YE, groups, base)

                def tiles_of(eng, body):
                    at = lambda k: Step(0, k, base)
                    body(at(-1), 2, False, False, False, True)
                    for n in (0, 1):
                        for c in range(GROUP):
                            body(at(n), c, n > 0 or c > 0, n > 0 or c > 1, True, c == 2)
                    with eng.Fori(1, groups // 2 - 1) as m:
                        for n in range(2):
                            for c in range(GROUP):
                                body(Step(m, n, base), c, True, True, True, c == 2)
                    for n in (groups - 2, groups - 1):
                        for c in range(GROUP):
                            body(at(n), c, True, True, True, c == 2 and n < groups - 1)
                    body(at(groups), 0, True, True, False, False)
                    body(at(groups), 1, False, True, False, False)

                def back(i, c, k):
                    return (i.at(-1), c - k + GROUP) if c < k else (i, c - k)

                @block.tensor
                def _(pe):
                    own = {}

                    def body(i, c, lag1, lag2, main, ahead):
                        if main and c == 0:
                            own[0] = experts_of(i, E1)
                            hold(pe, e["xt"], i.g + 1)
                        if main:
                            r = c % 2
                            if not (isinstance(i.n, int) and i.n * GROUP + c < 2):
                                hold(pe, e1["hidden1"], i.n * GROUP + c - 1)
                            x_e = own[0][c]
                            for u in range(2):
                                last = nc.tensor.matmul(H_[2 * r + u][:, 0:F1], XT[i.par][:, c * P:(c + 1) * P],
                                                        W1a[:, bass.ds(x_e, 1), u * F1:(u + 1) * F1],
                                                        start=True, stop=True)
                            last.then_inc(e1["h1_psum"], 1)
                        if c == 0 and lag1:
                            own[1] = experts_of(i.at(-1), E1)
                        if lag2:
                            j, d = back(i, c, 2)
                            count = j.n * GROUP + d
                            pe.wait_ge(e1["ht1"], count + 1)
                            if d == 0 and not (isinstance(j.n, int) and j.n < 2):
                                pe.wait_ge(e["y"], j.g - 1)
                            pe.nop(nofuse=True)
                            x_e = own[0][d] if c >= 2 else own[1][d]
                            for k, f in enumerate(F1_BLOCKS):
                                last = nc.tensor.matmul(Y_[j.par][:, d * P:(d + 1) * P],
                                                        AT[d % 2][0:f, k * P:(k + 1) * P],
                                                        W1b[0:f, bass.ds(x_e, 1), k * P:(k + 1) * P],
                                                        start=(k == 0), stop=(k == 2))
                            if d == GROUP - 1:
                                last.then_inc(e1["y1_psum"], 1)
                        if lag1:
                            j, d = back(i, c, 1)
                            count = j.n * GROUP + d
                            pe.wait_ge(e1["hidden1"], count + 1)
                            for k, f in enumerate(F1_BLOCKS):
                                last = nc.tensor.transpose(C_[0:f, k * P:(k + 1) * P],
                                                           HM[d % 2][:, k * P:k * P + f], ident[:])
                            last.then_inc(e1["ht1_psum"], 1)
                        if ahead:
                            nx = i.at(1)
                            pe.wait_ge(slots_in[nx.par], (nx.half + base // 2 + 1) * 16)
                            pe.wait_ge(e["xt"], nx.g)
                            for k in range(GROUP):
                                last = nc.tensor.transpose(A_[:, k * P:(k + 1) * P], XE[nx.par][:, k * P:(k + 1) * P],
                                                           ident[:])
                            last.then_inc(e["xt_psum"], 1)

                    tiles_of(pe, body)

                @block.scalar
                def _(act):
                    def body(i, c, lag1, lag2, main, ahead):
                        if main:
                            act.wait_ge(e1["h1_psum"], i.n * GROUP + c + 1)
                            nc.scalar.activation(SI[c % 2], H_[2 * (c % 2)][:, 0:F1], ACT.Silu
                                                 ).then_inc(e1["silu1"], 1)
                        if lag1:
                            j, d = back(i, c, 1)
                            count = j.n * GROUP + d
                            act.wait_ge(e1["ht1_psum"], count + 1)
                            nc.scalar.activation(AT[d % 2][:, 0:2 * P], C_[:, 0:2 * P], ACT.Copy)
                            nc.scalar.activation(AT[d % 2][0:96, 2 * P:3 * P], C_[0:96, 2 * P:3 * P], ACT.Copy
                                                 ).then_inc(e1["ht1"], 1)
                        if ahead:
                            nx = i.at(1)
                            act.wait_ge(e["xt_psum"], nx.g + 1)
                            nc.scalar.activation(XT[nx.par], A_[:, :], ACT.Copy).then_inc(e["xt"], 1)

                    tiles_of(act, body)

                @block.vector
                def _(dve):
                    def body(i, c, lag1, lag2, main, ahead):
                        if main:
                            dve.wait_ge(e1["silu1"], i.n * GROUP + c + 1)
                            nc.vector.tensor_tensor(HM[c % 2], H_[2 * (c % 2) + 1][:, 0:F1], SI[c % 2], ALU.mult
                                                    ).then_inc(e1["hidden1"], 1)
                        if lag2:
                            j, d = back(i, c, 2)
                            if d == GROUP - 1:
                                dve.wait_ge(e1["y1_psum"], j.n + 1)
                                if not (isinstance(j.n, int) and j.n < 2):
                                    dve.wait_ge(results_out[j.par], (j.half + base // 2) * 16)
                                nc.vector.tensor_copy(YE[j.par], Y_[j.par][:, :]).then_inc(e["y"], 1)

                    tiles_of(dve, body)

        final_index = sem("final_index")
        final_in = [sem(f"final_in{q}") for q in range(2)]
        final_sum = sem("final_sum")
        stored = [sem(f"stored{q}") for q in range(2)]

        def finish():
            place[0] = 0
            gb = carve2(2 * K1 * D)
            gi = carve2(2 * K1, I32)
            res = carve2(2 * D)
            out_rows = out.rearrange("b s d -> (b s) d").rearrange("(i p) d -> p i d", p=P)
            with nc.Block() as block:
                @block.gpsimd
                def _(pool):
                    def gather(i, skip):
                        q = i.par
                        if not skip:
                            pool.wait_ge(final_sum, (i.n - 1) * 2)
                        nc.gpsimd.tensor_copy(gi[q].rearrange("p (i k) -> p i k", i=2),
                                              slot[:, bass.ds(i.n * 2, 2), 0:K1]).then_inc(final_index, 1)
                        hold(pool, final_index, i.n + 1)
                        for k in range(2 * K1):
                            nc.gpsimd.indirect_dma_start(
                                out=gb[q][:, k * D:(k + 1) * D], out_offset=None, in_=ys,
                                in_offset=bass.IndirectOffsetOnAxis(ap=gi[q][:, k:k + 1], axis=0),
                            ).then_inc(final_in[q], 16)

                    gather(Step(0, 0), True)
                    gather(Step(0, 1), True)
                    with pool.Fori(1, ITERS // 2) as m:
                        for c in range(2):
                            gather(Step(m, c), False)

                @block.vector
                def _(dve):
                    def add(i, skip):
                        q = i.par
                        dve.wait_ge(final_in[q], (i.half + 1) * 16 * 2 * K1)
                        if not skip:
                            dve.wait_ge(stored[q], i.half * 16)
                        for k in range(K1):
                            for j in range(2):
                                xt = X[:, bass.ds(i.n * 2 + j, 1), :].rearrange("p i d -> p (i d)")
                                at = (j * K1 + k) * D
                                src = xt if k == 0 else res[q][:, j * D:(j + 1) * D]
                                last = nc.vector.scalar_tensor_tensor(
                                    res[q][:, j * D:(j + 1) * D], gb[q][:, at:at + D],
                                    wts[:, bass.ds(i.n * 2 + j, 1), k], src, ALU.mult, ALU.add)
                            last.then_inc(final_sum, 1)
                            if k < K1 - 1:
                                dve.wait_ge(final_sum, i.n * K1 + k + 1)

                    add(Step(0, 0), True)
                    add(Step(0, 1), True)
                    with dve.Fori(1, ITERS // 2) as m:
                        for c in range(2):
                            add(Step(m, c), False)

                @block.sync
                def _(sp):
                    with sp.Fori(0, ITERS // 2) as m:
                        for c in range(2):
                            i = Step(m, c)
                            sp.wait_ge(final_sum, (i.n + 1) * K1)
                            sp.dma_start(out_rows[:, bass.ds(i.n * 2, 2), :],
                                         res[i.par].rearrange("p (i d) -> p i d", i=2)).then_inc(stored[i.par], 16)
                    for q in range(2):
                        sp.wait_ge(stored[q], 16 * ITERS // 2)

        attention(0)
        chained_before = chained[0]
        slots(0)
        dispatch(0)
        experts0()
        attention(1)
        chained_before = chained[0]
        slots(1)
        dispatch(1)
        experts1()
        finish()


def kernel(**inputs):
    import numpy as np
    import concourse.bacc as bacc
    from concourse.bass_utils import run_bass_kernel_spmd as run

    nc = bacc.Bacc("TRN2", target_bir_lowering=False, num_devices=1)
    i = {k: np.ascontiguousarray(v) for k, v in inputs.items()}
    arrays = {k: i[k] for k in ("x", "ctx_1024", "L0_xattn_bq", "L0_xattn_bk", "L0_xattn_bv", "L0_xattn_bo",
                                "L1_xattn_bq", "L1_xattn_bk", "L1_xattn_bv", "L1_xattn_bo",
                                "L0_ffn_norm_scale", "L0_ffn_gate_b", "L0_ffn_b2")}
    arrays["mask"] = i["mask_BxS2_bf0"]
    half = np.arange(D).reshape(HEADS, 2, HD // 2)[:, ::-1].reshape(-1)
    arrays["proj"] = np.ascontiguousarray(np.stack(
        [i["L0_xattn_" + n] for n in ("Wq", "Wk", "Wv", "Wo")] + [i["L1_xattn_" + n] for n in ("Wq", "Wk", "Wv", "Wo")]
        + [i["L1_xattn_Wq"][:, half], i["L1_xattn_Wk"][:, half]], axis=1))
    arrays["bqr"] = np.ascontiguousarray(i["L1_xattn_bq"][half])
    arrays["bkr"] = np.ascontiguousarray(i["L1_xattn_bk"][half])
    arrays["gate0"] = np.ascontiguousarray(i["L0_ffn_gate_w"].T)
    arrays["gate1"] = np.ascontiguousarray(i["L1_ffn_gate_w"].T)
    w1 = i["L0_ffn_w1"].reshape(E0, F0, 2, D).transpose(3, 0, 2, 1).reshape(D, E0, 2 * F0)
    arrays["w1_0"] = np.ascontiguousarray(w1)
    arrays["b1_0"] = np.ascontiguousarray(i["L0_ffn_b1"].reshape(E0, F0, 2).transpose(0, 2, 1).reshape(E0, 2 * F0))
    arrays["w2_0"] = np.ascontiguousarray(i["L0_ffn_w2"].transpose(2, 0, 1))
    arrays["w13_1"] = np.ascontiguousarray(
        np.concatenate([i["L1_ffn_w1"].transpose(2, 0, 1), i["L1_ffn_w3"].transpose(2, 0, 1)], axis=2))
    w2 = np.zeros((E1, D, 3 * P), np.float32)
    w2[:, :, :F1] = i["L1_ffn_w2"]
    arrays["w2_1"] = np.ascontiguousarray(w2.reshape(E1, D, 3, P).transpose(3, 0, 2, 1).reshape(P, E1, 3 * P))
    arrays["ident"] = np.eye(P, dtype=np.float32)
    arrays["before"] = np.triu(np.ones((P, P), np.float32), 1)
    arrays["head_of"] = (np.arange(P)[:, None] // HD % 4 == np.arange(4)[None, :]).astype(np.float32)
    arrays["seq_of"] = (np.arange(P)[None, :] // S == np.arange(2)[:, None]).astype(np.float32)
    freq = (1.0 / np.float32(10000.0) ** (np.arange(0, HD, 2, dtype=np.float32) / np.float32(HD))).astype(np.float32)
    angle = (np.arange(S, dtype=np.float32)[None, :] * freq[np.arange(P) % (HD // 2)][:, None]).astype(np.float32)
    sign = np.where(np.arange(P) % HD < HD // 2, -1.0, 1.0).astype(np.float32)[:, None]
    arrays["cos"] = np.cos(angle).astype(np.float32)
    arrays["sin"] = (np.sin(angle) * sign).astype(np.float32)
    args = {n: nc.dram_tensor("in_" + n, v.shape, mybir.dt.from_np(v.dtype), kind="ExternalInput").ap()
            for n, v in arrays.items()}
    out = nc.dram_tensor("out_x", (B, S, D), F32, kind="ExternalOutput").ap()
    xs = nc.dram_tensor("slot_rows", (SLOT_TILES[0] * P, D), F32, kind="Internal").ap()
    ys = nc.dram_tensor("slot_results", (SLOT_TILES[0] * P, D), F32, kind="Internal").ap()
    parts = nc.dram_tensor("bias_parts", (3, E0, 3 * F0), BF16, kind="Internal").ap()
    build(nc, args, out, xs, ys, parts)
    r = run(nc, [{"in_" + n: v for n, v in arrays.items()}], core_ids=[0])
    return r.results[0]["out_x"]
```

```python
from contextlib import ExitStack
from functools import partial

import concourse.bass as bass
from concourse import mybir

F32 = mybir.dt.float32
BF16 = mybir.dt.bfloat16
F16 = mybir.dt.float16
I32 = mybir.dt.int32
U32 = mybir.dt.uint32
U8 = mybir.dt.uint8
ALU = mybir.AluOpType
ACT = mybir.ActivationFunctionType
AX = mybir.AxisListType

P = 128
B, S, D = 128, 64, 128
HEADS = 16
HD = D // HEADS
TOKENS = B * S
TILES = TOKENS // P
ITERS = TILES // 2
UNITS = 4
SCALE = float(HD) ** -0.5
EPS = 1e-5
MASKED = -1e30

E0, K0, F0 = 32, 4, 128
E1, K1, F1 = 8, 2, 352
F1_BLOCKS = [128, 128, 96]
GROUP = 4
SLOT_TILES = [TOKENS * K0 // P + E0, TOKENS * K1 // P + 2 * E1]
HALF_SLOT_TILES = SLOT_TILES[1] // 2
SUM_FROM = HALF_SLOT_TILES // GROUP + 2
RING = 4
STORE_LAG = 6
LIMIT = 7.0
ARENA = 15904


class Step:

    def __init__(self, m, c, base=0):
        self.m, self.c, self.base = m, c, base
        self.n = m * 2 + c
        self.half = m + c // 2
        self.par = c % 2
        self.g = self.n + base

    def at(self, k):
        return Step(self.m, self.c + k, self.base)

    def first(self, k):
        return isinstance(self.g, int) and self.g < k


def hold(eng, sem, value):
    eng.wait_ge(sem, value)
    eng.nop(nofuse=True)


def build(nc, a, out, ts, ys, bias_parts):
    with ExitStack() as ctx:
        def sb(name, shape, dt=F32):
            return ctx.enter_context(nc.sbuf_tensor(name, shape, dt))

        def sem(name):
            return ctx.enter_context(nc.semaphore(name))

        bank = [ctx.enter_context(nc.psum_tensor(f"bank{i}", [P, 512], F32)) for i in range(8)]

        X = sb("X", [P, TILES, D])
        token_of_slot = sb("token_of_slot", [P, SLOT_TILES[0]], I32)
        W = sb("W", [P, E0 * 3 * F0])
        top = sb("top", [P, TILES, 8])
        top_at = sb("top_at", [P, TILES, 8], U32)
        wts = sb("wts", [P, TILES, K0])
        slot = sb("slot", [P, TILES, K0], I32)
        group_experts = sb("group_experts", [1, SLOT_TILES[0] // GROUP], I32)
        ident = sb("ident", [P, P])
        head_of = sb("head_of", [P, 4])
        before = sb("before", [P, P], BF16)
        ones_b = sb("ones_b", [P, P], BF16)
        seq_of = sb("seq_of", [2, P], BF16)
        mask_rows = sb("mask_rows", [2, TILES, S], BF16)
        cos = sb("cos", [P, S])
        sin = sb("sin", [P, S])
        ones_f = sb("ones_f", [P, 1])
        power = sb("power", [P, 2])
        Wm = sb("Wm", [P, 10, D])
        bias_t = sb("bias_t", [P, 8])
        bias_r = sb("bias_r", [P, 3, D])
        gate_w = sb("gate_w", [P, E0 + E1])
        gate_b = sb("gate_b", [P, E0])
        Vbd = [sb(f"Vbd{q}", [P, 8, 4, 2, HD + 1]) for q in range(2)]

        arena = sb("arena", [P, ARENA])
        place = [0]

        def carve(width, dt=F32):
            lo = place[0]
            place[0] += width if dt in (F32, I32, U32) else (width + 1) // 2
            assert place[0] <= ARENA, place[0]
            v = arena[:, lo:place[0]]
            return v if dt == F32 else v.bitcast(dt)

        b12_words = E0 * 3 * F0 // 2
        b12 = arena[0:3, ARENA - b12_words:ARENA].bitcast(BF16).rearrange("r (e f) -> r e f", e=E0)

        def carve2(width, dt=F32):
            return [carve(width, dt) for _ in range(2)]

        W0a = W[:, 0:E0 * 256].rearrange("p (e f) -> p e f", e=E0)
        W0b = W[:, E0 * 256:E0 * 384].rearrange("p (e f) -> p e f", e=E0)
        W1a = W[:, 0:E1 * 704].rearrange("p (e f) -> p e f", e=E1)
        W1b = W[:, E1 * 704:E1 * 1088].rearrange("p (e f) -> p e f", e=E1)
        expert_in = sem("expert_in")

        const_in = sem("const_in")
        b_in, b_moved = sem("b_in"), sem("b_moved")
        setup_dve = sem("setup_dve")
        setup_pool = sem("setup_pool")
        N_CONST = 22
        wide_t = carve(P)
        mask_u8 = arena[0:2, 256:256 + TILES * S // 4].bitcast(U8)
        part_f, rest = (arena[0:E0, at:at + 3 * F0] for at in (5120, 5632))
        parts = [arena[0:E0, at:at + 3 * F0 // 2].bitcast(BF16) for at in (6144, 6400, 6656)]
        with nc.Block() as block:
            @block.scalar
            def _(act):
                act.dma_start(part_f[:, 0:2 * F0], a["b1_0"]).then_inc(b_in, 16)
                act.dma_start(part_f[:, 2 * F0:3 * F0], a["L0_ffn_b2"]).then_inc(b_in, 16)
                for n, moved in enumerate((1, 3, 4)):
                    act.wait_ge(b_moved, moved)
                    act.dma_start(bias_parts[n], parts[n]).then_inc(b_in, 16)
                act.wait_ge(b_in, 80)

            @block.sync
            def _(sp):
                row = lambda x: x.rearrange("(a n) -> a n", a=1).broadcast_to([P, D])
                col = lambda x: x.rearrange("(n a) -> n a", a=1)
                loads = [(ident[:], a["ident"]), (head_of[:], a["head_of"]), (wide_t, a["before"]),
                         (cos[:], a["cos"]), (sin[:], a["sin"]), (gate_w[:, 0:E0], a["gate0"]),
                         (gate_w[:, E0:E0 + E1], a["gate1"]),
                         (Wm[:].rearrange("p w d -> p (w d)").rearrange("p (w d) -> p w d", w=10), a["proj"]),
                         (gate_b[:], a["L0_ffn_gate_b"].rearrange("(a n) -> a n", a=1).broadcast_to([P, E0])),
                         (mask_u8.rearrange("b (i s) -> b i s", i=TILES),
                          a["mask"].rearrange("(i b) s -> b i s", b=2)),
                         (arena[0:2, 4096:4096 + P], a["seq_of"])]
                for n, name in enumerate(("L0_xattn_bq", "L0_xattn_bk", "L1_xattn_bq", "L1_xattn_bk", "bqr", "bkr",
                                          "L0_xattn_bv", "L1_xattn_bv")):
                    loads.append((bias_t[:, n:n + 1], col(a[name])))
                for n, name in enumerate(("L0_xattn_bo", "L0_ffn_norm_scale", "L1_xattn_bo")):
                    loads.append((bias_r[:, n, :], row(a[name])))
                assert len(loads) == N_CONST
                for dst, src in loads:
                    sp.dma_start(dst, src).then_inc(const_in, 16)
                sp.dma_start(W0a, a["w1_0"]).then_inc(expert_in, 16)
                sp.dma_start(W0b, a["w2_0"]).then_inc(expert_in, 16)

            @block.vector
            def _(dve):
                nc.vector.memset(ones_b[:], 1.0)
                nc.vector.memset(ones_f[:], 1.0)
                nc.vector.memset(power[:], -0.5)
                dve.wait_ge(b_in, 32)
                nc.vector.tensor_copy(parts[0], part_f).then_inc(b_moved, 1)
                dve.wait_ge(b_moved, 1)
                nc.vector.tensor_tensor(rest, part_f, parts[0], ALU.subtract).then_inc(b_moved, 1)
                dve.wait_ge(b_moved, 2)
                nc.vector.tensor_copy(parts[1], rest).then_inc(b_moved, 1)
                dve.wait_ge(b_moved, 3)
                nc.vector.tensor_tensor(parts[2], rest, parts[1], ALU.subtract).then_inc(b_moved, 1)
                dve.wait_ge(const_in, 16 * N_CONST)
                nc.vector.tensor_copy(before[:], wide_t)
                nc.vector.tensor_copy(seq_of[:], arena[0:2, 4096:4096 + P])
                nc.vector.tensor_scalar(mask_rows[:].rearrange("b i s -> b (i s)"), mask_u8, MASKED, None,
                                        ALU.mult).then_inc(setup_dve, 1)
                dve.wait_ge(setup_dve, 1)

            @block.gpsimd
            def _(pool):
                for q in range(2):
                    nc.gpsimd.memset(Vbd[q][:], 0.0).then_inc(setup_pool, 1)
                pool.wait_ge(setup_pool, 2)
                for q in range(2):
                    nc.gpsimd.memset(Vbd[q][0:64, :, :, 0, HD:HD + 1], 1.0)
                    nc.gpsimd.memset(Vbd[q][64:128, :, :, 1, HD:HD + 1], 1.0).then_inc(setup_pool, 1)
                pool.wait_ge(setup_pool, 4)

        x_rows = a["x"].rearrange("b s d -> (b s) d").rearrange("(i p) d -> p i d", p=P)
        ctx_rows = a["ctx_1024"].rearrange("b s d -> (b s) d").rearrange("(i p) d -> p i d", p=P)
        ts_rows = ts.rearrange("(i p) d -> p i d", p=P)
        ys_rows = ys.rearrange("(g c p) d -> g p c d", c=GROUP, p=P)

        x_in = [sem(f"x_in{q}") for q in range(2)]
        ctx_in = [sem(f"ctx_in{q}") for q in range(2)]
        t_stored = [sem(f"t_stored{q}") for q in range(2)]
        gathered = [sem(f"gathered{q}") for q in range(2)]
        names = ("stats_a", "moments_a", "eps_a", "rstd_a", "normed", "cx_psum", "cx", "v_psum", "vbd", "qk_psum",
                 "qk", "rot_psum", "rot", "keys", "queries", "rope", "kbd", "score_psum", "score_max", "centred",
                 "t_psum", "probs", "o_psum", "o_copied", "o_recip", "o_normed", "ot_psum", "ot", "wo_psum",
                 "x_plus_bo", "added", "stats_r", "moments_r", "pool_r", "rstd_r", "ms_r", "z", "t_ready", "tt_psum", "tt",
                 "gate_psum", "logits", "top8", "chosen", "top_kept", "index_copied", "combined", "q_zero", "z_added")
        s = {n: sem(n) for n in names}

        def attention(layer):
            place[0] = 0
            ctx_t = carve2(2 * D)
            xn = carve2(2 * D)
            CX = carve2(4 * D)
            Qz = carve2(UNITS * 2 * D)
            QKs = carve2(4 * D) if layer else None
            Kt = [v[:, 2 * D:4 * D] for v in QKs] if layer else carve2(2 * D)
            QKe, QKr = (carve(4 * D), carve(4 * D)) if layer else (None, None)
            Kbd = carve2(1024)
            mx = carve(32)
            Sc = carve2(512)
            Pt = carve2(512)
            AO = carve2(2 * HEADS * (HD + 1))
            rec = carve2(2 * HEADS)
            aon = carve2(2 * D)
            aoT = carve2(2 * D)
            xb = carve2(2 * D)
            z = None if layer else carve2(2 * D)
            t = carve2(2 * D)
            tT = carve2(2 * D)
            lg, tp, ta = carve2(2 * (E1 if layer else E0)), carve2(16), carve2(16, U32)
            small = {n: carve2(w) for n, w in (("st_a", 12), ("mv_a", 4), ("ve_a", 2), ("rs_a", 2), ("st_r", 12),
                                               ("mv_r", 4), ("ve_r", 2), ("rs_r", 2), ("ms", 2), ("ms1", 2),
                                               ("ms2", 2), ("r2", 2))}
            gb = carve2(2 * K0 * D) if layer else None
            gi = carve2(2 * K0, I32) if layer else None

            wq, wk, wv, wo = (Wm[:, 4 * layer + n, :] for n in range(4))
            bq, bk = bias_t[:, 2 * layer:2 * layer + 1], bias_t[:, 2 * layer + 1:2 * layer + 2]
            bv, bo = bias_t[:, 6 + layer:7 + layer], bias_r[:, 2 * layer, :]
            n_e = E1 if layer else E0
            pool_heads = 3 if layer else 4
            gw = gate_w[:, E0:E0 + E1] if layer else gate_w[:, 0:E0]
            S_, T_, O_, M_, P_ = bank[0:2], bank[2:4], bank[4:6], bank[6], bank[7]
            base = layer * ITERS

            def tiles(buf, i):
                return buf[:, bass.ds(i.n * 2, 2), :]

            def bodies(eng, body):
                at = lambda n: body(Step(0, n, base), lambda k: 0 <= n + k < ITERS)
                for n in range(-4, 4):
                    at(n)
                with eng.Fori(2, (ITERS - 4) // 2) as m:
                    for c in range(2):
                        body(Step(m, c, base), lambda k: True)
                for n in range(ITERS - 4, ITERS + 3):
                    at(n)

            with nc.Block() as block:
                @block.vector
                def _(dve):
                    for q in range(2):
                        nc.vector.memset(Qz[q], 0.0).then_inc(s["q_zero"], 1)
                    dve.wait_ge(s["q_zero"], 2 * layer + 2)

            with nc.Block() as block:
                @block.sync
                def _(sp):
                    def load(i):
                        q = i.par
                        if not i.first(2):
                            sp.wait_ge(s["cx_psum"], i.g - 1)
                        if not layer:
                            sp.dma_start(tiles(X, i), x_rows[:, bass.ds(i.n * 2, 2), :]).then_inc(x_in[q], 16)
                        sp.dma_start(ctx_t[q].rearrange("p (i d) -> p i d", i=2),
                                     ctx_rows[:, bass.ds(i.n * 2, 2), :]).then_inc(ctx_in[q], 16)

                    def store(i):
                        sp.wait_ge(s["t_ready"], i.g + 1)
                        sp.dma_start(ts_rows[:, bass.ds(i.n * 2, 2), :],
                                     t[i.par].rearrange("p (i d) -> p i d", i=2)).then_inc(t_stored[i.par], 16)

                    for n in range(STORE_LAG):
                        load(Step(0, n, base))
                    if layer:
                        sp.dma_start(W1a, a["w13_1"]).then_inc(expert_in, 16)
                        sp.dma_start(W1b, a["w2_1"]).then_inc(expert_in, 16)
                    with sp.Fori(STORE_LAG // 2, ITERS // 2) as m:
                        for c in range(2):
                            load(Step(m, c, base))
                            store(Step(m, c - STORE_LAG, base))
                    for n in range(ITERS - STORE_LAG, ITERS):
                        store(Step(0, n, base))
                    for q in range(2):
                        sp.wait_ge(t_stored[q], 16 * (ITERS + base) // 2)
                    if layer:
                        sp.wait_ge(expert_in, 64)

                @block.gpsimd
                def _(pool):
                    def gather(i, half):
                        q = i.par
                        if half == 0:
                            if not (isinstance(i.n, int) and i.n < 2):
                                pool.wait_ge(s["combined"], (i.n - 1) * K0)
                            nc.gpsimd.tensor_copy(gi[q].rearrange("p (i k) -> p i k", i=2),
                                                  tiles(slot, i)).then_inc(s["index_copied"], 1)
                            hold(pool, s["index_copied"], i.n + 1)
                        for k in range(half * K0, (half + 1) * K0):
                            nc.gpsimd.indirect_dma_start(
                                out=gb[q][:, k * D:(k + 1) * D], out_offset=None, in_=ys,
                                in_offset=bass.IndirectOffsetOnAxis(ap=gi[q][:, k:k + 1], axis=0),
                            ).then_inc(gathered[q], 16)

                    def scale_inputs(i):
                        ve, rs = small["ve_a"][i.par], small["rs_a"][i.par]
                        hold(pool, s["moments_a"], i.g + 1)
                        nc.gpsimd.tensor_scalar(ve, small["mv_a"][i.par].rearrange("p (i c) -> p i c", i=2)[:, :, 1],
                                                EPS, None, ALU.add).then_inc(s["eps_a"], 1)
                        pool.wait_ge(s["eps_a"], i.g + 1)
                        nc.gpsimd.tensor_tensor(rs, ve, power[:], ALU.pow).then_inc(s["rstd_a"], 1)

                    def spread_keys(i):
                        pool.wait_ge(s["rope" if layer else "keys"], i.n + 1)
                        n = pool_heads
                        nc.gpsimd.tensor_tensor(
                            Kbd[i.par].rearrange("p (b j k) -> p b j k", b=4, j=4)[:, :, 0:n, :],
                            Kt[i.par].rearrange("p (b k) -> p b k", b=4).unsqueeze(2).broadcast_to([P, 4, n, S]),
                            head_of[:, 0:n].unsqueeze(1).unsqueeze(3).broadcast_to([P, 4, n, S]),
                            ALU.mult).then_inc(s["kbd"], 1)

                    def scale_outputs(i):
                        q = i.par
                        mv, ve, rs = small["mv_r"][q], small["ve_r"][q], small["rs_r"][q]
                        var = mv.rearrange("p (i c) -> p i c", i=2)[:, :, 1]
                        hold(pool, s["moments_r"], i.g + 1)
                        nc.gpsimd.tensor_scalar(ve, var, EPS, None, ALU.add).then_inc(s["pool_r"], 1)
                        pool.wait_ge(s["pool_r"], i.g + 1)
                        nc.gpsimd.tensor_tensor(rs, ve, power[:], ALU.pow).then_inc(s["rstd_r"], 1)
                        if not layer:
                            ms, ms1, ms2 = small["ms"][q], small["ms1"][q], small["ms2"][q]
                            pool.wait_ge(s["rstd_r"], i.g + 1)
                            nc.gpsimd.tensor_tensor(ms, rs, rs, ALU.mult).then_inc(s["ms_r"], 1)
                            pool.wait_ge(s["ms_r"], i.g * 4 + 1)
                            nc.gpsimd.tensor_tensor(ms1, ms, var, ALU.mult).then_inc(s["ms_r"], 1)
                            hold(pool, s["ms_r"], i.g * 4 + 2)
                            nc.gpsimd.tensor_scalar(ms2, ms1, EPS, None, ALU.add).then_inc(s["ms_r"], 1)
                            pool.wait_ge(s["ms_r"], i.g * 4 + 3)
                            nc.gpsimd.tensor_tensor(small["r2"][q], ms2, power[:], ALU.pow).then_inc(s["ms_r"], 1)

                    def body(i, on):
                        ex, nx, pv, pp, p3 = i.at(2), i.at(1), i.at(-1), i.at(-2), i.at(-3)
                        if on(-1):
                            if not pv.first(2):
                                hold(pool, s["added"], pv.g - 1)
                            nc.gpsimd.tensor_tensor(xb[pv.par].rearrange("p (i d) -> p i d", i=2), tiles(X, pv),
                                                    bo.unsqueeze(1).broadcast_to([P, 2, D]),
                                                    ALU.add).then_inc(s["x_plus_bo"], 1)
                        if layer and on(4):
                            gather(i.at(4), 0)
                        if not layer and on(2):
                            scale_inputs(ex)
                        if on(1):
                            spread_keys(nx)
                        if layer and on(2):
                            scale_inputs(ex)
                        if not layer and on(-2):
                            hold(pool, s["z"], pp.n + 1)
                            nc.gpsimd.tensor_tensor(tiles(X, pp), tiles(X, pp),
                                                    z[pp.par].rearrange("p (i d) -> p i d", i=2), ALU.add
                                                    ).then_inc(s["z_added"], 1)
                        if layer and on(4):
                            gather(i.at(4), 1)
                        if on(-3):
                            pool.wait_ge(s["chosen"], p3.g + 1)
                            nc.gpsimd.tensor_copy(tiles(top, p3), tp[p3.par].rearrange("p (i e) -> p i e", i=2))
                            nc.gpsimd.tensor_copy(tiles(top_at, p3), ta[p3.par].rearrange("p (i e) -> p i e", i=2)
                                                  ).then_inc(s["top_kept"], 1)
                        if on(-1):
                            scale_outputs(pv)

                    bodies(pool, body)

                @block.vector
                def _(dve):
                    def stats(i, st, mv, stats_sem, moments_sem):
                        q = i.par
                        for j in range(2):
                            nc.vector.bn_stats(st[q][:, 6 * j:6 * j + 6],
                                               X[:, bass.ds(i.n * 2 + j, 1), :].rearrange("p i d -> p (i d)")
                                               ).then_inc(s[stats_sem], 1)
                        hold(dve, s[stats_sem], i.g * 2 + 2)
                        for j in range(2):
                            last = nc.vector.bn_aggr(mv[q][:, 2 * j:2 * j + 2], st[q][:, 6 * j:6 * j + 6])
                        last.then_inc(s[moments_sem], 1)

                    def normalise(i, dst, mv, rs):
                        q = i.par
                        for j in range(2):
                            last = nc.vector.tensor_scalar(
                                dst[q][:, j * D:(j + 1) * D],
                                X[:, bass.ds(i.n * 2 + j, 1), :].rearrange("p i d -> p (i d)"),
                                mv[q][:, 2 * j:2 * j + 1], rs[q][:, j:j + 1], ALU.subtract, ALU.mult)
                        return last

                    def combine(i, k):
                        q = i.par
                        if k == 0:
                            dve.wait_ge(gathered[q], (i.half + 1) * 16 * 2 * K0)
                        else:
                            dve.wait_ge(s["combined"], i.n * K0 + k)
                        for j in range(2):
                            xt = X[:, bass.ds(i.n * 2 + j, 1), :].rearrange("p i d -> p (i d)")
                            at = (j * K0 + k) * D
                            last = nc.vector.scalar_tensor_tensor(
                                xt, gb[q][:, at:at + D], wts[:, bass.ds(i.n * 2 + j, 1), k], xt,
                                ALU.mult, ALU.add)
                        last.then_inc(s["combined"], 1)

                    def score_unit(i, r):
                        g4 = i.g * UNITS
                        dve.wait_ge(s["score_psum"], g4 + r + 1)
                        src = S_[r % 2][:, :].rearrange("p (h k) -> p h k", k=S)
                        m8 = mx[:, 8 * r:8 * r + 8]
                        nc.vector.tensor_reduce(m8, src, AX.X, ALU.max).then_inc(s["score_max"], 1)
                        dve.wait_ge(s["score_max"], g4 + r + 1)
                        nc.vector.tensor_tensor(Sc[r % 2].rearrange("p (h k) -> p h k", k=S), src,
                                                m8.unsqueeze(2).broadcast_to([P, 8, S]),
                                                ALU.subtract).then_inc(s["centred"], 1)

                    def read_logits(i):
                        dve.wait_ge(s["gate_psum"], i.g + 1)
                        src = M_[:, 0:2 * n_e].rearrange("p (i e) -> p i e", i=2)
                        q = i.par
                        dst = lg[q][:, 0:2 * n_e].rearrange("p (i e) -> p i e", i=2)
                        if layer:
                            nc.vector.tensor_copy(dst, src).then_inc(s["logits"], 1)
                        else:
                            nc.vector.tensor_tensor(dst, src, gate_b[:].unsqueeze(1).broadcast_to([P, 2, E0]),
                                                    ALU.add).then_inc(s["logits"], 1)

                    def choose(i):
                        q = i.par
                        if not i.first(2):
                            dve.wait_ge(s["top_kept"], i.g - 1)
                        hold(dve, s["logits"], i.g + 1)
                        for j in range(2):
                            nc.vector.max(tp[q][:, 8 * j:8 * j + 8], lg[q][:, j * n_e:(j + 1) * n_e]
                                          ).then_inc(s["top8"], 1)
                        hold(dve, s["top8"], i.g * 2 + 2)
                        for j in range(2):
                            last = nc.vector.max_index(ta[q][:, 8 * j:8 * j + 8], tp[q][:, 8 * j:8 * j + 8],
                                                       lg[q][:, j * n_e:(j + 1) * n_e])
                        last.then_inc(s["chosen"], 1)

                    def divide(i):
                        q = i.par
                        dve.wait_ge(s["o_copied"], i.g + 1)
                        ao = AO[q].rearrange("p (h c) -> p h c", c=HD + 1)
                        nc.vector.reciprocal(rec[q].unsqueeze(2), ao[:, :, HD:HD + 1]).then_inc(s["o_recip"], 1)
                        dve.wait_ge(s["o_recip"], i.g + 1)
                        nc.vector.tensor_tensor(aon[q].rearrange("p (h c) -> p h c", c=HD), ao[:, :, 0:HD],
                                                rec[q].unsqueeze(2).broadcast_to([P, 2 * HEADS, HD]),
                                                ALU.mult).then_inc(s["o_normed"], 1)

                    def weigh(i, buf, b0, b1, tab, done):
                        for h, b in ((0, b0), (1, b1)):
                            at = slice(h * 2 * D, (h + 1) * 2 * D)
                            last = nc.vector.scalar_tensor_tensor(
                                buf[:, at].rearrange("p (b s) -> p b s", s=S),
                                P_[:, at].rearrange("p (b s) -> p b s", s=S), b,
                                tab[:].unsqueeze(1).broadcast_to([P, 4, S]), ALU.add, ALU.mult)
                        last.then_inc(s[done], 1)

                    def rotate(i):
                        dve.wait_ge(s["rot_psum"], i.n + 1)
                        weigh(i, QKr, bias_t[:, 4:5], bias_t[:, 5:6], sin, "rot")
                        dve.wait_ge(s["rot"], i.n + 1)
                        nc.vector.tensor_tensor(QKs[i.par], QKe, QKr, ALU.add).then_inc(s["rope"], 1)

                    def expert_rows(i):
                        q = i.par
                        dve.wait_ge(s["rstd_r"], i.g + 1)
                        if not i.first(2):
                            dve.wait_ge(t_stored[q], 16 * (i.half + base // 2))
                            if not layer:
                                dve.wait_ge(s["z_added"], i.n - 1)
                            dve.wait_ge(s["tt_psum"], i.g - 1)
                        if layer:
                            normalise(i, t, small["mv_r"], small["rs_r"]).then_inc(s["t_ready"], 1)
                        else:
                            normalise(i, z, small["mv_r"], small["rs_r"]).then_inc(s["z"], 1)
                            dve.wait_ge(s["z"], i.g + 1)
                            dve.wait_ge(s["ms_r"], i.g * 4 + 4)
                            for j in range(2):
                                last = nc.vector.scalar_tensor_tensor(
                                    t[q][:, j * D:(j + 1) * D], z[q][:, j * D:(j + 1) * D],
                                    small["r2"][q][:, j:j + 1], bias_r[:, 1, :], ALU.mult, ALU.mult)
                            last.then_inc(s["t_ready"], 1)

                    def body(i, on):
                        ex, nx, pv, pp = i.at(2), i.at(1), i.at(-1), i.at(-2)
                        if not layer and on(0):
                            score_unit(i, 1)
                        if layer and on(1):
                            dve.wait_ge(s["qk_psum"], nx.g + 1)
                            if not (isinstance(nx.n, int) and nx.n < 1):
                                dve.wait_ge(s["rope"], nx.n)
                            weigh(nx, QKe, bq, bk, cos, "qk")
                        if layer and on(0):
                            score_unit(i, 1)
                        if on(-3):
                            read_logits(i.at(-3))
                        if layer and on(3):
                            combine(i.at(3), 0)
                        if layer and on(1):
                            rotate(nx)
                        if layer and on(0):
                            score_unit(i, 2)
                        if on(-1):
                            divide(pv)
                        if layer and on(0):
                            score_unit(i, 3)
                        if layer and on(3):
                            combine(i.at(3), 1)
                        if on(-3):
                            choose(i.at(-3))
                        if on(2):
                            if layer:
                                hold(dve, s["combined"], (ex.n + 1) * K0)
                            else:
                                hold(dve, x_in[ex.par], (ex.half + 1) * 16)
                            stats(ex, small["st_a"], small["mv_a"], "stats_a", "moments_a")
                        if layer and on(3):
                            combine(i.at(3), 2)
                        if not layer and on(0):
                            score_unit(i, 2)
                            score_unit(i, 3)
                        if layer and on(-2):
                            expert_rows(pp)
                        if layer and on(3):
                            combine(i.at(3), 3)
                        if not layer and on(-2):
                            expert_rows(pp)
                        if on(2):
                            dve.wait_ge(s["rstd_a"], ex.g + 1)
                            normalise(ex, xn, small["mv_a"], small["rs_a"]).then_inc(s["normed"], 1)
                        if on(1):
                            score_unit(nx, 0)
                        if on(-1):
                            dve.wait_ge(s["wo_psum"], pv.g + 1)
                            dve.wait_ge(s["x_plus_bo"], pv.g + 1)
                            nc.vector.tensor_tensor(tiles(X, pv), P_[:, 0:2 * D].rearrange("p (i d) -> p i d", i=2),
                                                    xb[pv.par].rearrange("p (i d) -> p i d", i=2),
                                                    ALU.add).then_inc(s["added"], 1)
                            hold(dve, s["added"], pv.g + 1)
                            stats(pv, small["st_r"], small["mv_r"], "stats_r", "moments_r")
                    bodies(dve, body)

                @block.scalar
                def _(act):
                    def exps(i, r):
                        act.wait_ge(s["t_psum"], i.g * UNITS + r + 1)
                        nc.scalar.activation(Pt[r % 2], T_[r % 2][:, :], ACT.Exp, scale=SCALE
                                             ).then_inc(s["probs"], 1)

                    def projections(i):
                        if layer:
                            act.wait_ge(s["rope"], i.n + 1)
                        else:
                            act.wait_ge(s["qk_psum"], i.n + 1)
                            nc.scalar.activation(Kt[i.par], P_[:, 2 * D:4 * D], ACT.Identity, bias=bk
                                                 ).then_inc(s["keys"], 1)
                        for r in range(UNITS):
                            rows = slice(32 * r, 32 * r + 32)
                            at = Qz[i.par][rows, r * 2 * D:(r + 1) * 2 * D]
                            if layer:
                                last = nc.scalar.activation(at, QKs[i.par][rows, 0:2 * D], ACT.Copy)
                            else:
                                last = nc.scalar.activation(at, P_[rows, 0:2 * D], ACT.Identity, bias=bq[rows, :])
                        for j in range(pool_heads, 4):
                            last = nc.scalar.activation(
                                Kbd[i.par].rearrange("p (b j k) -> p b j k", b=4, j=4)[:, :, j, :],
                                Kt[i.par].rearrange("p (b k) -> p b k", b=4), ACT.Copy, scale=head_of[:, j:j + 1])
                        last.then_inc(s["queries"], 1)

                    def place_values(i):
                        act.wait_ge(s["v_psum"], i.g + 1)
                        for u in range(2):
                            rows = slice(64 * u, 64 * u + 64)
                            src = M_[rows, :].rearrange("p (b h u d) -> p h b u d", b=4, u=2, d=HD)[:, :, :, u, :]
                            last = nc.scalar.activation(Vbd[i.par][rows, :, :, u, 0:HD], src, ACT.Copy)
                        last.then_inc(s["vbd"], 1)

                    def copy_outputs(i):
                        act.wait_ge(s["o_psum"], i.g + 1)
                        for w in range(2):
                            for b in range(2):
                                rows = slice(64 * b, 64 * b + 64)
                                c = 2 * (HD + 1)
                                src = O_[w][rows, 0:16 * c].rearrange("p (h b c) -> p h b c", h=8, b=2)[:, :, b, :]
                                dst = AO[i.par][rows, w * 8 * c:(w + 1) * 8 * c].rearrange("p (h c) -> p h c", h=8)
                                last = nc.scalar.activation(dst, src, ACT.Copy)
                        last.then_inc(s["o_copied"], 1)

                    def body(i, on):
                        ex, nx, pv, pp = i.at(2), i.at(1), i.at(-1), i.at(-2)
                        if on(0):
                            exps(i, 0)
                        if on(1) and not layer:
                            projections(nx)
                        if on(0):
                            exps(i, 1)
                        if on(1):
                            place_values(nx)
                        if on(1) and layer:
                            projections(nx)
                        if on(0):
                            exps(i, 2)
                        if on(-1):
                            act.wait_ge(s["ot_psum"], pv.g + 1)
                            nc.scalar.activation(aoT[pv.par], P_[:, 0:2 * D], ACT.Identity, bias=bv
                                                 ).then_inc(s["ot"], 1)
                        if on(0):
                            exps(i, 3)
                        if on(-2):
                            act.wait_ge(s["tt_psum"], pp.g + 1)
                            nc.scalar.activation(tT[pp.par], M_[:, 0:2 * D], ACT.Copy).then_inc(s["tt"], 1)
                        if on(2):
                            act.wait_ge(s["cx_psum"], ex.g + 1)
                            nc.scalar.activation(CX[ex.par], M_[:, :], ACT.Copy).then_inc(s["cx"], 1)
                        if on(0):
                            copy_outputs(i)

                    bodies(act, body)

                @block.tensor
                def _(pe):
                    def scores(i, r):
                        g4 = i.g * UNITS
                        if not (isinstance(g4, int) and g4 + r < 2):
                            (pe.wait_ge if layer else partial(hold, pe))(s["centred"], g4 + r - 1)
                        sbk = S_[r % 2]
                        if not layer:
                            nc.tensor.matmul(sbk[:, :].rearrange("p (w j k) -> p w j k", w=2, j=4), seq_of[:],
                                             mask_rows[:, bass.ds(i.n * 2, 2), :].unsqueeze(2)
                                             .broadcast_to([2, 2, 4, S]), start=True, stop=False,
                                             skip_group_check=True)
                        for w in range(2):
                            for b in range(2):
                                sq = 2 * w + b
                                last = nc.tensor.matmul(
                                    sbk[64 * b:64 * b + 64, 256 * w:256 * w + 256],
                                    Qz[i.par][:, 256 * r + 64 * sq:256 * r + 64 * sq + 64],
                                    Kbd[i.par][:, 256 * sq:256 * sq + 256],
                                    start=bool(layer), stop=True, skip_group_check=True)
                        last.then_inc(s["score_psum"], 1)

                    def turn(i, r):
                        pe.wait_ge(s["centred"], i.g * UNITS + r + 1)
                        for k in range(4):
                            last = nc.tensor.transpose(T_[r % 2][:, k * P:(k + 1) * P],
                                                       Sc[r % 2][:, k * P:(k + 1) * P], ident[:])
                        last.then_inc(s["t_psum"], 1)

                    def values(i, r):
                        if r == 0:
                            pe.wait_ge(s["vbd"], i.g + 1)
                            if not i.first(1):
                                pe.wait_ge(s["o_copied"], i.g)
                        pe.wait_ge(s["probs"], i.g * UNITS + r + 1)
                        c = 4 * (HD + 1)
                        for w in range(2):
                            for jj in range(2):
                                hp = 2 * r + jj
                                k = 2 * w + jj
                                last = nc.tensor.matmul(
                                    O_[w][:, c * hp:c * hp + c], Pt[r % 2][:, k * P:(k + 1) * P],
                                    Vbd[i.par][:, hp, 2 * w:2 * w + 2, :, :], start=True, stop=True)
                        if r == UNITS - 1:
                            last.then_inc(s["o_psum"], 1)

                    def inputs(i):
                        q = i.par
                        pe.wait_ge(ctx_in[q], (i.half + i.base // 2 + 1) * 16)
                        pe.wait_ge(s["normed"], i.g + 1)
                        if not i.first(1):
                            pe.wait_ge(s["vbd"], i.g)
                        if not i.first(4):
                            pe.wait_ge(s["tt"], i.g - 3)
                        for w in range(2):
                            nc.tensor.transpose(M_[:, w * P:(w + 1) * P], ctx_t[q][:, w * P:(w + 1) * P], ident[:])
                        for w in range(2):
                            last = nc.tensor.transpose(M_[:, (2 + w) * P:(3 + w) * P],
                                                       xn[q][:, w * P:(w + 1) * P], ident[:])
                        last.then_inc(s["cx_psum"], 1)

                    def projections(i, wq, wk, done):
                        nc.tensor.matmul(P_[:, 0:2 * D], wq, CX[i.par][:, 2 * D:4 * D], start=True, stop=True)
                        nc.tensor.matmul(P_[:, 2 * D:4 * D], wk, CX[i.par][:, 0:2 * D], start=True, stop=True
                                         ).then_inc(done, 1)

                    def body(i, on):
                        ex, nx, pv, pp, p3 = (i.at(k) for k in (2, 1, -1, -2, -3))
                        if on(0):
                            turn(i, 0)
                        if on(1):
                            if not nx.first(3):
                                pe.wait_ge(s["added"], nx.g - 2)
                            pe.wait_ge(s["cx"], nx.g + 1)
                            projections(nx, wq, wk, s["qk_psum"])
                        if on(-3):
                            pe.wait_ge(s["tt"], p3.g + 1)
                            for w in range(2):
                                last = nc.tensor.matmul(M_[:, w * n_e:(w + 1) * n_e],
                                                        tT[p3.par][:, w * P:(w + 1) * P], gw, start=True, stop=True)
                            last.then_inc(s["gate_psum"], 1)
                        if on(0):
                            scores(i, 2)
                        if layer and on(1):
                            pe.wait_ge(s["qk"], nx.n + 1)
                            projections(nx, Wm[:, 8, :], Wm[:, 9, :], s["rot_psum"])
                        if on(0):
                            values(i, 0)
                            turn(i, 1)
                        if on(1):
                            if not nx.first(4):
                                pe.wait_ge(s["logits"], nx.g - 3)
                            for b in range(4):
                                for u in range(2):
                                    last = nc.tensor.matmul(M_[64 * u:64 * u + 64, b * P:(b + 1) * P],
                                                            CX[nx.par][:, b * S:(b + 1) * S], wv, start=True,
                                                            stop=True)
                            last.then_inc(s["v_psum"], 1)
                        if on(0):
                            scores(i, 3)
                            values(i, 1)
                            turn(i, 2)
                        if on(-1):
                            pe.wait_ge(s["o_normed"], pv.g + 1)
                            if on(1):
                                pe.wait_ge(s["rot" if layer else "queries"], nx.n + 1)
                            elif not pv.first(1):
                                pe.wait_ge(s["added"], pv.g)
                            for w in range(2):
                                last = nc.tensor.transpose(P_[:, w * P:(w + 1) * P],
                                                           aon[pv.par][:, w * P:(w + 1) * P], ident[:])
                            last.then_inc(s["ot_psum"], 1)
                        if on(1):
                            pe.wait_ge(s["kbd"], nx.g + 1)
                            pe.wait_ge(s["queries"], nx.g + 1)
                            scores(nx, 0)
                        if on(0):
                            turn(i, 3)
                        if on(-1):
                            pe.wait_ge(s["ot"], pv.g + 1)
                            for w in range(2):
                                last = nc.tensor.matmul(P_[:, w * P:(w + 1) * P],
                                                        aoT[pv.par][:, w * P:(w + 1) * P], wo, start=True, stop=True)
                            last.then_inc(s["wo_psum"], 1)
                        if on(0):
                            values(i, 2)
                        if on(1):
                            scores(nx, 1)
                        if on(-2):
                            pe.wait_ge(s["t_ready"], pp.g + 1)
                            if on(1):
                                pe.wait_ge(s["vbd"], nx.g + 1)
                            elif not pp.first(1):
                                pe.wait_ge(s["logits"], pp.g)
                            for w in range(2):
                                last = nc.tensor.transpose(M_[:, w * P:(w + 1) * P],
                                                           t[pp.par][:, w * P:(w + 1) * P], ident[:])
                            last.then_inc(s["tt_psum"], 1)
                        if on(0):
                            values(i, 3)
                        if on(2):
                            inputs(ex)

                    bodies(pe, body)

        chain = sem("chain")
        chained = [0]
        hot = sem("hot")
        ranks = sem("ranks")
        expo = sem("expo")
        at_least = sem("at_least")
        owner = sem("owner")
        slot_iota = sem("slot_iota")

        def slots(layer):
            E, K = (2 * E1, K1) if layer else (E0, K0)
            NT = SLOT_TILES[layer]
            TE = TILES * E
            chunks = TE // 512
            place[0] = 0
            oh = [carve(TE, BF16) for _ in range(K)]
            CT, INC, POS = (carve(TE) for _ in range(3))
            TMP = CT
            iota_e = carve(E)
            at_f = carve(TILES * K)
            expw = carve(TILES * K)
            wsum = carve(TILES)
            wrec = carve(TILES)
            count = carve(E)
            count_i = carve(E, I32)
            padded = carve(E)
            pad_end = carve(E)
            shift = carve(E)
            diag = carve(E)
            my_end = carve(1)
            slot_f = carve(TILES * K)
            start_of_tile = carve(NT)
            ge = carve(NT, BF16)
            e_f = carve(NT)
            word_f = carve(NT // GROUP)
            ie = lambda v: v.rearrange("p (i e) -> p i e", e=E)
            ei = lambda v: v.rearrange("p (e i) -> p e i", e=E)
            ik = lambda v: v.rearrange("p (i k) -> p i k", k=K)

            with nc.Block() as block:
                @block.gpsimd
                def _(pool):
                    nc.gpsimd.iota(iota_e, pattern=[[1, E]], base=0, channel_multiplier=0,
                                   allow_small_or_imprecise_dtypes=True).then_inc(slot_iota, 1)
                    nc.gpsimd.iota(start_of_tile, pattern=[[P, NT]], base=0, channel_multiplier=0,
                                   allow_small_or_imprecise_dtypes=True).then_inc(slot_iota, 1)

                @block.vector
                def _(dve):
                    def link(ins):
                        chained[0] += 1
                        ins.then_inc(chain, 1)
                        dve.wait_ge(chain, chained[0])

                    nc.vector.tensor_copy(ik(at_f), top_at[:, :, 0:K])
                    link(nc.vector.tensor_tensor(ik(expw), top[:, :, 0:K],
                                                 top[:, :, 0:1].broadcast_to([P, TILES, K]), ALU.subtract))
                    dve.wait_ge(slot_iota, 5 * layer + 2)
                    if layer:
                        link(nc.vector.tensor_scalar(at_f[:, TILES * K // 2:], at_f[:, TILES * K // 2:], float(E1),
                                                     None, ALU.add))
                    for k in range(K):
                        nc.vector.tensor_tensor(ie(oh[k]), iota_e.unsqueeze(1).broadcast_to([P, TILES, E]),
                                                ik(at_f)[:, :, k:k + 1].broadcast_to([P, TILES, E]),
                                                ALU.is_equal).then_inc(hot, 1)
                    dve.wait_ge(expo, layer + 1)
                    link(nc.vector.tensor_reduce(wsum, ik(expw), AX.X, ALU.add))
                    link(nc.vector.reciprocal(wrec, wsum))
                    link(nc.vector.tensor_tensor(wts[:, :, 0:K], ik(expw),
                                                 wrec.unsqueeze(2).broadcast_to([P, TILES, K]), ALU.mult))
                    dve.wait_ge(ranks, layer + 1)
                    w = 512 // E
                    for c in range(chunks):
                        last = nc.vector.tensor_copy(ei(CT)[:, :, c * w:(c + 1) * w],
                                                     bank[4 + c][:, :].rearrange("p (i e) -> p e i", e=E))
                    link(last)
                    link(nc.vector.tensor_tensor_scan(INC, ones_f[:].broadcast_to([P, TE]), CT, 0.0,
                                                      ALU.mult, ALU.add))
                    ends = ei(INC)[:, :, TILES - 1]
                    nc.vector.tensor_copy(count[:, 0:1], ends[:, 0:1])
                    link(nc.vector.tensor_tensor(count[:, 1:E], ends[:, 1:E], ends[:, 0:E - 1], ALU.subtract))
                    link(nc.vector.tensor_scalar(count_i, count, float(P - 1), None, ALU.add))
                    link(nc.vector.tensor_scalar(count_i, count_i, -P, None, ALU.bitwise_and))
                    link(nc.vector.tensor_copy(padded, count_i))
                    link(nc.vector.tensor_tensor_scan(pad_end, ones_f[:].broadcast_to([P, E]), padded, 0.0,
                                                      ALU.mult, ALU.add))
                    link(nc.vector.tensor_tensor(shift, pad_end, padded, ALU.subtract))
                    link(nc.vector.tensor_tensor(shift, shift, ends, ALU.subtract))
                    link(nc.vector.tensor_tensor(shift, shift, count, ALU.add))
                    link(nc.vector.tensor_tensor(diag[0:E, :], pad_end[0:E, :], ident[0:E, 0:E], ALU.mult))
                    link(nc.vector.tensor_reduce(my_end[0:E, :], diag[0:E, :], AX.X, ALU.add))
                    nc.vector.tensor_scalar(ge[0:E, :], start_of_tile[0:E, :], my_end[0:E, :], None,
                                            ALU.is_ge).then_inc(at_least, 1)
                    link(nc.vector.tensor_tensor(INC, INC, CT, ALU.subtract))
                    link(nc.vector.tensor_tensor(ei(INC), ei(INC), shift.unsqueeze(2).broadcast_to([P, E, TILES]),
                                                 ALU.add))
                    for c in range(chunks):
                        last = nc.vector.tensor_tensor(ie(POS)[:, c * w:(c + 1) * w, :],
                                                       bank[c][:, :].rearrange("p (i e) -> p i e", e=E),
                                                       INC.rearrange("p (e i) -> p i e", e=E)[:, c * w:(c + 1) * w, :],
                                                       ALU.add)
                    link(last)
                    for k in range(K):
                        link(nc.vector.tensor_tensor(TMP, oh[k], POS, ALU.mult))
                        link(nc.vector.tensor_reduce(ik(slot_f)[:, :, k], ie(TMP), AX.X, ALU.add))
                    link(nc.vector.tensor_copy(slot[:, :, 0:K], ik(slot_f)))
                    dve.wait_ge(owner, layer + 1)
                    link(nc.vector.tensor_scalar(e_f[0:1, :], bank[7][0:1, 0:NT], float(E - 1), None, ALU.min))
                    if layer:
                        link(nc.vector.tensor_scalar(start_of_tile[0:1, :], e_f[0:1, :], float(E1), -float(E1),
                                                     ALU.is_ge, ALU.mult))
                        link(nc.vector.tensor_tensor(e_f[0:1, :], e_f[0:1, :], start_of_tile[0:1, :], ALU.add))
                    digit = e_f[0:1, :].rearrange("a (g c) -> a g c", c=GROUP)
                    word = word_f[0:1, :].unsqueeze(2)
                    link(nc.vector.tensor_copy(word, digit[:, :, GROUP - 1:GROUP]))
                    for c in reversed(range(GROUP - 1)):
                        link(nc.vector.scalar_tensor_tensor(word, word, float(E0), digit[:, :, c:c + 1], ALU.mult,
                                                            ALU.add))
                    link(nc.vector.tensor_copy(group_experts[0:1, 0:NT // GROUP], word_f[0:1, :]))

                @block.scalar
                def _(act):
                    act.wait_ge(chain, chained_before + 1)
                    nc.scalar.activation(expw, expw, ACT.Exp).then_inc(expo, 1)

                @block.tensor
                def _(pe):
                    for k in range(K):
                        pe.wait_ge(hot, layer * K0 + k + 1)
                        for c in range(chunks):
                            nc.tensor.matmul(bank[c][:, :], before[:], oh[k][:, 512 * c:512 * c + 512],
                                             start=(k == 0), stop=(k == K - 1))
                            last = nc.tensor.matmul(bank[4 + c][:, :], ones_b[:], oh[k][:, 512 * c:512 * c + 512],
                                                    start=(k == 0), stop=(k == K - 1))
                    last.then_inc(ranks, 1)
                    pe.wait_ge(at_least, layer + 1)
                    nc.tensor.matmul(bank[7][0:1, 0:NT], ones_b[0:E, 0:1], ge[0:E, :], start=True, stop=True
                                     ).then_inc(owner, 1)

        hot_high, hot_low = sem("hot_high"), sem("hot_low")
        scaled = sem("scaled")
        summed = sem("summed")
        split = sem("split")

        def invert(layer):
            K = K1 if layer else K0
            NT = SLOT_TILES[layer]
            base = layer * TILES
            place[0] = 0
            high_i, low_i = carve(TILES * K, I32), carve(TILES * K, I32)
            high, low = carve(TILES * K), carve(TILES * K)
            iota_s = carve(NT, F16)
            row_of = carve(1)
            tile_first = carve(TILES)
            hot_a, hot_b, by_row, by_tile = ([carve(K * w, BF16) for _ in range(RING)] for w in (NT, P, P, P))
            total = bank[0]
            ik = lambda v: v.rearrange("p (i k) -> p i k", k=K)

            def tiles_of(eng, body):
                for c in range(RING):
                    body(c, c)
                with eng.Fori(1, TILES // RING - 1) as m:
                    for c in range(RING):
                        body(m * RING + c, c)
                for c in range(RING):
                    body(TILES - RING + c, c)

            with nc.Block() as block:
                if not layer:
                    assert place[0] <= ARENA - b12_words

                    @block.sync
                    def _(sp):
                        sp.dma_start(b12, bias_parts).then_inc(b_in, 16)
                        sp.wait_ge(b_in, 96)
                        sp.wait_ge(expert_in, 32)

                @block.gpsimd
                def _(pool):
                    nc.gpsimd.iota(iota_s, pattern=[[1, NT]], base=0, channel_multiplier=0,
                                   allow_small_or_imprecise_dtypes=True).then_inc(slot_iota, 1)
                    nc.gpsimd.iota(row_of, pattern=[[0, 1]], base=0, channel_multiplier=1,
                                   allow_small_or_imprecise_dtypes=True).then_inc(slot_iota, 1)
                    nc.gpsimd.iota(tile_first, pattern=[[P, TILES]], base=0, channel_multiplier=0,
                                   allow_small_or_imprecise_dtypes=True).then_inc(slot_iota, 1)
                @block.vector
                def _(dve):
                    nc.vector.tensor_scalar(ik(high_i), slot[:, :, 0:K], 7, None, ALU.arith_shift_right)
                    nc.vector.tensor_scalar(ik(low_i), slot[:, :, 0:K], P - 1, None, ALU.bitwise_and
                                            ).then_inc(split, 1)
                    dve.wait_ge(split, 2 * layer + 1)
                    nc.vector.tensor_copy(high, high_i)
                    nc.vector.tensor_copy(low, low_i).then_inc(split, 1)
                    dve.wait_ge(split, 2 * layer + 2)
                    dve.wait_ge(slot_iota, 5 * layer + 5)

                    def body(i, c):
                        if not (isinstance(i, int) and i < RING):
                            dve.wait_ge(summed, i + base - RING + 1)
                        for part, w, hot, done in ((low, P, hot_b, hot_low), (high, NT, hot_a, hot_high)):
                            for k in range(K):
                                last = nc.vector.tensor_scalar(hot[c][:, k * w:(k + 1) * w], iota_s[:, 0:w],
                                                               part[:, bass.ds(i * K + k, 1)], None, ALU.is_equal)
                            last.then_inc(done, 1)

                    tiles_of(dve, body)
                    dve.wait_ge(summed, TILES * (layer + 1))
                    nc.vector.tensor_copy(token_of_slot[:, 0:NT], total[:, 0:NT])

                @block.scalar
                def _(act):
                    def body(i, c):
                        act.wait_ge(hot_low, i + base + 1)
                        nc.scalar.activation(by_row[c], hot_b[c], ACT.Copy, scale=row_of)
                        nc.scalar.activation(by_tile[c], hot_b[c], ACT.Copy,
                                             scale=tile_first[:, bass.ds(i, 1)]).then_inc(scaled, 1)

                    tiles_of(act, body)

                @block.tensor
                def _(pe):
                    def body(i, c):
                        pe.wait_ge(hot_high, i + base + 1)
                        pe.wait_ge(scaled, i + base + 1)
                        at = (lambda n: isinstance(i, int) and i == n)
                        for k in range(K):
                            for rows in (by_row, by_tile):
                                last = nc.tensor.matmul(total[:, 0:NT], rows[c][:, k * P:(k + 1) * P],
                                                        hot_a[c][:, k * NT:(k + 1) * NT],
                                                        start=at(0) and k == 0 and rows is by_row,
                                                        stop=at(TILES - 1) and k == K - 1 and rows is by_tile)
                        last.then_inc(summed, 1)

                    tiles_of(pe, body)

        slots_in = [sem(f"slots_in{q}") for q in range(2)]
        results_out = [sem(f"results_out{q}") for q in range(2)]
        e = {n: sem(n) for n in ("xt_psum", "xt", "h_psum", "clipped", "gated", "hidden", "ht_psum", "ht", "y_psum",
                                 "y", "index")}
        e1 = {n: sem(n) for n in ("h1_psum", "silu1", "hidden1", "ht1_psum", "ht1", "y1_psum")}

        final_index = sem("final_index")
        final_in = [sem(f"final_in{q}") for q in range(2)]
        final_sum = sem("final_sum")
        stored = [sem(f"stored{q}") for q in range(2)]
        out_rows = out.rearrange("b s d -> (b s) d").rearrange("(i p) d -> p i d", p=P)

        def final_buffers():
            return carve2(2 * K1 * D), carve2(2 * K1, I32), carve2(2 * D)

        def final_gather(pool, i, gb, gi):
            q = i.par
            if not i.first(2):
                pool.wait_ge(final_sum, (i.n - 1) * K1)
            nc.gpsimd.tensor_copy(gi[q].rearrange("p (i k) -> p i k", i=2),
                                  slot[:, bass.ds(i.n * 2, 2), 0:K1]).then_inc(final_index, 1)
            hold(pool, final_index, i.n + 1)
            for k in range(2 * K1):
                nc.gpsimd.indirect_dma_start(
                    out=gb[q][:, k * D:(k + 1) * D], out_offset=None, in_=ys,
                    in_offset=bass.IndirectOffsetOnAxis(ap=gi[q][:, k:k + 1], axis=0),
                ).then_inc(final_in[q], 16)

        def final_add(dve, i, gb, res):
            q = i.par
            dve.wait_ge(final_in[q], (i.half + 1) * 16 * 2 * K1)
            if not i.first(2):
                dve.wait_ge(stored[q], i.half * 16)
            for k in range(K1):
                for j in range(2):
                    xt = X[:, bass.ds(i.n * 2 + j, 1), :].rearrange("p i d -> p (i d)")
                    at = (j * K1 + k) * D
                    src = xt if k == 0 else res[q][:, j * D:(j + 1) * D]
                    last = nc.vector.scalar_tensor_tensor(
                        res[q][:, j * D:(j + 1) * D], gb[q][:, at:at + D],
                        wts[:, bass.ds(i.n * 2 + j, 1), k], src, ALU.mult, ALU.add)
                last.then_inc(final_sum, 1)
                if k < K1 - 1:
                    dve.wait_ge(final_sum, i.n * K1 + k + 1)

        def final_store(sp, i, res):
            sp.wait_ge(final_sum, (i.n + 1) * K1)
            sp.dma_start(out_rows[:, bass.ds(i.n * 2, 2), :],
                         res[i.par].rearrange("p (i d) -> p i d", i=2)).then_inc(stored[i.par], 16)

        def group_loop(eng, lo, hi, body):
            with eng.Fori(lo // 2, hi // 2) as m:
                for c in range(2):
                    body(m, c)

        def gather_and_store(block, XE, YE, groups, base, final=None):
            gi = carve2(GROUP, I32)

            def in_order(eng, step):
                def alone(m, c):
                    step(Step(m, c, base), None)

                def both(m, c):
                    step(Step(m, c, base), Step(m, c - SUM_FROM))

                for c in range(2):
                    alone(0, c)
                group_loop(eng, 2, SUM_FROM if final else groups, alone)
                if final:
                    for c in range(2):
                        both(0, SUM_FROM + c)
                    group_loop(eng, SUM_FROM + 2, groups, both)

            @block.gpsimd
            def _(pool):
                def gather(i, j):
                    q = i.par
                    if not i.first(2):
                        pool.wait_ge(e["xt_psum"], i.g - 1)
                    nc.gpsimd.tensor_copy(gi[q], token_of_slot[:, bass.ds(i.n * GROUP, GROUP)]
                                          ).then_inc(e["index"], 1)
                    hold(pool, e["index"], i.g + 1)
                    for c in range(GROUP):
                        nc.gpsimd.indirect_dma_start(
                            out=XE[q][:, c * D:(c + 1) * D], out_offset=None, in_=ts,
                            in_offset=bass.IndirectOffsetOnAxis(ap=gi[q][:, c:c + 1], axis=0),
                        ).then_inc(slots_in[q], 16)
                    if j is not None:
                        if j.first(1):
                            for r in range(2):
                                pool.wait_ge(results_out[r], 16 * (HALF_SLOT_TILES // GROUP + base) // 2)
                        final_gather(pool, j, final[0], final[1])

                in_order(pool, gather)

            @block.sync
            def _(sp):
                def store(i, j):
                    if j is not None:
                        final_store(sp, j, final[2])
                    sp.wait_ge(e["y"], i.g + 1)
                    sp.dma_start(ys_rows[bass.ds(i.n, 1)].rearrange("a p c d -> p (a c) d"),
                                 YE[i.par].rearrange("p (c d) -> p c d", c=GROUP)
                                 ).then_inc(results_out[i.par], 16)

                in_order(sp, store)
                for q in range(2):
                    sp.wait_ge(results_out[q], 16 * (groups + base) // 2)
                    if final:
                        sp.wait_ge(stored[q], 16 * ITERS // 4)

        def pipeline(eng, groups, base, body):
            at = lambda k: Step(0, k, base)
            body(at(-1), True, False, False)
            body(at(0), True, True, False)
            for n in (1, 2, 3):
                body(at(n), True, True, True)
            with eng.Fori(2, groups // 2 - 1) as m:
                for c in range(2):
                    body(Step(m, c, base), True, True, True)
            body(at(groups - 2), True, True, True)
            body(at(groups - 1), False, True, True)
            body(at(groups), False, False, True)

        def transposed_rows(i, pe, XE, A_):
            pe.wait_ge(slots_in[i.par], (i.half + i.base // 2 + 1) * 16 * GROUP)
            if not i.first(2):
                pe.wait_ge(e["xt"], i.g - 1)
            for c in range(GROUP):
                last = nc.tensor.transpose(A_[i.par][:, c * P:(c + 1) * P], XE[i.par][:, c * P:(c + 1) * P], ident[:])
            last.then_inc(e["xt_psum"], 1)

        def word_of(register):
            return nc.tensor.snap(register, min_val=0, max_val=E0 ** GROUP - 1)

        def digits(word, experts):
            return [nc.s_assert_within(word // E0 ** c % E0, 0, experts - 1,
                                       skip_runtime_bounds_check_because="each is clamped to the experts when packed")
                    for c in range(GROUP)]

        def experts0():
            groups = SLOT_TILES[0] // GROUP
            place[0] = 0
            XE, XT, GL, LN, HA, AT, YE = (carve2(GROUP * D) for _ in range(7))
            AG = GL
            A_, H_, C_, Y_ = bank[0:2], bank[2:6], bank[6], bank[7]
            assert place[0] <= ARENA - b12_words
            with nc.Block() as block:
                gather_and_store(block, XE, YE, groups, 0)

                @block.tensor
                def _(pe):
                    held = [ctx.enter_context(pe.register(f"experts{q}")) for q in range(2)]

                    def hidden(i, half, own):
                        if half == 0:
                            pe.wait_ge(e["xt"], i.g + 1)
                        if not i.first(2):
                            pe.wait_ge(e["clipped"], (i.g - 2) * 2 + half + 1)
                        pe.nop(nofuse=True)
                        for c in (2 * half, 2 * half + 1):
                            x_e = own[c]
                            h = H_[2 * i.par + half][:, 256 * (c % 2):256 * (c % 2) + 256]
                            nc.tensor.matmul(h, ones_b[0:3, :], b12[:, bass.ds(x_e, 1), 0:256], start=True, stop=False,
                                             skip_group_check=True)
                            last = nc.tensor.matmul(h, XT[i.par][:, c * P:(c + 1) * P], W0a[:, bass.ds(x_e, 1), :],
                                                    start=False, stop=True, skip_group_check=True)
                        last.then_inc(e["h_psum"], 1)

                    def body(i, ahead, main, behind):
                        nx, pv = i.at(1), i.at(-1)
                        own = digits(word_of(held[i.par]), E0) if main else None
                        if ahead:
                            transposed_rows(nx, pe, XE, A_)
                        if main:
                            hidden(i, 0, own)
                        if behind:
                            pe.wait_ge(e["hidden"], pv.g + 1)
                            if not pv.first(1):
                                pe.wait_ge(e["ht"], pv.g)
                            for c in range(GROUP):
                                last = nc.tensor.transpose(C_[:, c * P:(c + 1) * P],
                                                           HA[pv.par][:, c * P:(c + 1) * P], ident[:])
                            last.then_inc(e["ht_psum"], 1)
                        if main:
                            hidden(i, 1, own)
                        own_before = digits(word_of(held[pv.par]), E0) if behind else None
                        if ahead:
                            pe.reg_load(held[nx.par], group_experts[0:1, bass.ds(nx.n, 1)])
                        if behind:
                            pe.wait_ge(e["ht"], pv.g + 1)
                            if not pv.first(1):
                                pe.wait_ge(e["y"], pv.g)
                            pe.nop(nofuse=True)
                            for c in range(GROUP):
                                x_e = own_before[c]
                                y = Y_[:, c * P:(c + 1) * P]
                                nc.tensor.matmul(y, ones_b[0:3, :], b12[:, bass.ds(x_e, 1), 256:384], start=True,
                                                 stop=False, skip_group_check=True)
                                last = nc.tensor.matmul(y, AT[pv.par][:, c * P:(c + 1) * P],
                                                        W0b[:, bass.ds(x_e, 1), :], start=False, stop=True,
                                                        skip_group_check=True)
                            last.then_inc(e["y_psum"], 1)

                    pipeline(pe, groups, 0, body)

                @block.scalar
                def _(act):
                    def body(i, ahead, main, behind):
                        nx, pv = i.at(1), i.at(-1)
                        if ahead:
                            act.wait_ge(e["xt_psum"], nx.g + 1)
                            nc.scalar.activation(XT[nx.par], A_[nx.par][:, :], ACT.Copy).then_inc(e["xt"], 1)
                        if behind:
                            act.wait_ge(e["ht_psum"], pv.g + 1)
                            nc.scalar.activation(AT[pv.par], C_[:, :], ACT.Copy).then_inc(e["ht"], 1)
                        if main:
                            act.wait_ge(e["clipped"], i.g * 2 + 2)
                            nc.scalar.activation(AG[i.par], GL[i.par], ACT.Gelu_apprx_sigmoid).then_inc(e["gated"], 1)

                    pipeline(act, groups, 0, body)

                @block.vector
                def _(dve):
                    def body(i, ahead, main, behind):
                        pv = i.at(-1)
                        if main:
                            for half in range(2):
                                dve.wait_ge(e["h_psum"], i.g * 2 + half + 1)
                                h = H_[2 * i.par + half][:, :].rearrange("p (c u f) -> p c u f", c=2, u=2)
                                at = slice(half * 256, half * 256 + 256)
                                nc.vector.tensor_scalar(GL[i.par][:, at].rearrange("p (c f) -> p c f", c=2),
                                                        h[:, :, 0, :], LIMIT, None, ALU.min)
                                nc.vector.tensor_scalar(LN[i.par][:, at].rearrange("p (c f) -> p c f", c=2),
                                                        h[:, :, 1, :], LIMIT, -LIMIT, ALU.min, ALU.max
                                                        ).then_inc(e["clipped"], 1)
                            dve.wait_ge(e["gated"], i.g + 1)
                            dve.wait_ge(e["clipped"], i.g * 2 + 2)
                            nc.vector.scalar_tensor_tensor(HA[i.par], LN[i.par], 1.0, AG[i.par], ALU.add, ALU.mult
                                                           ).then_inc(e["hidden"], 1)
                        if behind:
                            dve.wait_ge(e["y_psum"], pv.g + 1)
                            if not pv.first(2):
                                dve.wait_ge(results_out[pv.par], pv.half * 16)
                            nc.vector.tensor_copy(YE[pv.par], Y_[:, :]).then_inc(e["y"], 1)

                    pipeline(dve, groups, 0, body)

        def experts1():
            groups = SLOT_TILES[1] // GROUP
            base = SLOT_TILES[0] // GROUP
            place[0] = 0
            XE, XT, YE = (carve2(GROUP * D) for _ in range(3))
            SI, HM = carve2(F1), carve2(F1)
            AT = carve2(3 * P)
            final = final_buffers()
            A_, H_, C_, Y_ = bank[0], bank[1:5], bank[5], bank[6:8]

            with nc.Block() as block:
                gather_and_store(block, XE, YE, groups, base, final)

                def tiles_of(eng, body):
                    at = lambda k: Step(0, k, base)
                    body(at(-1), 2, False, False, False, True)
                    for n in (0, 1):
                        for c in range(GROUP):
                            body(at(n), c, n > 0 or c > 0, n > 0 or c > 1, True, c == 2)

                    def whole(m, n):
                        for c in range(GROUP):
                            body(Step(m, n, base), c, True, True, True, c == 2)

                    group_loop(eng, 2, SUM_FROM, whole)
                    sums[0] = True
                    for n in (SUM_FROM, SUM_FROM + 1):
                        whole(0, n)
                    group_loop(eng, SUM_FROM + 2, groups - 2, whole)
                    for n in (groups - 2, groups - 1):
                        for c in range(GROUP):
                            body(at(n), c, True, True, True, c == 2 and n < groups - 1)
                    sums[0] = False
                    body(at(groups), 0, True, True, False, False)
                    body(at(groups), 1, False, True, False, False)

                sums = [False]

                def back(i, c, k):
                    return (i.at(-1), c - k + GROUP) if c < k else (i, c - k)

                @block.tensor
                def _(pe):
                    held = [ctx.enter_context(pe.register(f"experts_1_{q}")) for q in range(2)]
                    own = {}

                    def body(i, c, lag1, lag2, main, ahead):
                        if c == 0:
                            own[0] = digits(word_of(held[i.par]), E1) if main else None
                            own[1] = digits(word_of(held[i.at(-1).par]), E1) if lag1 else None
                        if main and c == 0:
                            hold(pe, e["xt"], i.g + 1)
                        if main:
                            r = c % 2
                            if not (isinstance(i.n, int) and i.n * GROUP + c < 2):
                                hold(pe, e1["hidden1"], i.n * GROUP + c - 1)
                            x_e = own[0][c]
                            for u in range(2):
                                last = nc.tensor.matmul(H_[2 * r + u][:, 0:F1], XT[i.par][:, c * P:(c + 1) * P],
                                                        W1a[:, bass.ds(x_e, 1), u * F1:(u + 1) * F1],
                                                        start=True, stop=True)
                            last.then_inc(e1["h1_psum"], 1)
                        if lag2:
                            j, d = back(i, c, 2)
                            count = j.n * GROUP + d
                            pe.wait_ge(e1["ht1"], count + 1)
                            if d == 0 and not (isinstance(j.n, int) and j.n < 2):
                                pe.wait_ge(e["y"], j.g - 1)
                            pe.nop(nofuse=True)
                            x_e = own[0][d] if c >= 2 else own[1][d]
                            for k, f in enumerate(F1_BLOCKS):
                                last = nc.tensor.matmul(Y_[j.par][:, d * P:(d + 1) * P],
                                                        AT[d % 2][0:f, k * P:(k + 1) * P],
                                                        W1b[0:f, bass.ds(x_e, 1), k * P:(k + 1) * P],
                                                        start=(k == 0), stop=(k == 2))
                            if d == GROUP - 1:
                                last.then_inc(e1["y1_psum"], 1)
                        if lag1:
                            j, d = back(i, c, 1)
                            count = j.n * GROUP + d
                            pe.wait_ge(e1["hidden1"], count + 1)
                            for k, f in enumerate(F1_BLOCKS):
                                last = nc.tensor.transpose(C_[0:f, k * P:(k + 1) * P],
                                                           HM[d % 2][:, k * P:k * P + f], ident[:])
                            last.then_inc(e1["ht1_psum"], 1)
                        if ahead:
                            nx = i.at(1)
                            pe.reg_load(held[nx.par], group_experts[0:1, bass.ds(nx.n, 1)])
                            pe.wait_ge(slots_in[nx.par], (nx.half + base // 2 + 1) * 16 * GROUP)
                            pe.wait_ge(e["xt"], nx.g)
                            for k in range(GROUP):
                                last = nc.tensor.transpose(A_[:, k * P:(k + 1) * P], XE[nx.par][:, k * P:(k + 1) * P],
                                                           ident[:])
                            last.then_inc(e["xt_psum"], 1)

                    tiles_of(pe, body)

                @block.scalar
                def _(act):
                    def body(i, c, lag1, lag2, main, ahead):
                        if main:
                            act.wait_ge(e1["h1_psum"], i.n * GROUP + c + 1)
                            nc.scalar.activation(SI[c % 2], H_[2 * (c % 2)][:, 0:F1], ACT.Silu
                                                 ).then_inc(e1["silu1"], 1)
                        if lag1:
                            j, d = back(i, c, 1)
                            count = j.n * GROUP + d
                            act.wait_ge(e1["ht1_psum"], count + 1)
                            nc.scalar.activation(AT[d % 2][:, 0:2 * P], C_[:, 0:2 * P], ACT.Copy)
                            nc.scalar.activation(AT[d % 2][0:96, 2 * P:3 * P], C_[0:96, 2 * P:3 * P], ACT.Copy
                                                 ).then_inc(e1["ht1"], 1)
                        if ahead:
                            nx = i.at(1)
                            act.wait_ge(e["xt_psum"], nx.g + 1)
                            nc.scalar.activation(XT[nx.par], A_[:, :], ACT.Copy).then_inc(e["xt"], 1)

                    tiles_of(act, body)

                @block.vector
                def _(dve):
                    def body(i, c, lag1, lag2, main, ahead):
                        if main:
                            dve.wait_ge(e1["silu1"], i.n * GROUP + c + 1)
                            nc.vector.tensor_tensor(HM[c % 2], H_[2 * (c % 2) + 1][:, 0:F1], SI[c % 2], ALU.mult
                                                    ).then_inc(e1["hidden1"], 1)
                        if lag2:
                            j, d = back(i, c, 2)
                            if d == GROUP - 1:
                                dve.wait_ge(e1["y1_psum"], j.n + 1)
                                if not (isinstance(j.n, int) and j.n < 2):
                                    dve.wait_ge(results_out[j.par], (j.half + base // 2) * 16)
                                nc.vector.tensor_copy(YE[j.par], Y_[j.par][:, :]).then_inc(e["y"], 1)
                        if sums[0] and c == GROUP - 1:
                            final_add(dve, Step(i.m, i.c - SUM_FROM), final[0], final[2])

                    tiles_of(dve, body)

        def finish():
            place[0] = 0
            gb, gi, res = final_buffers()
            with nc.Block() as block:
                @block.gpsimd
                def _(pool):
                    group_loop(pool, ITERS // 2, ITERS, lambda m, c: final_gather(pool, Step(m, c), gb, gi))

                @block.vector
                def _(dve):
                    group_loop(dve, ITERS // 2, ITERS, lambda m, c: final_add(dve, Step(m, c), gb, res))

                @block.sync
                def _(sp):
                    group_loop(sp, ITERS // 2, ITERS, lambda m, c: final_store(sp, Step(m, c), res))
                    for q in range(2):
                        sp.wait_ge(stored[q], 16 * ITERS // 2)

        attention(0)
        chained_before = chained[0]
        slots(0)
        invert(0)
        experts0()
        attention(1)
        chained_before = chained[0]
        slots(1)
        invert(1)
        experts1()
        finish()


def kernel(**inputs):
    import numpy as np
    import concourse.bacc as bacc
    from concourse.bass_utils import run_bass_kernel_spmd as run

    nc = bacc.Bacc("TRN2", target_bir_lowering=False, num_devices=1)
    i = {k: np.ascontiguousarray(v) for k, v in inputs.items()}
    arrays = {k: i[k] for k in ("x", "ctx_1024", "L0_xattn_bq", "L0_xattn_bk", "L0_xattn_bv", "L0_xattn_bo",
                                "L1_xattn_bq", "L1_xattn_bk", "L1_xattn_bv", "L1_xattn_bo",
                                "L0_ffn_norm_scale", "L0_ffn_gate_b", "L0_ffn_b2")}
    arrays["mask"] = i["mask_BxS2_bf0"]
    half = np.arange(D).reshape(HEADS, 2, HD // 2)[:, ::-1].reshape(-1)
    arrays["proj"] = np.ascontiguousarray(np.stack(
        [i["L0_xattn_" + n] for n in ("Wq", "Wk", "Wv", "Wo")] + [i["L1_xattn_" + n] for n in ("Wq", "Wk", "Wv", "Wo")]
        + [i["L1_xattn_Wq"][:, half], i["L1_xattn_Wk"][:, half]], axis=1))
    arrays["bqr"] = np.ascontiguousarray(i["L1_xattn_bq"][half])
    arrays["bkr"] = np.ascontiguousarray(i["L1_xattn_bk"][half])
    arrays["gate0"] = np.ascontiguousarray(i["L0_ffn_gate_w"].T)
    arrays["gate1"] = np.ascontiguousarray(i["L1_ffn_gate_w"].T)
    w1 = i["L0_ffn_w1"].reshape(E0, F0, 2, D).transpose(3, 0, 2, 1).reshape(D, E0, 2 * F0)
    arrays["w1_0"] = np.ascontiguousarray(w1)
    arrays["b1_0"] = np.ascontiguousarray(i["L0_ffn_b1"].reshape(E0, F0, 2).transpose(0, 2, 1).reshape(E0, 2 * F0))
    arrays["w2_0"] = np.ascontiguousarray(i["L0_ffn_w2"].transpose(2, 0, 1))
    arrays["w13_1"] = np.ascontiguousarray(
        np.concatenate([i["L1_ffn_w1"].transpose(2, 0, 1), i["L1_ffn_w3"].transpose(2, 0, 1)], axis=2))
    w2 = np.zeros((E1, D, 3 * P), np.float32)
    w2[:, :, :F1] = i["L1_ffn_w2"]
    arrays["w2_1"] = np.ascontiguousarray(w2.reshape(E1, D, 3, P).transpose(3, 0, 2, 1).reshape(P, E1, 3 * P))
    arrays["ident"] = np.eye(P, dtype=np.float32)
    arrays["before"] = np.triu(np.ones((P, P), np.float32), 1)
    arrays["head_of"] = (np.arange(P)[:, None] // HD % 4 == np.arange(4)[None, :]).astype(np.float32)
    arrays["seq_of"] = (np.arange(P)[None, :] // S == np.arange(2)[:, None]).astype(np.float32)
    freq = (1.0 / np.float32(10000.0) ** (np.arange(0, HD, 2, dtype=np.float32) / np.float32(HD))).astype(np.float32)
    angle = (np.arange(S, dtype=np.float32)[None, :] * freq[np.arange(P) % (HD // 2)][:, None]).astype(np.float32)
    sign = np.where(np.arange(P) % HD < HD // 2, -1.0, 1.0).astype(np.float32)[:, None]
    arrays["cos"] = np.cos(angle).astype(np.float32)
    arrays["sin"] = (np.sin(angle) * sign).astype(np.float32)
    args = {n: nc.dram_tensor("in_" + n, v.shape, mybir.dt.from_np(v.dtype), kind="ExternalInput").ap()
            for n, v in arrays.items()}
    out = nc.dram_tensor("out_x", (B, S, D), F32, kind="ExternalOutput").ap()
    ts = nc.dram_tensor("expert_rows", (TOKENS, D), F32, kind="Internal").ap()
    ys = nc.dram_tensor("slot_results", (SLOT_TILES[0] * P, D), F32, kind="Internal").ap()
    parts = nc.dram_tensor("bias_parts", (3, E0, 3 * F0), BF16, kind="Internal").ap()
    build(nc, args, out, ts, ys, parts)
    r = run(nc, [{"in_" + n: v for n, v in arrays.items()}], core_ids=[0])
    return r.results[0]["out_x"]
```
